# Optimizing a Trainium2 kernel written in Bass

```python
import numpy as np
import jax
import jax.numpy as jnp

def _softmax(x, axis=-1):
    return jax.nn.softmax(x, axis=axis)

def _gelu(x):
    return jax.nn.gelu(x, approximate=True)

def _silu(x):
    return jax.nn.silu(x)

def _sigmoid(x):
    return jax.nn.sigmoid(x)

def _layernorm(x, axis=-1, eps=1e-05):
    m = jnp.mean(x, axis=axis, keepdims=True)
    v = jnp.var(x, axis=axis, keepdims=True)
    return (x - m) / jnp.sqrt(v + eps)

def _scatter_add(tgt, idx, src, axis=0):
    return tgt.at[idx].add(src)

def _segment_sum(src, seg, n):
    return jax.ops.segment_sum(src, seg, n)
kernel_name = 'mk_flamingo_gated_d4_seqx_r8_1aeb56'

def setup_inputs(seed: int=0):
    np.random.seed(seed)
    _w = jnp.asarray

    def _rec_inputs():
        import jax
        import jax.numpy as jnp
        _rk = jax.random.key(seed)
        x = 7.22e-05 + 1 * jax.random.normal(jax.random.fold_in(_rk, 1), (8, 256, 128), jnp.float32)
        _lenS = 256 - jax.random.randint(jax.random.fold_in(_rk, 7), (8,), 0, max(1, 256 // 4) + 1, jnp.int32)
        _lenS2 = 256 - jax.random.randint(jax.random.fold_in(_rk, 8), (8,), 0, max(1, 256 // 4) + 1, jnp.int32)
        _ctx_1024P = jax.random.normal(jax.random.fold_in(_rk, 11), (8, 16, 128), jnp.float32)
        _ctx_1024c = jax.random.dirichlet(jax.random.fold_in(_rk, 511), 0.3 * jnp.ones((16,), jnp.float32), (8, 256))
        _ctx_1024t = jnp.einsum('bsk,bkd->bsd', _ctx_1024c, _ctx_1024P)
        _ctx_1024t = _ctx_1024t * jax.lax.rsqrt(jnp.mean(jnp.square(_ctx_1024t)) + 1e-12) * 0.953939
        ctx_1024 = -0.000107592 + 0.9999 * (_ctx_1024t + 0.3 * jax.random.normal(jax.random.fold_in(_rk, 611), (8, 256, 128), jnp.float32))
        _validS = jnp.arange(256)[None, :] < _lenS[:, None]
        _validS2 = jnp.arange(256)[None, :] < _lenS2[:, None]
        _causal = jnp.tril(jnp.ones((256, 256), dtype=bool))
        mask_SxS2_ik0 = jnp.where(jnp.broadcast_to(_validS2[0:1, :], (256, 256)), 0, 1).astype(jnp.int32)
        mask_BxS2_ik0 = jnp.where(jnp.broadcast_to(_validS2[:, :], (8, 256)), 0, 1).astype(jnp.int32)
        _g = jax.random.normal(jax.random.fold_in(_rk, 9001), (2, 4), jnp.float32)
        _g = jnp.sign(_g) * jnp.maximum(jnp.abs(_g), 1.0) + (_g == 0) * 1.0
        g_xattn = _g[0]
        g_ffn = _g[1]
        return (x, ctx_1024, mask_SxS2_ik0, mask_BxS2_ik0, g_xattn, g_ffn)
    x, ctx_1024, mask_SxS2_ik0, mask_BxS2_ik0, g_xattn, g_ffn = _rec_inputs()

    def _L0_xattn_setup():
        import jax, jax.numpy as jnp
        import numpy as np
        DIM = 128
        N_HEADS = 16
        HEAD_DIM = DIM // N_HEADS
        EPS = 1e-06
        Q_THETA = 32.0
        K_THETA = 1000.0

        def precompute_freqs_1d(dim, seq_len, theta):
            freqs = theta ** (-jnp.arange(0, dim, 2, dtype=jnp.float32) / dim)
            t = jnp.arange(seq_len, dtype=jnp.float32)
            ang = t[:, None] * freqs[None, :]
            return (jnp.cos(ang), jnp.sin(ang))

        def rms_norm(x, w):
            var = jnp.mean(x * x, axis=-1, keepdims=True)
            return x * jax.lax.rsqrt(var + EPS) * w

        def apply_rope(t, cos, sin):
            cos = cos[None, None, :, :]
            sin = sin[None, None, :, :]
            t1, t2 = jnp.split(t, 2, axis=-1)
            return jnp.concatenate([t1 * cos - t2 * sin, t2 * cos + t1 * sin], axis=-1)
        key = jax.random.key(seed)
        ks = jax.random.split(key, 8)
        B, T, S = (128, 64, 48)
        s = 1.0 / np.sqrt(DIM)
        return {'x': jax.random.normal(ks[0], (B, T, DIM), jnp.float32), 'context': jax.random.normal(ks[1], (B, S, DIM), jnp.float32), 'Wq': jax.random.normal(ks[2], (DIM, DIM), jnp.float32) * s, 'Wk': jax.random.normal(ks[3], (DIM, DIM), jnp.float32) * s, 'Wv': jax.random.normal(ks[4], (DIM, DIM), jnp.float32) * s, 'Wo': jax.random.normal(ks[5], (DIM, DIM), jnp.float32) * s, 'q_norm_w': jnp.ones((HEAD_DIM,), jnp.float32), 'k_norm_w': jnp.ones((HEAD_DIM,), jnp.float32)}
    _L0_xattn_all = _L0_xattn_setup()
    _L0_xattn_in = {k: v for k, v in _L0_xattn_all.items() if k in ('Wq', 'Wk', 'Wv', 'Wo', 'q_norm_w', 'k_norm_w')}
    del _L0_xattn_all

    def _L0_ffn_setup():
        import jax, jax.numpy as jnp
        import numpy as np
        DIM = 128
        DEPTH = 6
        HEADS = 16
        DIM_HEAD = 64
        WINDOW = 32
        INNER = HEADS * DIM_HEAD
        DIM_INNER = int(DIM * 4 * 2 / 3)
        QK_SCALE = 8.0

        def shift_tokens(t):
            a, s = jnp.split(t, 2, -1)
            s = jnp.pad(s, ((0, 0), (1, 0), (0, 0)))[:, :-1]
            return jnp.concatenate([a, s], -1)

        def l2norm(t):
            return t / jnp.maximum(jnp.linalg.norm(t, axis=-1, keepdims=True), 1e-12)

        def rotate_half(x):
            x1, x2 = jnp.split(x, 2, -1)
            return jnp.concatenate([-x2, x1], -1)

        def rotary_tables(n):
            half = jnp.arange(0, DIM_HEAD, 2, dtype=jnp.float32)
            inv_freq = 1.0 / 10000.0 ** (half / DIM_HEAD)
            t = jnp.arange(n, dtype=jnp.float32)
            freqs = t[:, None] * inv_freq[None, :]
            freqs = jnp.concatenate([freqs, freqs], -1)
            base_scale = (half + 0.4 * DIM_HEAD) / (1.4 * DIM_HEAD)
            power = (t - n // 2) / (WINDOW // 2)
            scale = base_scale[None, :] ** power[:, None]
            scale = jnp.concatenate([scale, scale], -1)
            return (freqs, scale)

        def local_attention(q, k, v):
            b, h, n, d = q.shape
            w = WINDOW
            nw = n // w
            bq = q.reshape(b, h, nw, w, d)
            bk = k.reshape(b, h, nw, w, d)
            bv = v.reshape(b, h, nw, w, d)

            def look(t):
                p = jnp.pad(t, ((0, 0), (0, 0), (1, 0), (0, 0), (0, 0)))
                return jnp.concatenate([p[:, :, :nw], p[:, :, 1:]], axis=3)
            bk2, bv2 = (look(bk), look(bv))
            seq = jnp.arange(n).reshape(nw, w)
            seq_p = jnp.pad(seq, ((1, 0), (0, 0)), constant_values=-1)
            jt = jnp.concatenate([seq_p[:nw], seq_p[1:]], axis=1)
            it = seq[:, :, None]
            jb = jt[:, None, :]
            mask = (it < jb) | (it > jb + w) | (jb == -1)
            sim = jnp.einsum('bhwie,bhwje->bhwij', bq, bk2) * QK_SCALE
            sim = jnp.where(mask, -jnp.finfo(sim.dtype).max, sim)
            attn = jax.nn.softmax(sim, -1)
            out = jnp.einsum('bhwij,bhwje->bhwie', attn, bv2)
            return out.reshape(b, h, n, d)

        def attn_layer(x, Wqkv, qs, ksc, Wo):
            b, n, _ = x.shape
            qkv = x @ Wqkv
            q, k, v = jnp.split(qkv, 3, -1)
            sh = lambda t: t.reshape(b, n, HEADS, DIM_HEAD).transpose(0, 2, 1, 3)
            q, k, v = (sh(q), sh(k), sh(v))
            q = l2norm(q) * qs
            k = l2norm(k) * ksc
            freqs, scale = rotary_tables(n)
            cos, sin = (jnp.cos(freqs), jnp.sin(freqs))
            q = q * cos * scale + rotate_half(q) * sin * scale
            inv = 1.0 / scale
            k = k * cos * inv + rotate_half(k) * sin * inv
            out = local_attention(q, k, v)
            out = out.transpose(0, 2, 1, 3).reshape(b, n, INNER)
            return out @ Wo

        def ffn_layer(x, g, bln, W1, b1, W2, b2):
            mu = x.mean(-1, keepdims=True)
            var = ((x - mu) ** 2).mean(-1, keepdims=True)
            xn = (x - mu) / jnp.sqrt(var + 1e-05) * g + bln
            hg = xn @ W1 + b1
            a, gate = jnp.split(hg, 2, -1)
            return a * jax.nn.gelu(gate, approximate=False) @ W2 + b2
        key = jax.random.key(seed)
        ks = jax.random.split(key, 8)
        B, N = (2, 256)
        init = lambda k, shape: jax.random.normal(k, shape, jnp.float32) * 0.02
        return {'x': jax.random.normal(ks[0], (B, N, DIM), jnp.float32), 'Wqkv': init(ks[1], (DEPTH, DIM, 3 * INNER)), 'q_scale': jnp.ones((DEPTH, DIM_HEAD), jnp.float32), 'k_scale': jnp.ones((DEPTH, DIM_HEAD), jnp.float32), 'Wo': init(ks[2], (DEPTH, INNER, DIM)), 'ln_g': jnp.ones((DEPTH, DIM), jnp.float32), 'ln_b': jnp.zeros((DEPTH, DIM), jnp.float32), 'W1': init(ks[3], (DEPTH, DIM, 2 * DIM_INNER)), 'b1': jnp.zeros((DEPTH, 2 * DIM_INNER), jnp.float32), 'W2': init(ks[4], (DEPTH, DIM_INNER, DIM)), 'b2': jnp.zeros((DEPTH, DIM), jnp.float32)}
    _L0_ffn_all = _L0_ffn_setup()
    _L0_ffn_in = {k: v for k, v in _L0_ffn_all.items() if k in ('Wqkv', 'q_scale', 'k_scale', 'Wo', 'ln_g', 'ln_b', 'W1', 'b1', 'W2', 'b2')}
    del _L0_ffn_all

    def _L1_xattn_setup():
        import jax, jax.numpy as jnp
        import numpy as np
        D_MODEL = 128
        N_HEAD = 16
        B, S = (2, 256)
        key = jax.random.key(seed)
        ks = jax.random.split(key, 12)
        std = 1.0 / np.sqrt(D_MODEL)
        inp = {'q': jax.random.normal(ks[0], (B, S, D_MODEL), jnp.float32), 'k': jax.random.normal(ks[1], (B, S, D_MODEL), jnp.float32), 'v': jax.random.normal(ks[2], (B, S, D_MODEL), jnp.float32), 'mask': jnp.tril(jnp.ones((S, S), jnp.int32)), 'Wq': jax.random.normal(ks[3], (D_MODEL, D_MODEL), jnp.float32) * std, 'bq': jax.random.normal(ks[4], (D_MODEL,), jnp.float32) * std, 'Wk': jax.random.normal(ks[5], (D_MODEL, D_MODEL), jnp.float32) * std, 'bk': jax.random.normal(ks[6], (D_MODEL,), jnp.float32) * std, 'Wv': jax.random.normal(ks[7], (D_MODEL, D_MODEL), jnp.float32) * std, 'bv': jax.random.normal(ks[8], (D_MODEL,), jnp.float32) * std, 'Wo': jax.random.normal(ks[9], (D_MODEL, D_MODEL), jnp.float32) * std, 'bo': jax.random.normal(ks[10], (D_MODEL,), jnp.float32) * std}
        return inp
    _L1_xattn_all = _L1_xattn_setup()
    _L1_xattn_in = {k: v for k, v in _L1_xattn_all.items() if k in ('Wq', 'bq', 'Wk', 'bk', 'Wv', 'bv', 'Wo', 'bo')}
    del _L1_xattn_all

    def _L1_ffn_setup():
        import jax, jax.numpy as jnp
        import numpy as np
        TOP_K = 2
        key = jax.random.key(seed)
        ks = jax.random.split(key, 6)
        B, S, D, E = (8, 512, 128, 8)
        s = 1.0 / np.sqrt(D)
        return {'x': jax.random.normal(ks[0], (B, S, D), dtype=jnp.float32), 'Wr': jax.random.normal(ks[1], (D, E), dtype=jnp.float32) * s, 'br': jnp.zeros((E,), dtype=jnp.float32), 'W1': jax.random.normal(ks[2], (E, D, D), dtype=jnp.float32) * s, 'b1': jnp.zeros((E, D), dtype=jnp.float32), 'W2': jax.random.normal(ks[3], (E, D, D), dtype=jnp.float32) * s, 'b2': jnp.zeros((E, D), dtype=jnp.float32)}
    _L1_ffn_all = _L1_ffn_setup()
    _L1_ffn_in = {k: v for k, v in _L1_ffn_all.items() if k in ('Wr', 'br', 'W1', 'b1', 'W2', 'b2')}
    del _L1_ffn_all

    def _L2_xattn_setup():
        import jax, jax.numpy as jnp
        import numpy as np
        HEADS = 16
        DIM_Q = 128
        DIM_KV = 128
        INNER = 128
        key = jax.random.key(seed)
        k1, k2, k3, k4, k5, k6, k7 = jax.random.split(key, 7)
        B, Lq, Lkv = (2, 256, 512)
        H = jax.random.normal(k1, (B, Lq, DIM_Q), dtype=jnp.float32)
        T = jax.random.normal(k2, (B, Lkv, DIM_KV), dtype=jnp.float32)
        mask = jax.random.randint(k3, (B, Lkv), 0, 2, dtype=jnp.int32)
        s = 0.02
        Wq = jax.random.normal(k4, (DIM_Q, INNER), dtype=jnp.float32) * s
        Wk = jax.random.normal(k5, (DIM_KV, INNER), dtype=jnp.float32) * s
        Wv = jax.random.normal(k6, (DIM_KV, INNER), dtype=jnp.float32) * s
        Wo = jax.random.normal(k7, (INNER, DIM_Q), dtype=jnp.float32) * s
        return {'H': H, 'T': T, 'mask': mask, 'Wq': Wq, 'Wk': Wk, 'Wv': Wv, 'Wo': Wo}
    _L2_xattn_all = _L2_xattn_setup()
    _L2_xattn_in = {k: v for k, v in _L2_xattn_all.items() if k in ('Wq', 'Wk', 'Wv', 'Wo')}
    del _L2_xattn_all

    def _L2_ffn_setup():
        import jax, jax.numpy as jnp
        import numpy as np
        NEG_INF = -1e+30
        K = 2
        key = jax.random.key(seed)
        ks = jax.random.split(key, 5)
        B, S, D, O, E = (8, 256, 128, 128, 8)
        scale = 1.0 / np.sqrt(D)
        return {'x': jax.random.normal(ks[0], (B, S, D), dtype=jnp.float32), 'gate_w': jax.random.normal(ks[1], (E, D), dtype=jnp.float32) * scale, 'gate_b': jnp.zeros((E,), dtype=jnp.float32), 'expert_w': jax.random.normal(ks[2], (E, O, D), dtype=jnp.float32) * scale, 'expert_b': jnp.zeros((E, O), dtype=jnp.float32)}
    _L2_ffn_all = _L2_ffn_setup()
    _L2_ffn_in = {k: v for k, v in _L2_ffn_all.items() if k in ('gate_w', 'gate_b', 'expert_w', 'expert_b')}
    del _L2_ffn_all

    def _L3_xattn_setup():
        import jax, jax.numpy as jnp
        import numpy as np
        FEATURE_DIM = 128
        NUM_HEADS = 16
        HEAD_DIM = FEATURE_DIM // NUM_HEADS
        key = jax.random.key(seed)
        ks = jax.random.split(key, 11)
        B, SQ, SKV, D = (4, 128, 256, FEATURE_DIM)
        s = 1.0 / np.sqrt(D)
        return {'query': jax.random.normal(ks[0], (B, SQ, D), jnp.float32), 'key': jax.random.normal(ks[1], (B, SKV, D), jnp.float32), 'value': jax.random.normal(ks[2], (B, SKV, D), jnp.float32), 'wq': jax.random.normal(ks[3], (D, D), jnp.float32) * s, 'bq': jnp.zeros((D,), jnp.float32), 'wk': jax.random.normal(ks[4], (D, D), jnp.float32) * s, 'bk': jnp.zeros((D,), jnp.float32), 'wv': jax.random.normal(ks[5], (D, D), jnp.float32) * s, 'bv': jnp.zeros((D,), jnp.float32), 'wo': jax.random.normal(ks[6], (D, D), jnp.float32) * s, 'bo': jnp.zeros((D,), jnp.float32)}
    _L3_xattn_all = _L3_xattn_setup()
    _L3_xattn_in = {k: v for k, v in _L3_xattn_all.items() if k in ('wq', 'bq', 'wk', 'bk', 'wv', 'bv', 'wo', 'bo')}
    del _L3_xattn_all

    def _L3_ffn_setup():
        import jax, jax.numpy as jnp
        import numpy as np
        LN_EPS = 0.001
        EPS = 1e-05
        QB = 128.0

        def ste_round(x):
            return x + jax.lax.stop_gradient(jnp.round(x) - x)
        key = jax.random.key(seed)
        k1, k2 = jax.random.split(key)
        x = jax.random.normal(k1, (4, 1024, 128), dtype=jnp.float32)
        weight = jax.random.normal(k2, (128, 128), dtype=jnp.float32) * 0.02
        ln_gamma = jnp.ones((128,), dtype=jnp.float32)
        ln_beta = jnp.zeros((128,), dtype=jnp.float32)
        return {'x': x, 'weight': weight, 'ln_gamma': ln_gamma, 'ln_beta': ln_beta}
    _L3_ffn_all = _L3_ffn_setup()
    _L3_ffn_in = {k: v for k, v in _L3_ffn_all.items() if k in ('weight', 'ln_gamma', 'ln_beta')}
    del _L3_ffn_all
    return {'x': x, 'ctx_1024': ctx_1024, 'mask_SxS2_ik0': mask_SxS2_ik0, 'mask_BxS2_ik0': mask_BxS2_ik0, 'g_xattn': g_xattn, 'g_ffn': g_ffn, 'L0_xattn_Wq': _L0_xattn_in['Wq'], 'L0_xattn_Wk': _L0_xattn_in['Wk'], 'L0_xattn_Wv': _L0_xattn_in['Wv'], 'L0_xattn_Wo': _L0_xattn_in['Wo'], 'L0_xattn_q_norm_w': _L0_xattn_in['q_norm_w'], 'L0_xattn_k_norm_w': _L0_xattn_in['k_norm_w'], 'L0_ffn_Wqkv': _L0_ffn_in['Wqkv'], 'L0_ffn_q_scale': _L0_ffn_in['q_scale'], 'L0_ffn_k_scale': _L0_ffn_in['k_scale'], 'L0_ffn_Wo': _L0_ffn_in['Wo'], 'L0_ffn_ln_g': _L0_ffn_in['ln_g'], 'L0_ffn_ln_b': _L0_ffn_in['ln_b'], 'L0_ffn_W1': _L0_ffn_in['W1'], 'L0_ffn_b1': _L0_ffn_in['b1'], 'L0_ffn_W2': _L0_ffn_in['W2'], 'L0_ffn_b2': _L0_ffn_in['b2'], 'L1_xattn_Wq': _L1_xattn_in['Wq'], 'L1_xattn_bq': _L1_xattn_in['bq'], 'L1_xattn_Wk': _L1_xattn_in['Wk'], 'L1_xattn_bk': _L1_xattn_in['bk'], 'L1_xattn_Wv': _L1_xattn_in['Wv'], 'L1_xattn_bv': _L1_xattn_in['bv'], 'L1_xattn_Wo': _L1_xattn_in['Wo'], 'L1_xattn_bo': _L1_xattn_in['bo'], 'L1_ffn_Wr': _L1_ffn_in['Wr'], 'L1_ffn_br': _L1_ffn_in['br'], 'L1_ffn_W1': _L1_ffn_in['W1'], 'L1_ffn_b1': _L1_ffn_in['b1'], 'L1_ffn_W2': _L1_ffn_in['W2'], 'L1_ffn_b2': _L1_ffn_in['b2'], 'L2_xattn_Wq': _L2_xattn_in['Wq'], 'L2_xattn_Wk': _L2_xattn_in['Wk'], 'L2_xattn_Wv': _L2_xattn_in['Wv'], 'L2_xattn_Wo': _L2_xattn_in['Wo'], 'L2_ffn_gate_w': _L2_ffn_in['gate_w'], 'L2_ffn_gate_b': _L2_ffn_in['gate_b'], 'L2_ffn_expert_w': _L2_ffn_in['expert_w'], 'L2_ffn_expert_b': _L2_ffn_in['expert_b'], 'L3_xattn_wq': _L3_xattn_in['wq'], 'L3_xattn_bq': _L3_xattn_in['bq'], 'L3_xattn_wk': _L3_xattn_in['wk'], 'L3_xattn_bk': _L3_xattn_in['bk'], 'L3_xattn_wv': _L3_xattn_in['wv'], 'L3_xattn_bv': _L3_xattn_in['bv'], 'L3_xattn_wo': _L3_xattn_in['wo'], 'L3_xattn_bo': _L3_xattn_in['bo'], 'L3_ffn_weight': _L3_ffn_in['weight'], 'L3_ffn_ln_gamma': _L3_ffn_in['ln_gamma'], 'L3_ffn_ln_beta': _L3_ffn_in['ln_beta']}

def reference(x, ctx_1024, mask_SxS2_ik0, mask_BxS2_ik0, g_xattn, g_ffn, L0_xattn_Wq, L0_xattn_Wk, L0_xattn_Wv, L0_xattn_Wo, L0_xattn_q_norm_w, L0_xattn_k_norm_w, L0_ffn_Wqkv, L0_ffn_q_scale, L0_ffn_k_scale, L0_ffn_Wo, L0_ffn_ln_g, L0_ffn_ln_b, L0_ffn_W1, L0_ffn_b1, L0_ffn_W2, L0_ffn_b2, L1_xattn_Wq, L1_xattn_bq, L1_xattn_Wk, L1_xattn_bk, L1_xattn_Wv, L1_xattn_bv, L1_xattn_Wo, L1_xattn_bo, L1_ffn_Wr, L1_ffn_br, L1_ffn_W1, L1_ffn_b1, L1_ffn_W2, L1_ffn_b2, L2_xattn_Wq, L2_xattn_Wk, L2_xattn_Wv, L2_xattn_Wo, L2_ffn_gate_w, L2_ffn_gate_b, L2_ffn_expert_w, L2_ffn_expert_b, L3_xattn_wq, L3_xattn_bq, L3_xattn_wk, L3_xattn_bk, L3_xattn_wv, L3_xattn_bv, L3_xattn_wo, L3_xattn_bo, L3_ffn_weight, L3_ffn_ln_gamma, L3_ffn_ln_beta):
    import jax
    import jax.numpy as jnp

    def _L0_xattn_ref(x, context, Wq, Wk, Wv, Wo, q_norm_w, k_norm_w):
        import jax, jax.numpy as jnp
        import numpy as np
        DIM = 128
        N_HEADS = 16
        HEAD_DIM = DIM // N_HEADS
        EPS = 1e-06
        Q_THETA = 32.0
        K_THETA = 1000.0

        def precompute_freqs_1d(dim, seq_len, theta):
            freqs = theta ** (-jnp.arange(0, dim, 2, dtype=jnp.float32) / dim)
            t = jnp.arange(seq_len, dtype=jnp.float32)
            ang = t[:, None] * freqs[None, :]
            return (jnp.cos(ang), jnp.sin(ang))

        def rms_norm(x, w):
            var = jnp.mean(x * x, axis=-1, keepdims=True)
            return x * jax.lax.rsqrt(var + EPS) * w

        def apply_rope(t, cos, sin):
            cos = cos[None, None, :, :]
            sin = sin[None, None, :, :]
            t1, t2 = jnp.split(t, 2, axis=-1)
            return jnp.concatenate([t1 * cos - t2 * sin, t2 * cos + t1 * sin], axis=-1)
        B, T, C = x.shape
        S = context.shape[1]
        H, D = (N_HEADS, HEAD_DIM)
        q = (x @ Wq.T).reshape(B, T, H, D).transpose(0, 2, 1, 3)
        k = (context @ Wk.T).reshape(B, S, H, D).transpose(0, 2, 1, 3)
        v = (context @ Wv.T).reshape(B, S, H, D).transpose(0, 2, 1, 3)
        q = rms_norm(q, q_norm_w)
        k = rms_norm(k, k_norm_w)
        q_cos, q_sin = precompute_freqs_1d(D, T, Q_THETA)
        k_cos, k_sin = precompute_freqs_1d(D, S, K_THETA)
        q = apply_rope(q, q_cos, q_sin)
        k = apply_rope(k, k_cos, k_sin)
        scale = D ** (-0.5)
        attn = jnp.einsum('bhtd,bhsd->bhts', q, k) * scale
        attn = jax.nn.softmax(attn, axis=-1)
        out = jnp.einsum('bhts,bhsd->bhtd', attn, v)
        out = out.transpose(0, 2, 1, 3).reshape(B, T, C)
        return out @ Wo.T

    def _L0_ffn_ref(x, Wqkv, q_scale, k_scale, Wo, ln_g, ln_b, W1, b1, W2, b2):
        import jax, jax.numpy as jnp
        import numpy as np
        DIM = 128
        DEPTH = 6
        HEADS = 16
        DIM_HEAD = 64
        WINDOW = 32
        INNER = HEADS * DIM_HEAD
        DIM_INNER = int(DIM * 4 * 2 / 3)
        QK_SCALE = 8.0

        def shift_tokens(t):
            a, s = jnp.split(t, 2, -1)
            s = jnp.pad(s, ((0, 0), (1, 0), (0, 0)))[:, :-1]
            return jnp.concatenate([a, s], -1)

        def l2norm(t):
            return t / jnp.maximum(jnp.linalg.norm(t, axis=-1, keepdims=True), 1e-12)

        def rotate_half(x):
            x1, x2 = jnp.split(x, 2, -1)
            return jnp.concatenate([-x2, x1], -1)

        def rotary_tables(n):
            half = jnp.arange(0, DIM_HEAD, 2, dtype=jnp.float32)
            inv_freq = 1.0 / 10000.0 ** (half / DIM_HEAD)
            t = jnp.arange(n, dtype=jnp.float32)
            freqs = t[:, None] * inv_freq[None, :]
            freqs = jnp.concatenate([freqs, freqs], -1)
            base_scale = (half + 0.4 * DIM_HEAD) / (1.4 * DIM_HEAD)
            power = (t - n // 2) / (WINDOW // 2)
            scale = base_scale[None, :] ** power[:, None]
            scale = jnp.concatenate([scale, scale], -1)
            return (freqs, scale)

        def local_attention(q, k, v):
            b, h, n, d = q.shape
            w = WINDOW
            nw = n // w
            bq = q.reshape(b, h, nw, w, d)
            bk = k.reshape(b, h, nw, w, d)
            bv = v.reshape(b, h, nw, w, d)

            def look(t):
                p = jnp.pad(t, ((0, 0), (0, 0), (1, 0), (0, 0), (0, 0)))
                return jnp.concatenate([p[:, :, :nw], p[:, :, 1:]], axis=3)
            bk2, bv2 = (look(bk), look(bv))
            seq = jnp.arange(n).reshape(nw, w)
            seq_p = jnp.pad(seq, ((1, 0), (0, 0)), constant_values=-1)
            jt = jnp.concatenate([seq_p[:nw], seq_p[1:]], axis=1)
            it = seq[:, :, None]
            jb = jt[:, None, :]
            mask = (it < jb) | (it > jb + w) | (jb == -1)
            sim = jnp.einsum('bhwie,bhwje->bhwij', bq, bk2) * QK_SCALE
            sim = jnp.where(mask, -jnp.finfo(sim.dtype).max, sim)
            attn = jax.nn.softmax(sim, -1)
            out = jnp.einsum('bhwij,bhwje->bhwie', attn, bv2)
            return out.reshape(b, h, n, d)

        def attn_layer(x, Wqkv, qs, ksc, Wo):
            b, n, _ = x.shape
            qkv = x @ Wqkv
            q, k, v = jnp.split(qkv, 3, -1)
            sh = lambda t: t.reshape(b, n, HEADS, DIM_HEAD).transpose(0, 2, 1, 3)
            q, k, v = (sh(q), sh(k), sh(v))
            q = l2norm(q) * qs
            k = l2norm(k) * ksc
            freqs, scale = rotary_tables(n)
            cos, sin = (jnp.cos(freqs), jnp.sin(freqs))
            q = q * cos * scale + rotate_half(q) * sin * scale
            inv = 1.0 / scale
            k = k * cos * inv + rotate_half(k) * sin * inv
            out = local_attention(q, k, v)
            out = out.transpose(0, 2, 1, 3).reshape(b, n, INNER)
            return out @ Wo

        def ffn_layer(x, g, bln, W1, b1, W2, b2):
            mu = x.mean(-1, keepdims=True)
            var = ((x - mu) ** 2).mean(-1, keepdims=True)
            xn = (x - mu) / jnp.sqrt(var + 1e-05) * g + bln
            hg = xn @ W1 + b1
            a, gate = jnp.split(hg, 2, -1)
            return a * jax.nn.gelu(gate, approximate=False) @ W2 + b2
        for i in range(DEPTH):
            x = attn_layer(shift_tokens(x), Wqkv[i], q_scale[i], k_scale[i], Wo[i]) + x
            x = ffn_layer(shift_tokens(x), ln_g[i], ln_b[i], W1[i], b1[i], W2[i], b2[i]) + x
        return x

    def _L1_xattn_ref(q, k, v, mask, Wq, bq, Wk, bk, Wv, bv, Wo, bo):
        import jax, jax.numpy as jnp
        import numpy as np
        D_MODEL = 128
        N_HEAD = 16
        B, S = (2, 256)
        H = N_HEAD
        b, s, d = q.shape
        dh = d // H

        def split_heads(x, W, bias):
            y = x @ W.T + bias
            return y.reshape(b, -1, H, dh).transpose(2, 0, 1, 3)
        qh = split_heads(q, Wq, bq)
        kh = split_heads(k, Wk, bk)
        vh = split_heads(v, Wv, bv)
        scale = 1.0 / jnp.sqrt(jnp.float32(dh))
        scores = jnp.einsum('hbsd,hbtd->hbst', qh, kh) * scale
        scores = jnp.where(mask == 0, jnp.float32(-1000000000.0), scores)
        attn = jax.nn.softmax(scores, axis=-1)
        out = jnp.einsum('hbst,hbtd->hbsd', attn, vh)
        out = out.transpose(1, 2, 0, 3).reshape(b, s, d)
        return out @ Wo.T + bo

    def _L1_ffn_ref(x, Wr, br, W1, b1, W2, b2):
        import jax, jax.numpy as jnp
        import numpy as np
        TOP_K = 2
        k = TOP_K
        scores0 = x[:, 0, :] @ Wr + br
        _, idx = jax.lax.top_k(scores0, k)
        W1g, b1g = (W1[idx], b1[idx])
        W2g, b2g = (W2[idx], b2[idx])
        h = jnp.einsum('bsd,bkde->bkse', x, W1g) + b1g[:, :, None, :]
        h = jax.nn.gelu(h, approximate=False)
        o = jnp.einsum('bkse,bkef->bksf', h, W2g) + b2g[:, :, None, :]
        return jnp.sum(o, axis=1) / k

    def _L2_xattn_ref(H, T, mask, Wq, Wk, Wv, Wo):
        import jax, jax.numpy as jnp
        import numpy as np
        HEADS = 16
        DIM_Q = 128
        DIM_KV = 128
        INNER = 128
        B, Lq, _ = H.shape
        Lkv = T.shape[1]
        dph = INNER // HEADS

        def shape(x, L):
            return x.reshape(B, L, HEADS, dph).transpose(0, 2, 1, 3)
        q = shape(H @ Wq, Lq) * dph ** (-0.5)
        k = shape(T @ Wk, Lkv)
        v = shape(T @ Wv, Lkv)
        scores = jnp.einsum('bhqd,bhkd->bhqk', q, k)
        ext = (1.0 - mask.astype(scores.dtype))[:, None, None, :] * jnp.finfo(scores.dtype).min
        scores = scores + ext
        attn = jax.nn.softmax(scores.astype(jnp.float32), axis=-1).astype(scores.dtype)
        out = jnp.einsum('bhqk,bhkd->bhqd', attn, v)
        out = out.transpose(0, 2, 1, 3).reshape(B, Lq, INNER)
        return out @ Wo

    def _L2_ffn_ref(x, gate_w, gate_b, expert_w, expert_b):
        import jax, jax.numpy as jnp
        import numpy as np
        NEG_INF = -1e+30
        K = 2
        pooled = x.mean(axis=1)
        logits = pooled @ gate_w.T + gate_b
        topk_vals, _ = jax.lax.top_k(logits, K)
        min_topk = topk_vals[:, -1:]
        masked = jnp.where(logits < min_topk, -jnp.inf, logits)
        gates = jax.nn.softmax(masked, axis=-1)
        expert_out = jax.nn.gelu(jnp.einsum('bsd,eod->beso', x, expert_w) + expert_b[None, :, None, :], approximate=False)
        return jnp.einsum('be,beso->bso', gates, expert_out)

    def _L3_xattn_ref(query, key, value, wq, bq, wk, bk, wv, bv, wo, bo):
        import jax, jax.numpy as jnp
        import numpy as np
        FEATURE_DIM = 128
        NUM_HEADS = 16
        HEAD_DIM = FEATURE_DIM // NUM_HEADS
        B, SQ, D = query.shape
        H, HD = (NUM_HEADS, HEAD_DIM)
        q = (query @ wq.T + bq).reshape(B, SQ, H, HD).transpose(0, 2, 1, 3)
        k = (key @ wk.T + bk).reshape(B, -1, H, HD).transpose(0, 2, 1, 3)
        v = (value @ wv.T + bv).reshape(B, -1, H, HD).transpose(0, 2, 1, 3)
        scores = jnp.einsum('bhqd,bhkd->bhqk', q, k) / jnp.sqrt(jnp.asarray(HD, q.dtype))
        attn = jax.nn.softmax(scores, axis=-1)
        ctx = jnp.einsum('bhqk,bhkd->bhqd', attn, v)
        ctx = ctx.transpose(0, 2, 1, 3).reshape(B, SQ, D)
        return ctx @ wo.T + bo

    def _L3_ffn_ref(x, weight, ln_gamma, ln_beta):
        import jax, jax.numpy as jnp
        import numpy as np
        LN_EPS = 0.001
        EPS = 1e-05
        QB = 128.0

        def ste_round(x):
            return x + jax.lax.stop_gradient(jnp.round(x) - x)
        mu = jnp.mean(x, axis=-1, keepdims=True)
        var = jnp.var(x, axis=-1, keepdims=True)
        xn = (x - mu) * jax.lax.rsqrt(var + LN_EPS) * ln_gamma + ln_beta
        beta = jnp.mean(jnp.abs(weight))
        w_q = jnp.clip(ste_round(weight / (beta + EPS)), -1.0, 1.0)
        gamma = jnp.max(jnp.abs(xn))
        xq = jnp.clip(xn * QB / gamma, -QB + EPS, QB - EPS)
        y = jnp.einsum('bsd,du->bsu', xq, w_q)
        return y * (gamma * beta / QB)
    x = x + jnp.tanh(g_xattn[0]) * _L0_xattn_ref(_layernorm(x, axis=-1), ctx_1024, L0_xattn_Wq, L0_xattn_Wk, L0_xattn_Wv, L0_xattn_Wo, L0_xattn_q_norm_w, L0_xattn_k_norm_w)
    x = x + jnp.tanh(g_ffn[0]) * _L0_ffn_ref(_layernorm(x, axis=-1), L0_ffn_Wqkv, L0_ffn_q_scale, L0_ffn_k_scale, L0_ffn_Wo, L0_ffn_ln_g, L0_ffn_ln_b, L0_ffn_W1, L0_ffn_b1, L0_ffn_W2, L0_ffn_b2)
    x = x + jnp.tanh(g_xattn[1]) * _L1_xattn_ref(_layernorm(x, axis=-1), ctx_1024, ctx_1024, mask_SxS2_ik0, L1_xattn_Wq, L1_xattn_bq, L1_xattn_Wk, L1_xattn_bk, L1_xattn_Wv, L1_xattn_bv, L1_xattn_Wo, L1_xattn_bo)
    x = x + jnp.tanh(g_ffn[1]) * _L1_ffn_ref(_layernorm(x, axis=-1), L1_ffn_Wr, L1_ffn_br, L1_ffn_W1, L1_ffn_b1, L1_ffn_W2, L1_ffn_b2)
    x = x + jnp.tanh(g_xattn[2]) * _L2_xattn_ref(_layernorm(x, axis=-1), ctx_1024, mask_BxS2_ik0, L2_xattn_Wq, L2_xattn_Wk, L2_xattn_Wv, L2_xattn_Wo)
    x = x + jnp.tanh(g_ffn[2]) * _L2_ffn_ref(_layernorm(x, axis=-1), L2_ffn_gate_w, L2_ffn_gate_b, L2_ffn_expert_w, L2_ffn_expert_b)
    x = x + jnp.tanh(g_xattn[3]) * _L3_xattn_ref(_layernorm(x, axis=-1), ctx_1024, ctx_1024, L3_xattn_wq, L3_xattn_bq, L3_xattn_wk, L3_xattn_bk, L3_xattn_wv, L3_xattn_bv, L3_xattn_wo, L3_xattn_bo)
    x = x + jnp.tanh(g_ffn[3]) * _L3_ffn_ref(_layernorm(x, axis=-1), L3_ffn_weight, L3_ffn_ln_gamma, L3_ffn_ln_beta)
    return x

_drawn_inputs = setup_inputs


def setup_inputs(seed=0):
    import zlib

    import numpy as np

    out = dict(_drawn_inputs(seed))
    spreads = {'L0_xattn_q_norm_w': (1.0, 0.6),
     'L0_xattn_k_norm_w': (1.0, 0.6),
     'L0_ffn_q_scale': (1.0, 0.6),
     'L0_ffn_k_scale': (1.0, 0.6),
     'L0_ffn_ln_g': (1.0, 0.6),
     'L0_ffn_ln_b': (0.0, 0.8),
     'L0_ffn_b1': (0.0, 0.358),
     'L0_ffn_b2': (0.0, 0.1),
     'L1_ffn_br': (0.0, 0.1),
     'L1_ffn_b1': (0.0, 0.1),
     'L1_ffn_b2': (0.0, 0.1),
     'L2_ffn_gate_b': (0.0, 0.1),
     'L2_ffn_expert_b': (0.0, 0.1),
     'L3_xattn_bq': (0.0, 0.421),
     'L3_xattn_bk': (0.0, 2.0),
     'L3_xattn_bv': (0.0, 0.1),
     'L3_xattn_bo': (0.0, 0.1),
     'L3_ffn_ln_gamma': (1.0, 0.552),
     'L3_ffn_ln_beta': (0.0, 0.641)}
    factors = {'L1_xattn_bk': 200.0, 'L2_xattn_Wq': 8.0, 'L2_xattn_Wk': 8.0, 'g_ffn': 22.16}
    for name, (base, spread) in spreads.items():
        noise = np.random.default_rng([zlib.crc32(name.encode()), seed]).standard_normal(out[name].shape)
        drawn = base * np.exp(spread * noise) if base else spread * noise
        out[name] = jnp.asarray(drawn.astype(out[name].dtype))
    for name, factor in factors.items():
        out[name] = (out[name] * factor).astype(out[name].dtype)
    return out
```

```python
from contextlib import ExitStack

import numpy as np

import concourse.bass as bass
from concourse import mybir

F32 = mybir.dt.float32
F32R = mybir.dt.float32r
BF16 = mybir.dt.bfloat16
I32 = mybir.dt.int32
ALU = mybir.AluOpType
ACT = mybir.ActivationFunctionType
AX = mybir.AxisListType

P = 128
NB, SEQ = 8, 256
TOK = NB * SEQ
HEADS = 16
HD = P // HEADS
DEPTH, LHD, WIN = 6, 64, 32
INNER = HEADS * LHD
FFN_IN = int(P * 4 * 2 / 3)
FFC = -(-FFN_IN // P)
EXPERTS = 8
KSPAN = P + WIN
PACK = KSPAN + P
MASKED = -(2.0 ** 100)
C = 512

W_NAMES = (["q0", "q0r", "k0", "k0r", "v0", "o0", "q1", "k1", "v1", "o1", "q2", "k2", "v2", "o2", "q3", "k3", "v3", "o3"]
           + [f"m1_{e}" for e in range(EXPERTS)] + [f"m2_{e}" for e in range(EXPERTS)]
           + [f"e_{e}" for e in range(EXPERTS)] + ["quant"])
W_AT = {n: P * i for i, n in enumerate(W_NAMES)}
V_NAMES = (["bq1", "bk1", "bv1", "bo1", "bq3", "bk3", "bv3", "bo3", "qn", "qnr", "kn", "knr", "gamma", "beta", "zero"]
           + [f"mb1_{e}" for e in range(EXPERTS)] + [f"mb2_{e}" for e in range(EXPERTS)]
           + [f"eb_{e}" for e in range(EXPERTS)] + [f"r1_{e}" for e in range(EXPERTS)] + [f"r2_{e}" for e in range(EXPERTS)])
V_AT = {n: i for i, n in enumerate(V_NAMES)}
D_QKV, D_WO, D_W1, D_W2 = 0, 3 * INNER, 3 * INNER + 8 * P, 3 * INNER + 8 * P + 2 * FFC * P
D_VEC = D_W2 + FFC * P
D_ALL = D_VEC + 3 + 2 * FFC
F_AT, B_AT = {}, {}


def constants():
    f, b = {}, {}
    eye = np.eye(P)
    f["ident"] = eye
    f["mean"] = np.full((P, P), 1.0 / P)
    f["center"] = eye - 1.0 / P
    f["ones"] = np.ones((P, P))
    p = np.arange(P)
    f["headmean"] = (p[:, None] // HD == p[None, :] // HD) / HD
    f["headmask"] = (p[:, None] // HD == np.arange(HEADS)[None, :]) * 1.0
    opad = np.zeros((P, 4, 32))
    for j in range(4):
        opad[:, j, HD * j:HD * j + HD] = 1.0
    f["sumpad"] = opad.reshape(P, -1)
    osel = np.zeros((P, 4, 32))
    osel[:, :, 4:] = 1.0
    for j in range(4):
        osel[:, j, j] = 1.0
    f["sumsel"] = osel.reshape(P, -1)
    t = np.arange(SEQ)
    d = p % HD
    for n, theta, scale in (("q", 32.0, HD ** -0.5), ("k", 1000.0, 1.0)):
        fr = np.float32(theta) ** (-(np.arange(0, HD, 2, dtype=np.float32)) / np.float32(HD))
        ang = (t[None, :].astype(np.float32) * fr[d % (HD // 2)][:, None]).astype(np.float64)
        f[n + "cos"] = np.cos(ang) * scale
        f[n + "sin"] = np.sin(ang) * np.where(d < HD // 2, -1.0, 1.0)[:, None] * scale
    half = np.arange(0, LHD, 2, dtype=np.float32)
    inv = (1.0 / np.float32(10000.0) ** (half / np.float32(LHD))).astype(np.float32)
    fr = (t[:, None].astype(np.float32) * inv[None, :]).astype(np.float64)
    fr = np.concatenate([fr, fr], -1)
    base = (half.astype(np.float64) + 0.4 * LHD) / (1.4 * LHD)
    power = (t - SEQ // 2) / (WIN // 2)
    sc = base[None, :] ** power[:, None]
    sc = np.concatenate([sc, sc], -1)
    sign = np.where(np.arange(LHD) < LHD // 2, -1.0, 1.0)[None, :]
    for n, s in (("lq", 8.0 * sc), ("lk", 1.0 / sc)):
        for w, tab in (("cos", np.cos(fr) * s), ("sin", np.sin(fr) * sign * s)):
            f[n + w] = tab.reshape(2, P, LHD).transpose(1, 0, 2).reshape(P, -1)
    e = np.arange(EXPERTS)
    for n, v in (("eps5", 1e-5), ("eps6", 1e-6), ("eps3", 1e-3), ("lnoff", 10 * np.log(2.0))):
        f[n] = np.full((P, 1), v)
    f["earlier"] = np.broadcast_to((e[None, :] < e[:, None]).reshape(1, -1) * 1.0, (P, EXPERTS * EXPERTS))
    b["ident"] = eye
    first = np.zeros((P, P))
    first[0] = 1.0
    b["first"] = first
    sel = np.zeros((P, HEADS, P))
    for h in range(HEADS):
        sel[h, h] = 1.0
        sel[32 + h, h] = 1.0
    b["sel"] = sel.reshape(P, -1)
    selr = np.zeros((P, HEADS // 2, P))
    for c in range(HEADS // 2):
        for m in range(P):
            h = 2 * c + m // LHD
            selr[32 * (h % 4) + h // 4, c, m] = 1.0
    b["selr"] = selr.reshape(P, -1)
    q0, k0 = np.arange(P)[:, None], np.arange(P)[None, :]
    b["band0"] = np.where((q0 - k0 >= 0) & (q0 - k0 <= WIN), 0.0, MASKED)
    k1 = np.arange(KSPAN)[None, :]
    b["band1"] = np.where((q0 - k1 + WIN >= 0) & (q0 - k1 + WIN <= WIN), 0.0, MASKED)
    qq = np.arange(KSPAN)[None, :]
    b["bandT"] = np.where((qq - q0 >= 0) & (qq - q0 <= WIN), 0.0, MASKED)
    out = []
    for tables, at in ((f, F_AT), (b, B_AT)):
        n = 0
        for name, tab in tables.items():
            at[name] = n
            n += tab.shape[1]
        out.append(np.concatenate([np.asarray(v, np.float64) for v in tables.values()], axis=1))
    return out


F_TAB, B_TAB = constants()



class Chain:

    def __init__(self, eng, sem):
        self.eng, self.sem, self.n, self.off = eng, sem, 0, 0

    def start(self, off):
        self.n, self.off = 0, off

    def link(self, ins):
        ins.then_inc(self.sem, 1)
        self.n += 1
        self.eng.wait_ge(self.sem, self.off + self.n)

    def ends(self, n):
        assert self.n == n, (self.n, n)


class Core:

    def __init__(self, nc, ctx, a):
        self.nc, self.a, self.ctx = nc, a, ctx
        sb = self.sb
        self.x = sb("x", [P, TOK], F32)
        self.y = sb("y", [P, TOK], F32)
        self.ctxT = sb("ctxT", [P, TOK], F32)
        self.w = sb("w", [P, P * len(W_NAMES)], F32)
        self.v = sb("v", [P, len(V_NAMES)], F32)
        self.cf = sb("cf", [P, F_TAB.shape[1]], F32)
        self.cb = sb("cb", [P, B_TAB.shape[1]], BF16)
        self.gates = sb("gates", [P, 8], F32)
        self.gbo = sb("gbo", [P, 4], F32)
        self.rbias = sb("rbias", [P, 2 * EXPERTS], F32)
        self.maskq = sb("maskq", [P, 2, SEQ], BF16)
        self.maskk = sb("maskk", [P, 2, SEQ], BF16)
        self.padrow = sb("padrow", [P, TOK], BF16)
        self.padcol = sb("padcol", [P, 2 * NB], F32)
        self.ring = ctx.enter_context(nc.psum_tensor("ring", [P, 2, C], F32))
        self.st = ctx.enter_context(nc.psum_tensor("st", [P, 4, C], F32))
        self.ov = ctx.enter_context(nc.psum_tensor("ov", [P, C], F32))
        self.sm = ctx.enter_context(nc.psum_tensor("sm", [P, C], F32))
        self.sems = {}

    def sb(self, name, shape, dt):
        return self.ctx.enter_context(self.nc.sbuf_tensor(name, shape, dt))

    def sem(self, name):
        if name not in self.sems:
            self.sems[name] = self.ctx.enter_context(self.nc.semaphore(name))
        return self.sems[name]

    def f(self, name, width=P):
        return self.cf[:, F_AT[name]:F_AT[name] + width]

    def b(self, name, width=P):
        return self.cb[:, B_AT[name]:B_AT[name] + width]

    def wm(self, name):
        return self.w[:, W_AT[name]:W_AT[name] + P]

    def vec(self, name, n=1):
        return self.v[:, V_AT[name]:V_AT[name] + n]


def cols(c, width=C):
    return bass.ds(c * width, width)


def load_everything(g, tmp):
    nc, a = g.nc, g.a
    loaded, prepared = g.sem("inputs_loaded"), g.sem("inputs_prepared")
    mask_q, mask_k, pad_r, pad_c = (tmp(n, s, I32) for n, s in (
        ("mask_q", [P, 2, SEQ]), ("mask_k", [P, 2, SEQ]), ("pad_r", [1, TOK]), ("pad_c", [P, 2 * NB])))
    loads = ((g.x[:, :], a["xT"]), (g.cf[:, :], a["cf"]), (g.ctxT[:, :], a["ctxT"]),
             (g.w[:, :], a["w"]), (g.cb[:, :], a["cb"]), (g.v[:, :], a["v"]),
             (mask_q[:, :, :], a["mask_q"]), (mask_k[:, :, :], a["mask_k"]), (pad_r[:, :], a["pad_r"]),
             (pad_c[:, :], a["pad_c"]), (g.gates[:, :], a["gates"].broadcast_to([P, 8])),
             (g.rbias[:, :], a["rbias"].broadcast_to([P, 2 * EXPERTS])))
    with nc.Block() as block:
        @block.sync
        def _(sp):
            for dst, src in loads:
                sp.dma_start(dst, src).then_inc(loaded, 16)
            sp.wait_ge(loaded, 16 * len(loads))

        @block.scalar
        def _(act):
            act.wait_ge(loaded, 16 * len(loads))
            act.activation(g.gates[:, :], g.gates[:, :], ACT.Tanh).then_inc(prepared, 1)

        @block.vector
        def _(dve):
            dve.memset(g.padrow[:, :], 0.0).then_inc(prepared, 1)
            dve.wait_ge(loaded, 16 * len(loads))
            dve.tensor_scalar(g.maskq[:, :, :], mask_q[:, :, :], 0.0, MASKED, ALU.is_equal, ALU.mult)
            dve.tensor_scalar(g.maskk[:, :, :], mask_k[:, :, :], 0.0, MASKED, ALU.is_equal, ALU.mult)
            dve.tensor_scalar(g.padcol[:, :], pad_c[:, :], 0.0, MASKED, ALU.is_equal, ALU.mult)
            dve.wait_ge(prepared, 2)
            dve.tensor_scalar(g.padrow[0:1, :], pad_r[:, :], 0.0, MASKED, ALU.is_equal, ALU.mult)
            for l in range(4):
                bo = g.vec(f"bo{l}") if l in (1, 3) else g.vec("zero")
                dve.tensor_tensor(g.gbo[:, l:l + 1], g.gates[:, l:l + 1], bo, ALU.mult)


def layernorm(g, use, src, out, eps, tmp, scale=None, shift=None):
    nc = g.nc
    centered, squared, variance, rstd, normed = (
        g.sem("ln_" + n) for n in ("centered", "squared", "variance", "rstd", "normed"))
    sq, rs = tmp("ln_sq", [P, 2, C], F32), tmp("ln_rs", [P, 2, C], F32)
    base = use * 4
    with nc.Block() as block:
        @block.tensor
        def _(pe):
            with pe.Fori(0, 2) as k:
                for u in range(2):
                    pe.matmul(g.st[:, u, :], g.f("center"), src(k * 2 + u), start=True, stop=True).then_inc(centered, 1)
                for u in range(2):
                    pe.wait_ge(squared, base + k * 2 + u + 1)
                    pe.matmul(g.st[:, 2 + u, :], g.f("mean"), sq[:, u, :], start=True, stop=True).then_inc(variance, 1)
                pe.wait_ge(normed, base + k * 2 + 2)

        @block.scalar
        def _(act):
            with act.Fori(0, 2) as k:
                for u in range(2):
                    act.wait_ge(centered, base + k * 2 + u + 1)
                    act.activation(sq[:, u, :], g.st[:, u, :], ACT.Square).then_inc(squared, 1)
                for u in range(2):
                    act.wait_ge(variance, base + k * 2 + u + 1)
                    act.activation(rs[:, u, :], g.st[:, 2 + u, :], ACT.Ln, bias=g.f(eps, 1)).then_inc(rstd, 1)
                    act.wait_ge(rstd, 2 * (base + k * 2 + u) + 1)
                    act.activation(rs[:, u, :], rs[:, u, :], ACT.Exp, scale=-0.5).then_inc(rstd, 1)

        @block.vector
        def _(dve):
            affine = g.sem("ln_affine")
            with dve.Fori(0, 2) as k:
                for u in range(2):
                    dve.wait_ge(rstd, 2 * (base + k * 2 + u) + 2)
                    dve.tensor_tensor(out(k * 2 + u), g.st[:, u, :], rs[:, u, :], ALU.mult).then_inc(normed, 1)
                    if scale is not None:
                        dve.wait_ge(normed, base + k * 2 + u + 1)
                        dve.tensor_scalar(out(k * 2 + u), out(k * 2 + u), scale, shift, ALU.mult, ALU.add)


def project(g, l, q_all, k_all, tmp):
    nc = g.nc
    lane = (l - 1) * 4
    filled = g.sem("proj_filled" if l else "rope_filled")
    out_done = g.sem("proj_done" if l else "rope_done")
    if l:
        with nc.Block() as block:
            @block.tensor
            def _(pe):
                with pe.Fori(0, 2) as k:
                    for u in range(2):
                        pe.matmul(g.st[:, 2 * u, :], g.wm(f"q{l}"), g.y[:, cols(k * 2 + u)], start=True, stop=True)
                        pe.matmul(g.st[:, 2 * u + 1, :], g.wm(f"k{l}"), g.ctxT[:, cols(k * 2 + u)],
                                  start=True, stop=True).then_inc(filled, 1)
                    pe.wait_ge(out_done, lane + k * 2 + 2)

            @block.vector
            def _(dve):
                with dve.Fori(0, 2) as k:
                    for u in range(2):
                        dve.wait_ge(filled, lane + k * 2 + u + 1)
                        dve.tensor_scalar(q_all[:, cols(k * 2 + u)], g.st[:, 2 * u, :],
                                          g.vec(f"bq{l}" if l != 2 else "zero"), None, ALU.add)
                        dve.tensor_scalar(k_all[:, cols(k * 2 + u)], g.st[:, 2 * u + 1, :],
                                          g.vec(f"bk{l}" if l != 2 else "zero"), HD ** -0.5,
                                          ALU.add, ALU.mult).then_inc(out_done, 1)
        return

    squared, mean_sq, rstd = g.sem("head_squared"), g.sem("head_mean_sq"), g.sem("head_rstd")
    rotated = g.sem("head_rotated")
    sq, rs, t1, t2 = (tmp(n, [P, 2, C], F32) for n in ("rope_sq", "rope_rs", "rope_t1", "rope_t2"))
    outs = (q_all, k_all)
    with nc.Block() as block:
        @block.tensor
        def _(pe):
            with pe.Fori(0, 4) as c:
                for i, (n, src) in enumerate((("q", g.y), ("k", g.ctxT))):
                    pe.matmul(g.st[:, 2 * i, :], g.wm(n + "0"), src[:, cols(c)], start=True, stop=True)
                    pe.matmul(g.st[:, 2 * i + 1, :], g.wm(n + "0r"), src[:, cols(c)],
                              start=True, stop=True).then_inc(filled, 1)
                for i in range(2):
                    pe.wait_ge(squared, c * 2 + i + 1)
                    pe.matmul(g.ring[:, i, :], g.f("headmean"), sq[:, i, :], start=True, stop=True).then_inc(mean_sq, 1)
                pe.wait_ge(out_done, c * 2 + 2)

        @block.scalar
        def _(act):
            with act.Fori(0, 4) as c:
                for i in range(2):
                    act.wait_ge(filled, c * 2 + i + 1)
                    act.activation(sq[:, i, :], g.st[:, 2 * i, :], ACT.Square).then_inc(squared, 1)
                for i in range(2):
                    act.wait_ge(mean_sq, c * 2 + i + 1)
                    act.activation(rs[:, i, :], g.ring[:, i, :], ACT.Ln, bias=g.f("eps6", 1)).then_inc(rstd, 1)
                    act.wait_ge(rstd, 2 * (c * 2 + i) + 1)
                    act.activation(rs[:, i, :], rs[:, i, :], ACT.Exp, scale=-0.5).then_inc(rstd, 1)

        @block.vector
        def _(dve):
            def per_batch(ap):
                return ap.rearrange("p (b s) -> p b s", b=2)

            def twice(name):
                return g.f(name, SEQ).unsqueeze(1).broadcast_to([P, 2, SEQ])

            with dve.Fori(0, 4) as c:
                for i, n in enumerate("qk"):
                    dve.wait_ge(squared, c * 2 + i + 1)
                    dve.scalar_tensor_tensor(out=per_batch(t1[:, i, :]), in0=per_batch(g.st[:, 2 * i, :]),
                                             scalar=g.vec(n + "n"), in1=twice(n + "cos"), op0=ALU.mult, op1=ALU.mult)
                    dve.scalar_tensor_tensor(out=per_batch(t2[:, i, :]), in0=per_batch(g.st[:, 2 * i + 1, :]),
                                             scalar=g.vec(n + "nr"), in1=twice(n + "sin"),
                                             op0=ALU.mult, op1=ALU.mult).then_inc(rotated, 1)
                    dve.wait_ge(rotated, 2 * (c * 2 + i) + 1)
                    dve.tensor_tensor(t1[:, i, :], t1[:, i, :], t2[:, i, :], ALU.add).then_inc(rotated, 1)
                for i in range(2):
                    dve.wait_ge(rotated, 2 * (c * 2 + i) + 2)
                    dve.wait_ge(rstd, 2 * (c * 2 + i) + 2)
                    dve.tensor_tensor(outs[i][:, cols(c)], t1[:, i, :], rs[:, i, :], ALU.mult).then_inc(out_done, 1)


def head_at(n):
    return 4 * (n % 4) + n // 4


def cross_attention(g, l, q_all, k_all, tmp):
    nc = g.nc
    filled, ring_dve = g.sem("x_ring_filled"), g.sem("x_ring_read")
    keys_staged, queries_r, queries_f = g.sem("x_keys_staged"), g.sem("x_queries_r"), g.sem("x_queries_f")
    scores_ready, probs_ready = g.sem("x_scores_ready"), g.sem("x_probs_ready")
    values_summed, sums_read, out_ready = g.sem("x_values_summed"), g.sem("x_sums_read"), g.sem("x_out_ready")
    own = g.sem("x_dve_own")
    vpad_zeroed, pad_staged = g.sem("x_vpad_zeroed"), g.sem("x_pad_staged")
    qm = [tmp(f"qm{u}", [P, HEADS, SEQ], F32) for u in range(2)]
    qmr = [tmp(f"qmr{u}", [P, HEADS, SEQ], F32R) for u in range(2)]
    kt = [tmp(f"kt{u}", [P, SEQ], F32) for u in range(2)]
    ktr = [tmp(f"ktr{u}", [P, SEQ], F32R) for u in range(2)]
    cs = [tmp(f"cs{u}", [P, SEQ], F32) for u in range(2)]
    vpad = [tmp(f"vpad{u}", [P, 2, 4 * 160], F32) for u in range(2)]
    pt = tmp("pt", [P, 8, C], F32)
    mrow = [tmp(f"mrow{u}", [P, 2 * HEADS], F32) for u in range(2)]
    mt = [tmp(f"mt{u}", [P, SEQ], BF16) for u in range(2)]
    on = [tmp(f"on{u}", [P, SEQ], F32) for u in range(2)]
    rsum = tmp("rsum", [P, SEQ], F32)
    upd = tmp("upd", [P, SEQ], F32)
    pad = [tmp(f"pad{u}", [P, 2], F32) for u in range(2)]
    ring = g.ring
    layer_items = 8 * 19
    first = 18

    def item(b, k):
        return l * layer_items + first + 19 * b + k

    with nc.Block() as block:
        @block.tensor
        def _(pe):
            def claim(n):
                pe.wait_ge(ring_dve, n - 1)

            def values(u, b, n, slot):
                pe.wait_ge(keys_staged, 3 * (l * 8 + b) + 2)
                for t in range(2):
                    mm = pe.matmul(ring[:, slot, t * P:(t + 1) * P], cs[u][:, t * P:(t + 1) * P], g.wm(f"v{l}"),
                                   start=True, stop=True)
                mm.then_inc(filled, 1)

            def row_scores(u, b, i, slot):
                t, h0 = i // 8, i % 8 * 2
                for h in (h0, h0 + 1):
                    out = ring[:, slot, (h - h0) * SEQ:(h - h0 + 1) * SEQ]
                    mm = pe.matmul(out, qmr[u][:, h, t * P:(t + 1) * P], ktr[u][:, :], start=True, stop=l not in (1, 2))
                    if l == 1:
                        mm = pe.matmul(out, g.b("ident"), g.maskq[:, t, :], start=False, stop=True)
                    if l == 2:
                        mm = pe.matmul(out, g.b("first"), g.padrow[:, cols(b, SEQ)], start=False, stop=True)
                mm.then_inc(filled, 1)

            def turn_maxima(u, slot):
                for t in range(2):
                    mm = pe.transpose(ring[0:HEADS, slot, t * P:(t + 1) * P], mrow[u][:, t * HEADS:(t + 1) * HEADS],
                                      g.f("ident"))
                mm.then_inc(filled, 1)

            def scores(u, b, quad):
                for j in range(4 * quad, 4 * quad + 4):
                    pair, kc = j // 2, j % 2
                    if j >= 4:
                        pe.wait_ge(probs_ready, 16 * (l * 8 + b) + j - 3)
                    for x in range(2):
                        h = head_at(2 * pair + x)
                        out = g.st[:, j % 4, x * SEQ:(x + 1) * SEQ]
                        pe.matmul(out, kt[u][:, kc * P:(kc + 1) * P], qm[u][:, h, :], start=True, stop=False)
                        if l == 1:
                            pe.matmul(out, g.b("ident"), g.maskk[:, kc, :], start=False, stop=False)
                        mm = pe.matmul(out, g.cb[:, B_AT["sel"] + h * P:B_AT["sel"] + (h + 1) * P], mt[u][:, :],
                                       start=False, stop=True)
                    mm.then_inc(scores_ready, 1)

            def sum_values(u, b, quad):
                pe.wait_ge(probs_ready, 16 * (l * 8 + b) + 4 * (quad + 1))
                for bank, lhs in ((g.ov, lambda kc, c: vpad[u][:, kc, c * 160 + 32 * quad:c * 160 + 32 * quad + 32]),
                                  (g.sm, lambda kc, c: g.cf[:, F_AT["sumpad"] + 32 * quad:F_AT["sumpad"] + 32 * quad + 32])):
                    for kc in range(2):
                        for c in range(4):
                            n = 4 * quad + c
                            mm = pe.matmul(bank[32 * c:32 * c + 32, 0:SEQ], lhs(kc, c),
                                           pt[:, (2 * (n // 2) + kc) % 8, (n % 2) * SEQ:(n % 2 + 1) * SEQ],
                                           start=quad == 0 and kc == 0, stop=quad == 3 and kc == 1)
                mm.then_inc(values_summed, 1)

            def body(b, u, more):
                n, s = item(b, 0), u
                if more:
                    claim(n)
                    values(1 - u, b + 1, n, s % 2)
                    pe.wait_ge(queries_r, l * 8 + b + 2)
                    pe.wait_ge(keys_staged, 3 * (l * 8 + b + 1) + 1)
                pe.wait_ge(queries_f, l * 8 + b + 1)
                pe.wait_ge(keys_staged, 3 * (l * 8 + b) + 3)
                pe.wait_ge(ring_dve, n - 1)
                for quad in range(4):
                    scores(u, b, quad)
                    if more and quad < 3:
                        for i in range((0, 5, 10)[quad], (5, 10, 16)[quad]):
                            claim(n + 1 + i)
                            row_scores(1 - u, b + 1, i, (s + 1 + i) % 2)
                    if quad == 3 and more:
                        pe.wait_ge(ring_dve, n + 17)
                        turn_maxima(1 - u, (s + 17) % 2)
                    if quad:
                        sum_values(u, b, quad - 1)
                sum_values(u, b, 3)
                k = 18 if more else 0
                claim(n + k)
                pe.wait_ge(out_ready, l * 8 + b + 1)
                pe.matmul(ring[:, (s + k) % 2, 0:SEQ], g.wm(f"o{l}"), on[u][:, :], start=True, stop=True).then_inc(filled, 1)

            pe.wait_ge(vpad_zeroed, l + 1)
            values(0, 0, 0, 0)
            pe.wait_ge(queries_r, l * 8 + 1)
            for i in range(16):
                if i >= 1:
                    claim(l * layer_items + 1 + i)
                row_scores(0, 0, i, (1 + i) % 2)
            pe.wait_ge(ring_dve, l * layer_items + 17)
            turn_maxima(0, 1)
            pe.wait_ge(ring_dve, l * layer_items + first)
            with pe.Fori(0, 3) as k:
                body(k * 2, 0, True)
                body(k * 2 + 1, 1, True)
            body(6, 0, True)
            body(7, 1, False)

        @block.scalar
        def _(act):
            def stage_r(u, b):
                act.activation(ktr[u][:, :], k_all[:, cols(b, SEQ)], ACT.Copy).then_inc(keys_staged, 1)

            def stage_ctx(u, b):
                act.activation(cs[u][:, :], g.ctxT[:, cols(b, SEQ)], ACT.Copy).then_inc(keys_staged, 1)

            def stage_pad(u, b):
                act.activation(pad[u][:, :], g.padcol[:, bass.ds(b * 2, 2)], ACT.Copy).then_inc(pad_staged, 1)

            def stage_f(u, b):
                act.activation(kt[u][:, :], k_all[:, cols(b, SEQ)], ACT.Copy).then_inc(keys_staged, 1)

            def body(b, u, more, stage):
                if more:
                    stage_ctx(1 - u, b + 1)
                    stage_f(1 - u, b + 1)
                if l == 2:
                    act.wait_ge(pad_staged, b + 1)
                for j in range(16):
                    act.wait_ge(scores_ready, 16 * (l * 8 + b) + j + 1)
                    if j >= 8:
                        act.wait_ge(values_summed, 4 * (l * 8 + b) + j // 4 - 1)
                    kw = {"bias": pad[u][:, j % 2:j % 2 + 1]} if l == 2 else {}
                    act.activation(pt[:, j % 8, :], g.st[:, j % 4, :], ACT.Exp, **kw).then_inc(probs_ready, 1)
                    if j == 0 and l == 2 and more:
                        stage_pad(1 - u, b + 1)
                    if j == 11 and stage:
                        stage_r(u, b + 2)

            stage_r(0, 0)
            stage_ctx(0, 0)
            stage_f(0, 0)
            if l == 2:
                stage_pad(0, 0)
            stage_r(1, 1)
            with act.Fori(0, 3) as k:
                body(k * 2, 0, True, True)
                body(k * 2 + 1, 1, True, True)
            body(6, 0, True, False)
            body(7, 1, False, False)

        @block.vector
        def _(dve):
            chain = Chain(dve, own)

            def queries(dst, u, b, sem):
                for h in range(HEADS):
                    ins = dve.tensor_scalar(dst[u][:, h, :], q_all[:, cols(b, SEQ)], g.f("headmask", HEADS)[:, h:h + 1],
                                            None, ALU.mult)
                ins.then_inc(sem, 1)

            def values(u, n, slot):
                dve.wait_ge(filled, n + 1)
                for t in range(2):
                    dst = vpad[u][:, t, :].rearrange("p (c w) -> p c w", c=4).rearrange(
                        "p c (j s) -> p c j s", j=4)[:, :, :, 0:HD]
                    ins = dve.tensor_copy(dst, ring[:, slot, t * P:(t + 1) * P].rearrange("p (c j s) -> p c j s", c=4, j=4))
                ins.then_inc(ring_dve, 1)

            def row_max(u, i, n, slot):
                dve.wait_ge(filled, n + 1)
                at = i // 8 * HEADS + i % 8 * 2
                dve.tensor_reduce(mrow[u][:, at:at + 2], ring[:, slot, :].rearrange("p (h k) -> p h k", h=2),
                                  AX.X, ALU.max).then_inc(ring_dve, 1)

            def store_maxima(u, n, slot):
                dve.wait_ge(filled, n + 1)
                chain.link(dve.tensor_scalar(mt[u][0:HEADS, :], ring[0:HEADS, slot, 0:SEQ], -1.0, None, ALU.mult))
                dve.scalar_tensor_tensor(out=mt[u][32:32 + HEADS, :], in0=ring[0:HEADS, slot, 0:SEQ], scalar=-1.0,
                                         in1=mt[u][0:HEADS, :], op0=ALU.mult, op1=ALU.subtract).then_inc(ring_dve, 1)

            def normalise(u, b):
                dve.wait_ge(values_summed, 4 * (l * 8 + b + 1))
                chain.link(dve.reciprocal(rsum[:, :], g.sm[:, 0:SEQ]))
                dve.tensor_tensor(on[u][:, :], g.ov[:, 0:SEQ], rsum[:, :], ALU.mult).then_inc(sums_read, 1)
                dve.wait_ge(sums_read, l * 8 + b + 1)
                dve.tensor_scalar(on[u][:, :], on[u][:, :], g.vec(f"bv{l}" if l in (1, 3) else "zero"), None,
                                  ALU.add).then_inc(out_ready, 1)

            def residual(b, n, slot):
                dve.wait_ge(filled, n + 1)
                dve.tensor_scalar(upd[:, :], ring[:, slot, 0:SEQ], g.gates[:, l:l + 1], g.gbo[:, l:l + 1],
                                  ALU.mult, ALU.add).then_inc(ring_dve, 1)
                dve.wait_ge(ring_dve, n + 1)
                xs = g.x[:, cols(b, SEQ)]
                chain.link(dve.tensor_tensor(xs, xs, upd[:, :], ALU.add))

            def body(b, u, more, stage):
                n = item(b, 0)
                chain.start(l * 24 + 1 + b * 3)
                if more:
                    values(1 - u, n, u % 2)
                    for i in range(16):
                        row_max(1 - u, i, n + 1 + i, (u + 1 + i) % 2)
                    store_maxima(1 - u, n + 17, (u + 17) % 2)
                    queries(qm, 1 - u, b + 1, queries_f)
                normalise(u, b)
                residual(b, n + (18 if more else 0), (u + (18 if more else 0)) % 2)
                if stage:
                    queries(qmr, u, b + 2, queries_r)
                chain.ends(3 if more else 2)

            for u in range(2):
                dve.memset(vpad[u][:, :, :], 0.0)
                ins = dve.memset(mt[u][:, :], 0.0)
            ins.then_inc(vpad_zeroed, 1)
            dve.wait_ge(vpad_zeroed, l + 1)
            chain.start(l * 24)
            queries(qmr, 0, 0, queries_r)
            values(0, l * layer_items, 0)
            for i in range(16):
                row_max(0, i, l * layer_items + 1 + i, (1 + i) % 2)
            store_maxima(0, l * layer_items + 17, 1)
            queries(qm, 0, 0, queries_f)
            queries(qmr, 1, 1, queries_r)
            chain.ends(1)
            with dve.Fori(0, 3) as k:
                body(k * 2, 0, True, True)
                body(k * 2 + 1, 1, True, True)
            body(6, 0, True, False)
            body(7, 1, False, False)


def released(seq, k, who):
    return sum(who in s for s in seq[:k + 1])


QKV_ITEMS = (["AD"] * 4 + ["A"] * 2) * 2
ROW_GROUPS = [(0, h, 4) for h in range(0, HEADS, 4)] + [(1, h, min(3, HEADS - h)) for h in range(0, HEADS, 3)]
TURN_ITEMS = ["AD"] * 8
ROWS_ITEMS = ["D"] * (len(ROW_GROUPS) + 1)
END_ITEMS = ["D"] * 5
BODY = TURN_ITEMS + ROWS_ITEMS + QKV_ITEMS + END_ITEMS
LAST = TURN_ITEMS + ROWS_ITEMS + END_ITEMS
PER_STEP = {"F": len(BODY), "A": released(BODY, len(BODY), "A"), "D": released(BODY, len(BODY), "D")}
AHEAD = {"F": len(QKV_ITEMS), "A": released(QKV_ITEMS, 99, "A"), "D": released(QKV_ITEMS, 99, "D")}


def local_attention(g, d, t):
    nc = g.nc
    filled, ring_act, ring_dve = g.sem("l_ring_filled"), g.sem("l_ring_read_act"), g.sem("l_ring_read_dve")
    w_loaded, wf_loaded, tables = g.sem("l_weights_loaded"), g.sem("l_ffn_weights_loaded"), g.sem("l_tables_ready")
    shifted, sq_reduced = g.sem("l_shifted"), g.sem("l_squares_reduced")
    ab_summed, n2_ready, guess, rn_ready = g.sem("l_ab_summed"), g.sem("l_n2_ready"), g.sem("l_rnorm_guess"), g.sem("l_rnorm_ready")
    qk_normed = g.sem("l_qk_normed")
    scores_ready, probs_ready = g.sem("l_scores_ready"), g.sem("l_probs_ready")
    values_summed, values_out = g.sem("l_values_summed"), g.sem("l_values_out")
    parts_ready, own, aown = g.sem("l_sum_parts_ready"), g.sem("l_dve_own"), g.sem("l_act_own")
    ring = g.ring

    def pos(b, k):
        return (d * NB + b) * PER_STEP["F"] + AHEAD["F"] + k

    def count(who, seq, b, k):
        return (d * NB + b) * PER_STEP[who] + AHEAD[who] + released(seq, k, who)

    with nc.Block() as block:
        @block.sync
        def _(sp):
            sp.dma_start(t.qkscale[:, :, :], g.a["qkscale"][bass.ds(d, 1), :].rearrange("o (r k) -> o r k", r=4)
                         .broadcast_to([P, 4, LHD])).then_inc(w_loaded, 16)
            sp.dma_start(t.wa[:, :], g.a["wa"][:, cols(d, D_W1)]).then_inc(w_loaded, 16)
            sp.dma_start(t.wf[:, :], g.a["wf"][:, cols(d, D_ALL - D_W1)]).then_inc(wf_loaded, 16)

        @block.tensor
        def _(pe):
            def claim(seq, b, k):
                pe.wait_ge(ring_act, count("A", seq, b, k - 2))
                pe.wait_ge(ring_dve, count("D", seq, b, k - 2))

            def project(i, slot):
                tile, j = divmod(i, 6)
                pe.matmul(ring[:, slot, :], t.xs[:, tile * P:(tile + 1) * P], t.wa[:, j * C:(j + 1) * C],
                          start=True, stop=True).then_inc(filled, 1)

            def turn(p, slot):
                for cc in range(2):
                    for tile in range(2):
                        mm = pe.transpose(ring[:, slot, cc * SEQ + tile * P:cc * SEQ + (tile + 1) * P],
                                          t.qk[:, tile, (2 * p + cc) * P:(2 * p + cc + 1) * P], g.f("ident"))
                mm.then_inc(filled, 1)

            def rows(group, slot):
                tile, h0, n = group
                width, k0 = (P, 0) if tile == 0 else (KSPAN, P - WIN)
                for x in range(n):
                    c, hh = divmod(h0 + x, 2)
                    out = ring[:, slot, x * width:(x + 1) * width]
                    pe.matmul(out, t.qzr[:, c, hh, tile * P:(tile + 1) * P], t.ktr[:, c, k0:k0 + width],
                              start=True, stop=False)
                    mm = pe.matmul(out, g.b("ident"), g.b(f"band{tile}", width), start=False, stop=True)
                mm.then_inc(filled, 1)

            def turn_maxima(slot):
                for tile in range(2):
                    mm = pe.transpose(ring[0:HEADS, slot, tile * P:(tile + 1) * P],
                                      t.mrow[:, tile * HEADS:(tile + 1) * HEADS], g.f("ident"))
                mm.then_inc(filled, 1)

            def scores(b, quad):
                for h in range(4 * quad, 4 * quad + 4):
                    c, hh = divmod(h, 2)
                    if quad:
                        pe.wait_ge(probs_ready, 8 * (d * NB + b) + (h - 4) // 2 + 1)
                    for kt, q0, q1, at in ((0, 0, KSPAN, 0), (1, P, SEQ, KSPAN)):
                        out = g.st[:, h % 4, at:at + q1 - q0]
                        pe.matmul(out, t.kt[:, c, kt * P:(kt + 1) * P], t.qz[:, c, hh, q0:q1], start=True, stop=False)
                        pe.matmul(out, g.b("ident"), g.b("bandT", q1 - q0), start=False, stop=False)
                        mm = pe.matmul(out, g.cb[:, B_AT["sel"] + h * P:B_AT["sel"] + (h + 1) * P], t.mt[:, q0:q1],
                                       start=False, stop=True)
                    if h % 2:
                        mm.then_inc(scores_ready, 1)

            def sum_values(b, u, quad):
                pe.wait_ge(probs_ready, 8 * (d * NB + b) + 2 * quad + 2)
                if quad:
                    pe.wait_ge(values_out, 4 * (d * NB + b) + quad)
                for kt, q0, q1, at in ((0, 0, KSPAN, 0), (1, P, SEQ, KSPAN)):
                    for x in range(4):
                        h = 4 * quad + x
                        c, hh = divmod(h, 2)
                        pe.matmul(g.ov[hh * LHD:(hh + 1) * LHD, c % 2 * SEQ + q0:c % 2 * SEQ + q1],
                                  t.v[u][:, kt, h * LHD:(h + 1) * LHD], t.pt[:, quad % 2 * 4 + x, at:at + q1 - q0],
                                  start=kt == 0 and x < 2, stop=kt == 1, skip_group_check=True)
                for kt, q0, q1, at in ((0, 0, KSPAN, 0), (1, P, SEQ, KSPAN)):
                    for x in range(4):
                        mm = pe.matmul(g.sm[32 * x:32 * x + 32, q0:q1],
                                       g.cf[:, F_AT["sumsel"] + 32 * quad:F_AT["sumsel"] + 32 * quad + 32],
                                       t.pt[:, quad % 2 * 4 + x, at:at + q1 - q0],
                                       start=kt == 0 and quad == 0, stop=kt == 1 and quad == 3, skip_group_check=True)
                mm.then_inc(values_summed, 1)

            def body(b, u, more):
                seq = BODY if more else LAST
                pe.wait_ge(qk_normed, 8 * (d * NB + b + 1))
                pe.wait_ge(ring_act, count("A", seq, b, -1))
                pe.wait_ge(ring_dve, count("D", seq, b, -1))
                k = 0
                for p in range(8):
                    if p >= 2:
                        claim(seq, b, k)
                    turn(p, k % 2)
                    k += 1
                pe.wait_ge(ring_dve, count("D", seq, b, 7))
                for group in ROW_GROUPS:
                    claim(seq, b, k)
                    rows(group, k % 2)
                    k += 1
                pe.wait_ge(ring_dve, count("D", seq, b, k - 1))
                turn_maxima(k % 2)
                k += 1
                pe.wait_ge(ring_dve, count("D", seq, b, k - 1))
                pe.wait_ge(ring_act, count("A", seq, b, 7))
                for quad in range(4):
                    scores(b, quad)
                    if more:
                        if quad == 0:
                            pe.wait_ge(shifted, d * NB + b + 2)
                        for i in range(3 * quad, 3 * quad + 3):
                            claim(seq, b, k)
                            project(i, k % 2)
                            k += 1
                    if quad:
                        sum_values(b, u, quad - 1)
                sum_values(b, u, 3)
                pe.wait_ge(parts_ready, d * NB + b + 1)
                for p in range(4):
                    claim(seq, b, k)
                    for cc in range(2):
                        for part in range(3):
                            c = 2 * p + cc
                            mm = pe.matmul(ring[:, k % 2, cc * SEQ:(cc + 1) * SEQ],
                                           g.cb[:, B_AT["selr"] + c * P:B_AT["selr"] + (c + 1) * P],
                                           t.rpart[:, part, :], start=part == 0, stop=part == 2)
                    mm.then_inc(filled, 1)
                    k += 1
                claim(seq, b, k)
                pe.wait_ge(ring_dve, count("D", seq, b, k - 1))
                for c in range(8):
                    mm = pe.matmul(ring[:, k % 2, 0:SEQ], t.wa[:, D_WO + c * P:D_WO + (c + 1) * P], t.o[:, c, :],
                                   start=c == 0, stop=c == 7)
                mm.then_inc(filled, 1)
                k += 1
                assert k == len(seq)

            pe.wait_ge(w_loaded, d * 32 + 32)
            pe.wait_ge(shifted, d * NB + 1)
            for i in range(12):
                if i >= 2:
                    pe.wait_ge(ring_act, d * NB * PER_STEP["A"] + released(QKV_ITEMS, i - 2, "A"))
                    pe.wait_ge(ring_dve, d * NB * PER_STEP["D"] + released(QKV_ITEMS, i - 2, "D"))
                project(i, i % 2)
            with pe.Fori(0, 3) as kk:
                body(kk * 2, 0, True)
                body(kk * 2 + 1, 1, True)
            body(6, 0, True)
            body(7, 1, False)

        @block.scalar
        def _(act):
            chain = Chain(act, aown)

            def qkv_item(s, u, i, slot, n, chain_off):
                tile, j = divmod(i, 6)
                act.wait_ge(filled, n + 1)
                if j < 4:
                    e = 4 * tile + j
                    if e >= 2:
                        act.wait_ge(sq_reduced, 8 * s + e - 1)
                    act.activation(t.sq[:, e % 2, :], ring[:, slot, :], ACT.Square).then_inc(ring_act, 1)
                else:
                    act.activation(t.v[u][:, tile, (j - 4) * C:(j - 3) * C], ring[:, slot, :], ACT.Copy).then_inc(ring_act, 1)
                if j == 5:
                    act.wait_ge(n2_ready, 2 * s + tile + 1)
                    chain.link(act.activation(t.lnv[:, tile, :], t.n2[:, tile, :], ACT.Ln, scale=2.0 ** 20))
                    act.activation(t.rn[:, tile, :], t.lnv[:, tile, :], ACT.Exp, scale=-0.5,
                                   bias=g.f("lnoff", 1)).then_inc(guess, 1)

            def turned(p, slot, n):
                act.wait_ge(filled, n + 1)
                bank = ring[:, slot, :].rearrange("p (c s) -> p c s", c=2)
                if p < 4:
                    act.activation(t.qz[0:LHD, 2 * p:2 * p + 2, 0, :], bank[0:LHD], ACT.Copy)
                    act.activation(t.qz[LHD:P, 2 * p:2 * p + 2, 1, :], bank[LHD:P], ACT.Copy).then_inc(ring_act, 1)
                else:
                    act.activation(t.kt[:, 2 * (p - 4):2 * (p - 4) + 2, :], bank, ACT.Copy).then_inc(ring_act, 1)

            def probabilities(b, quad):
                for pair in range(2 * quad, 2 * quad + 2):
                    act.wait_ge(scores_ready, 8 * (d * NB + b) + pair + 1)
                    if quad >= 2 and pair % 2 == 0:
                        act.wait_ge(values_summed, 4 * (d * NB + b) + quad - 1)
                    act.activation(t.pt[:, pair % 4 * 2:pair % 4 * 2 + 2, :],
                                   g.st[:, pair % 2 * 2:pair % 2 * 2 + 2, 0:PACK], ACT.Exp).then_inc(probs_ready, 1)

            def values_to_sbuf(b, quad):
                act.wait_ge(values_summed, 4 * (d * NB + b) + quad + 1)
                act.activation(t.o[:, 2 * quad:2 * quad + 2, :].rearrange("p c s -> p (c s)"), g.ov[:, :],
                               ACT.Copy).then_inc(values_out, 1)

            def body(b, u, more):
                chain.start((d * NB + b) * 2 + 2)
                for p in range(8):
                    turned(p, p % 2, pos(b, p))
                k = 8 + len(ROWS_ITEMS)
                for quad in range(4):
                    probabilities(b, quad)
                    if more:
                        for i in range(3 * quad, 3 * quad + 3):
                            qkv_item(d * NB + b + 1, 1 - u, i, k % 2, pos(b, k), None)
                            k += 1
                    if quad:
                        values_to_sbuf(b, quad - 1)
                values_to_sbuf(b, 3)
                if more:
                    chain.ends(2)

            chain.start(d * NB * 2)
            for i in range(12):
                qkv_item(d * NB, 0, i, i % 2, d * NB * PER_STEP["F"] + i, None)
            with act.Fori(0, 3) as kk:
                body(kk * 2, 0, True)
                body(kk * 2 + 1, 1, True)
            body(6, 0, True)
            body(7, 1, False)

        @block.gpsimd
        def _(pool):
            pool.wait_ge(w_loaded, d * 32 + 32)
            for i, name in enumerate(("lqcos", "lqsin", "lkcos", "lksin")):
                pool.tensor_tensor(t.tab[:, i, :, :], g.f(name, 2 * LHD).rearrange("p (t k) -> p t k", t=2),
                                   t.qkscale[:, i, :].unsqueeze(1).broadcast_to([P, 2, LHD]), ALU.mult).then_inc(tables, 1)

            def rotate(s, i, cd):
                tile, j = divmod(i, 6)
                if j < 4:
                    e = 4 * tile + j
                    pool.wait_ge(ring_dve, cd)
                    pool.tensor_tensor(t.qk[:, tile, j * C:(j + 1) * C], t.ta[:, e % 2, :], t.tb[:, e % 2, :],
                                       ALU.add).then_inc(ab_summed, 1)

            def normalise(s, tile):
                pool.wait_ge(rn_ready, 2 * s + tile + 1)
                for j in range(4):
                    pool.wait_ge(ab_summed, 8 * s + 4 * tile + j + 1)
                    part = t.qk[:, tile, j * C:(j + 1) * C].rearrange("p (h k) -> p h k", k=LHD)
                    pool.tensor_tensor(part, part, t.rn[:, tile, 8 * j:8 * j + 8].unsqueeze(2).broadcast_to([P, 8, LHD]),
                                       ALU.mult).then_inc(qk_normed, 1)

            def batch(s, at):
                for i in range(12):
                    if i == 11:
                        normalise(s, 0)
                    rotate(s, i, at(i))
                normalise(s, 1)

            def body(b):
                k0 = 8 + len(ROWS_ITEMS)
                pool.wait_ge(filled, pos(b, 8))
                batch(d * NB + b + 1, lambda i: count("D", BODY, b, k0 + i))

            batch(d * NB, lambda i: d * NB * PER_STEP["D"] + released(QKV_ITEMS, i, "D"))
            with pool.Fori(0, 7) as b:
                body(b)
            pool.wait_ge(wf_loaded, d * 16 + 16)

        @block.vector
        def _(dve):
            chain = Chain(dve, own)

            def shift(b):
                dve.tensor_copy(t.xs[0:64, :], g.y[0:64, cols(b, SEQ)])
                dve.tensor_copy(t.xs[64:P, 1:SEQ], g.y[64:P, bass.ds(b * SEQ, SEQ - 1)]).then_inc(shifted, 1)

            def qkv_item(s, i, slot, n, ca):
                tile, j = divmod(i, 6)
                if j < 4:
                    e = 4 * tile + j
                    dve.wait_ge(ring_act, ca)
                    if e >= 2:
                        dve.wait_ge(ab_summed, 8 * s + e - 1)
                    bank = ring[:, slot, :].rearrange("p (h k) -> p h k", k=LHD)
                    ta = t.ta[:, e % 2, :].rearrange("p (h k) -> p h k", k=LHD)
                    tb = t.tb[:, e % 2, :].rearrange("p (h k) -> p h k", k=LHD)
                    q = j // 2 * 2

                    def table(i, lo, hi):
                        return t.tab[:, q + i, tile, lo:hi].unsqueeze(1).broadcast_to([P, 8, hi - lo])

                    half = LHD // 2
                    dve.tensor_tensor(ta, bank, table(0, 0, LHD), ALU.mult)
                    dve.tensor_tensor(tb[:, :, 0:half], bank[:, :, half:LHD], table(1, 0, half), ALU.mult)
                    dve.tensor_tensor(tb[:, :, half:LHD], bank[:, :, 0:half], table(1, half, LHD), ALU.mult).then_inc(ring_dve, 1)
                    dve.tensor_reduce(t.n2[:, tile, 8 * j:8 * j + 8],
                                      t.sq[:, e % 2, :].rearrange("p (h k) -> p h k", k=LHD),
                                      AX.X, ALU.add).then_inc(sq_reduced, 1)
                    if j == 3:
                        dve.wait_ge(sq_reduced, 8 * s + e + 1)
                        dve.tensor_scalar(t.n2[:, tile, :], t.n2[:, tile, :], 1e-24, None, ALU.max).then_inc(n2_ready, 1)
                if i == 7:
                    refine(s, 0)

            def refine(s, tile):
                dve.wait_ge(guess, 2 * s + tile + 1)
                r, n2, w = t.rn[:, tile, :], t.n2[:, tile, :], t.nw[:, tile, :]
                chain.link(dve.tensor_tensor(w, r, r, ALU.mult))
                chain.link(dve.tensor_tensor(w, w, n2, ALU.mult))
                chain.link(dve.tensor_scalar(w, w, -0.5, 1.5, ALU.mult, ALU.add))
                dve.tensor_tensor(r, r, w, ALU.mult).then_inc(rn_ready, 1)

            def turned(p, slot, ca):
                dve.wait_ge(ring_act, ca)
                bank = ring[:, slot, :].rearrange("p (c s) -> p c s", c=2)
                if p < 4:
                    dve.tensor_copy(t.qzr[0:LHD, 2 * p:2 * p + 2, 0, :], bank[0:LHD])
                    dve.tensor_copy(t.qzr[LHD:P, 2 * p:2 * p + 2, 1, :], bank[LHD:P]).then_inc(ring_dve, 1)
                else:
                    dve.tensor_copy(t.ktr[:, 2 * (p - 4):2 * (p - 4) + 2, :], bank).then_inc(ring_dve, 1)

            def row_max(group, slot, n):
                tile, h0, m = group
                width = P if tile == 0 else KSPAN
                dve.wait_ge(filled, n + 1)
                dve.tensor_reduce(t.mrow[:, tile * HEADS + h0:tile * HEADS + h0 + m],
                                  ring[:, slot, 0:m * width].rearrange("p (h k) -> p h k", h=m),
                                  AX.X, ALU.max).then_inc(ring_dve, 1)

            def store_maxima(slot, n):
                dve.wait_ge(filled, n + 1)
                chain.link(dve.tensor_scalar(t.mt[0:HEADS, :], ring[0:HEADS, slot, 0:SEQ], -1.0, None, ALU.mult))
                dve.scalar_tensor_tensor(out=t.mt[32:32 + HEADS, :], in0=ring[0:HEADS, slot, 0:SEQ], scalar=-1.0,
                                         in1=t.mt[0:HEADS, :], op0=ALU.mult, op1=ALU.subtract).then_inc(ring_dve, 1)

            def sums(b):
                dve.wait_ge(values_summed, 4 * (d * NB + b + 1))
                r, p0, p1, p2 = t.rsum[:, :], t.rpart[:, 0, :], t.rpart[:, 1, :], t.rpart[:, 2, :]
                chain.link(dve.reciprocal(r, g.sm[:, 0:SEQ]))
                chain.link(dve.tensor_copy(p0, r))
                chain.link(dve.tensor_tensor(r, r, p0, ALU.subtract))
                chain.link(dve.tensor_copy(p1, r))
                dve.tensor_tensor(p2, r, p1, ALU.subtract).then_inc(parts_ready, 1)

            def normalise(b, p, slot, n):
                dve.wait_ge(filled, n + 1)
                dve.wait_ge(values_out, 4 * (d * NB + b) + p + 1)
                o = t.o[:, 2 * p:2 * p + 2, :].rearrange("p c s -> p (c s)")
                dve.tensor_tensor(o, o, ring[:, slot, :], ALU.mult).then_inc(ring_dve, 1)

            def body(b, u, more):
                seq = BODY if more else LAST
                chain.start((d * NB + b) * 11 + 6)
                k = 0
                for p in range(8):
                    turned(p, k % 2, count("A", seq, b, k))
                    k += 1
                for group in ROW_GROUPS:
                    row_max(group, k % 2, pos(b, k))
                    k += 1
                store_maxima(k % 2, pos(b, k))
                k += 1
                if more:
                    shift(b + 1)
                    for i in range(12):
                        qkv_item(d * NB + b + 1, i, k % 2, pos(b, k), count("A", seq, b, k))
                        k += 1
                    refine(d * NB + b + 1, 1)
                sums(b)
                for p in range(4):
                    normalise(b, p, k % 2, pos(b, k))
                    k += 1
                dve.wait_ge(filled, pos(b, k) + 1)
                ys = g.y[:, cols(b, SEQ)]
                dve.tensor_tensor(ys, ys, ring[:, k % 2, 0:SEQ], ALU.add).then_inc(ring_dve, 1)
                chain.ends(11 if more else 5)

            shift(0)
            dve.wait_ge(tables, d * 4 + 4)
            chain.start(d * NB * 11)
            for i in range(12):
                qkv_item(d * NB, i, i % 2, d * NB * PER_STEP["F"] + i,
                         d * NB * PER_STEP["A"] + released(QKV_ITEMS, i, "A"))
            refine(d * NB, 1)
            chain.ends(6)
            with dve.Fori(0, 3) as kk:
                body(kk * 2, 0, True)
                body(kk * 2 + 1, 1, True)
            body(6, 0, True)
            body(7, 1, False)


def local_ffn(g, d, t):
    nc = g.nc
    shifted, centered, squared, variance, rstd, normed = (
        g.sem("f_" + n) for n in ("shifted", "centered", "squared", "variance", "rstd", "normed"))
    pair_filled, gelu_done, gated, sum_filled, updated = (
        g.sem("f_" + n) for n in ("pair_filled", "gelu_done", "gated", "sum_filled", "updated"))
    vec = D_VEC - D_W1
    gain, bias, b2 = (t.wf[:, vec + i:vec + i + 1] for i in (0, 1, 2 + 2 * FFC))
    with nc.Block() as block:
        @block.tensor
        def _(pe):
            with pe.Fori(0, 2) as k:
                for u in range(2):
                    pe.wait_ge(shifted, d * 4 + k * 2 + u + 1)
                    pe.matmul(g.st[:, u, :], g.f("center"), t.fs[:, u, :], start=True, stop=True).then_inc(centered, 1)
                for u in range(2):
                    pe.wait_ge(squared, d * 4 + k * 2 + u + 1)
                    pe.matmul(g.st[:, 2 + u, :], g.f("mean"), t.fsq[:, u, :], start=True, stop=True).then_inc(variance, 1)
                pe.wait_ge(normed, 2 * (d * 4 + k * 2) + 4)

            def pair(c, i):
                if i >= 2:
                    pe.wait_ge(gated, 3 * (d * 4 + c) + i - 1)
                for x in range(2):
                    mm = pe.matmul(g.st[:, 2 * (i % 2) + x, :], t.wf[:, (x * FFC + i) * P:(x * FFC + i + 1) * P],
                                   t.xn[:, cols(c)], start=True, stop=True)
                mm.then_inc(pair_filled, 1)

            def down(c, i):
                pe.wait_ge(gated, 3 * (d * 4 + c) + i + 1)
                w2 = D_W2 - D_W1 + i * P
                mm = pe.matmul(g.ov[:, :], t.wf[:, w2:w2 + P], t.h[:, i, :], start=i == 0, stop=i == FFC - 1)
                if i == FFC - 1:
                    mm.then_inc(sum_filled, 1)

            with pe.Fori(0, 4) as c:
                pair(c, 0)
                pair(c, 1)
                down(c, 0)
                pair(c, 2)
                down(c, 1)
                down(c, 2)
                pe.wait_ge(updated, d * 4 + c + 1)

        @block.scalar
        def _(act):
            with act.Fori(0, 2) as k:
                for u in range(2):
                    act.wait_ge(centered, d * 4 + k * 2 + u + 1)
                    act.activation(t.fsq[:, u, :], g.st[:, u, :], ACT.Square).then_inc(squared, 1)
                for u in range(2):
                    act.wait_ge(variance, d * 4 + k * 2 + u + 1)
                    act.activation(t.frs[:, u, :], g.st[:, 2 + u, :], ACT.Ln, bias=g.f("eps5", 1)).then_inc(rstd, 1)
                    act.wait_ge(rstd, 2 * (d * 4 + k * 2 + u) + 1)
                    act.activation(t.frs[:, u, :], t.frs[:, u, :], ACT.Exp, scale=-0.5).then_inc(rstd, 1)
            with act.Fori(0, 4) as c:
                for i in range(FFC):
                    act.wait_ge(pair_filled, 3 * (d * 4 + c) + i + 1)
                    act.activation(t.gl[:, i % 2, :], g.st[:, 2 * (i % 2) + 1, :], ACT.Gelu,
                                   bias=t.wf[:, vec + 2 + FFC + i:vec + 3 + FFC + i]).then_inc(gelu_done, 1)

        @block.vector
        def _(dve):
            with dve.Fori(0, 2) as k:
                for u in range(2):
                    c = k * 2 + u
                    src = g.y[:, cols(c)].rearrange("p (b s) -> p b s", b=2)
                    dst = t.fs[:, u, :].rearrange("p (b s) -> p b s", b=2)
                    dve.memset(dst[64:P, :, 0:1], 0.0)
                    dve.tensor_copy(dst[0:64], src[0:64])
                    dve.tensor_copy(dst[64:P, :, 1:SEQ], src[64:P, :, 0:SEQ - 1]).then_inc(shifted, 1)
                for u in range(2):
                    c = k * 2 + u
                    dve.wait_ge(rstd, 2 * (d * 4 + c) + 2)
                    dve.tensor_tensor(t.xn[:, cols(c)], g.st[:, u, :], t.frs[:, u, :], ALU.mult).then_inc(normed, 1)
                    dve.wait_ge(normed, 2 * (d * 4 + c) + 1)
                    dve.tensor_scalar(t.xn[:, cols(c)], t.xn[:, cols(c)], gain, bias, ALU.mult, ALU.add).then_inc(normed, 1)
            with dve.Fori(0, 4) as c:
                for i in range(FFC):
                    dve.wait_ge(gelu_done, 3 * (d * 4 + c) + i + 1)
                    dve.scalar_tensor_tensor(out=t.h[:, i, :], in0=g.st[:, 2 * (i % 2), :],
                                             scalar=t.wf[:, vec + 2 + i:vec + 3 + i], in1=t.gl[:, i % 2, :],
                                             op0=ALU.add, op1=ALU.mult).then_inc(gated, 1)
                dve.wait_ge(sum_filled, d * 4 + c + 1)
                ys = g.y[:, cols(c)]
                dve.scalar_tensor_tensor(out=ys, in0=g.ov[:, :], scalar=b2, in1=ys,
                                         op0=ALU.add, op1=ALU.add).then_inc(updated, 1)


class LocalMemory:

    def __init__(self, tmp):
        self.qkscale = tmp("l_qkscale", [P, 4, LHD], F32)
        self.tab = tmp("l_tab", [P, 4, 2, LHD], F32)
        self.wa = tmp("l_wa", [P, D_W1], F32)
        self.wf = tmp("l_wf", [P, D_ALL - D_W1], F32)
        self.xs = tmp("l_xs", [P, SEQ], F32)
        self.sq = tmp("l_sq", [P, 2, C], F32)
        self.ta = tmp("l_ta", [P, 2, C], F32)
        self.tb = tmp("l_tb", [P, 2, C], F32)
        self.n2 = tmp("l_n2", [P, 2, 2 * HEADS], F32)
        self.lnv = tmp("l_lnv", [P, 2, 2 * HEADS], F32)
        self.rn = tmp("l_rn", [P, 2, 2 * HEADS], F32)
        self.nw = tmp("l_nw", [P, 2, 2 * HEADS], F32)
        self.qk = tmp("l_qk", [P, 2, 2 * INNER], F32)
        self.qz = tmp("l_qz", [P, 8, 2, SEQ], F32)
        self.qzr = tmp("l_qzr", [P, 8, 2, SEQ], F32R)
        self.kt = tmp("l_kt", [P, 8, SEQ], F32)
        self.ktr = tmp("l_ktr", [P, 8, SEQ], F32R)
        self.v = [tmp(f"l_v{u}", [P, 2, INNER], F32) for u in range(2)]
        self.mrow = tmp("l_mrow", [P, 2 * HEADS], F32)
        self.mt = tmp("l_mt", [P, SEQ], BF16)
        self.pt = tmp("l_pt", [P, 8, PACK], F32)
        self.rsum = tmp("l_rsum", [P, SEQ], F32)
        self.rpart = tmp("l_rpart", [P, 3, SEQ], BF16)
        self.o = tmp("l_o", [P, 8, SEQ], F32)


class FfnMemory:

    def __init__(self, t):
        self.wf = t.wf
        big = t.qk[:, :, :].rearrange("p a b -> p (a b)")
        self.xn = big[:, 0:TOK]
        at = TOK
        self.fs = t.tb[:, :, :]
        self.fsq = big[:, at:at + 2 * C].rearrange("p (u s) -> p u s", u=2)
        self.frs = big[:, at + 2 * C:at + 4 * C].rearrange("p (u s) -> p u s", u=2)
        self.gl = t.ta[:, :, :]
        self.h = t.o[:, :, :].rearrange("p c s -> p (c s)")[:, 0:FFC * C].rearrange("p (i s) -> p i s", i=FFC)


def local_transformer(g, tmp):
    nc = g.nc
    t = LocalMemory(tmp)
    zeroed = g.sem("l_zeroed")
    with nc.Block() as block:
        @block.vector
        def _(dve):
            dve.memset(t.qz[:, :, :, :], 0.0)
            dve.memset(t.xs[:, :], 0.0)
            dve.memset(t.mt[:, :], 0.0).then_inc(zeroed, 1)
            dve.wait_ge(zeroed, 1)
            dve.tensor_copy(t.qzr[:, :, :, :], t.qz[:, :, :, :]).then_inc(zeroed, 1)
            dve.wait_ge(zeroed, 2)
    with nc.Fori(0, DEPTH) as d:
        local_attention(g, d, t)
        local_ffn(g, d, FfnMemory(t))


def add_gated(g):
    with g.nc.Block() as block:
        @block.vector
        def _(dve):
            dve.scalar_tensor_tensor(out=g.x[:, :], in0=g.y[:, :], scalar=g.gates[:, 4:5], in1=g.x[:, :],
                                     op0=ALU.mult, op1=ALU.add)


def gate_scores(g, pooled, weights, bias, prod, out, sem, seen):
    nc = g.nc
    with nc.Block() as block:
        @block.vector
        def _(dve):
            shape = [P, NB, EXPERTS]
            dve.tensor_tensor(prod[:, :, :], pooled.unsqueeze(2).broadcast_to(shape),
                              weights.unsqueeze(1).broadcast_to(shape), ALU.mult).then_inc(sem, 1)
            dve.wait_ge(sem, seen + 2)
            dve.tensor_tensor(out[:, :, :], g.ov[:, 0:NB * EXPERTS].rearrange("p (b e) -> p b e", b=NB),
                              bias.unsqueeze(1).broadcast_to(shape), ALU.add)

        @block.tensor
        def _(pe):
            pe.wait_ge(sem, seen + 1)
            pe.matmul(g.ov[:, 0:NB * EXPERTS], g.f("ones"), prod[:, :, :].rearrange("p b e -> p (b e)"),
                      start=True, stop=True).then_inc(sem, 1)


def moe_ffn(g, tmp):
    nc = g.nc
    prod, sc = tmp("m_prod", [P, NB, EXPERTS], F32), tmp("m_scores", [P, NB, EXPERTS], F32)
    above, tied = (tmp(n, [P, NB, EXPERTS, EXPERTS], F32) for n in ("m_above", "m_tied"))
    gate, gb = tmp("m_gate", [P, NB, EXPERTS], F32), tmp("m_gate_bias", [P, NB], F32)
    h, tmp_out = tmp("m_hidden", [P, 4, C], F32), tmp("m_out", [P, C], F32)
    first_tokens = g.y[:, :].rearrange("p (b s) -> p b s", b=NB)[:, :, 0]
    gate_scores(g, first_tokens, g.vec("r1_0", EXPERTS), g.rbias[:, 0:EXPERTS], prod, sc, g.sem("gate_steps"), 0)
    own = g.sem("m_own")
    hidden_filled, gelu_done, gated = g.sem("m_hidden_filled"), g.sem("m_gelu_done"), g.sem("m_gated")
    out_filled, updated = g.sem("m_out_filled"), g.sem("m_updated")
    wide = [P, NB, EXPERTS, EXPERTS]
    with nc.Block() as block:
        @block.vector
        def _(dve):
            chain = Chain(dve, own)
            mine = sc[:, :, :].unsqueeze(3).broadcast_to(wide)
            others = sc[:, :, :].unsqueeze(2).broadcast_to(wide)
            flat = [P, NB, EXPERTS * EXPERTS]
            dve.tensor_tensor(above[:, :, :, :], others, mine, ALU.is_gt)
            chain.link(dve.tensor_tensor(tied[:, :, :, :], others, mine, ALU.is_equal))
            tf, af = (x[:, :, :, :].rearrange("p b e j -> p b (e j)") for x in (tied, above))
            chain.link(dve.tensor_tensor(tf, tf, g.f("earlier", EXPERTS * EXPERTS).unsqueeze(1).broadcast_to(flat), ALU.mult))
            chain.link(dve.tensor_tensor(af, af, tf, ALU.add))
            chain.link(dve.tensor_reduce(gate[:, :, :], above[:, :, :, :], AX.X, ALU.add))
            chain.link(dve.tensor_scalar(gate[:, :, :], gate[:, :, :], 2.0, 0.5, ALU.is_lt, ALU.mult))
            chain.link(dve.tensor_tensor(prod[:, :, :], gate[:, :, :],
                                         g.vec("mb2_0", EXPERTS).unsqueeze(1).broadcast_to([P, NB, EXPERTS]), ALU.mult))
            dve.tensor_reduce(gb[:, :], prod[:, :, :], AX.X, ALU.add)
    with nc.Block() as block:
        @block.tensor
        def _(pe):
            def down(c, e):
                pe.wait_ge(gated, EXPERTS * c + e + 1)
                mm = pe.matmul(g.ov[:, :], g.wm(f"m2_{e}"), h[:, e % 4, :], start=e == 0, stop=e == EXPERTS - 1)
                if e == EXPERTS - 1:
                    mm.then_inc(out_filled, 1)

            with pe.Fori(0, 4) as c:
                for e in range(EXPERTS):
                    if e >= 4:
                        pe.wait_ge(gelu_done, EXPERTS * c + e - 3)
                    pe.matmul(g.st[:, e % 4, :], g.wm(f"m1_{e}"), g.y[:, cols(c)], start=True, stop=True)\
                        .then_inc(hidden_filled, 1)
                    if e >= 2:
                        down(c, e - 2)
                down(c, EXPERTS - 2)
                down(c, EXPERTS - 1)
                pe.wait_ge(updated, 2 * c + 2)

        @block.scalar
        def _(act):
            with act.Fori(0, 4) as c:
                for e in range(EXPERTS):
                    act.wait_ge(hidden_filled, EXPERTS * c + e + 1)
                    act.activation(h[:, e % 4, :], g.st[:, e % 4, :], ACT.Gelu, bias=g.vec(f"mb1_{e}")).then_inc(gelu_done, 1)

        @block.vector
        def _(dve):
            with dve.Fori(0, 4) as c:
                for e in range(EXPERTS):
                    dve.wait_ge(gelu_done, EXPERTS * c + e + 1)
                    for x in range(2):
                        part = h[:, e % 4, x * SEQ:(x + 1) * SEQ]
                        ins = dve.tensor_scalar(part, part, gate[:, :, :].rearrange("p b e -> p (b e)")[
                            :, bass.ds((c * 2 + x) * EXPERTS + e, 1)], None, ALU.mult)
                    ins.then_inc(gated, 1)
                dve.wait_ge(out_filled, c + 1)
                for x in range(2):
                    ins = dve.tensor_scalar(tmp_out[:, x * SEQ:(x + 1) * SEQ], g.ov[:, x * SEQ:(x + 1) * SEQ],
                                            gb[:, bass.ds(c * 2 + x, 1)], g.gates[:, 5:6], ALU.add, ALU.mult)
                ins.then_inc(updated, 1)
                dve.wait_ge(updated, 2 * c + 1)
                xs = g.x[:, cols(c)]
                dve.tensor_tensor(xs, xs, tmp_out[:, :], ALU.add).then_inc(updated, 1)


def soft_moe_ffn(g, tmp):
    nc = g.nc
    pooled, prod, sc = tmp("s_pooled", [P, NB], F32), tmp("s_prod", [P, NB, EXPERTS], F32), tmp("s_scores", [P, NB, EXPERTS], F32)
    top, ex, total = tmp("s_top", [P, NB, 8], F32), tmp("s_exp", [P, NB, EXPERTS], F32), tmp("s_total", [P, NB], F32)
    gate = tmp("s_gate", [P, NB, EXPERTS], F32)
    h, acc = tmp("s_hidden", [P, 4, C], F32), tmp("s_acc", [P, C], F32)
    shape = [P, NB, EXPERTS]
    own = g.sem("s_own")
    with nc.Block() as block:
        @block.vector
        def _(dve):
            chain = Chain(dve, own)
            chain.link(dve.tensor_reduce(pooled[:, :], g.y[:, :].rearrange("p (b s) -> p b s", b=NB), AX.X, ALU.add))
            dve.tensor_scalar(pooled[:, :], pooled[:, :], 1.0 / SEQ, None, ALU.mult)
    gate_scores(g, pooled[:, :], g.vec("r2_0", EXPERTS), g.rbias[:, EXPERTS:2 * EXPERTS], prod, sc, g.sem("gate_steps"), 2)
    exp_done = g.sem("s_exp_done")
    with nc.Block() as block:
        @block.scalar
        def _(act):
            act.wait_ge(own, 2 + NB)
            act.activation(ex[:, :, :], ex[:, :, :], ACT.Exp).then_inc(exp_done, 1)

        @block.vector
        def _(dve):
            chain = Chain(dve, own)
            chain.start(1)
            for b in range(NB):
                chain.link(dve.max(top[:, b, :], sc[:, b, :]))
            chain.link(dve.tensor_tensor(ex[:, :, :], sc[:, :, :], top[:, :, 0:1].broadcast_to(shape), ALU.subtract))
            chain.link(dve.tensor_tensor(gate[:, :, :], sc[:, :, :], top[:, :, 1:2].broadcast_to(shape), ALU.is_ge))
            dve.wait_ge(exp_done, 1)
            chain.link(dve.tensor_tensor(gate[:, :, :], gate[:, :, :], ex[:, :, :], ALU.mult))
            chain.link(dve.tensor_reduce(total[:, :], gate[:, :, :], AX.X, ALU.add))
            chain.link(dve.reciprocal(total[:, :], total[:, :]))
            dve.tensor_tensor(gate[:, :, :], gate[:, :, :], total[:, :].unsqueeze(2).broadcast_to(shape), ALU.mult)
    hidden_filled, gelu_done, summed = g.sem("s_hidden_filled"), g.sem("s_gelu_done"), g.sem("s_summed")
    with nc.Block() as block:
        @block.tensor
        def _(pe):
            with pe.Fori(0, 4) as c:
                for e in range(EXPERTS):
                    if e >= 4:
                        pe.wait_ge(gelu_done, EXPERTS * c + e - 3)
                    pe.matmul(g.st[:, e % 4, :], g.wm(f"e_{e}"), g.y[:, cols(c)], start=True, stop=True)\
                        .then_inc(hidden_filled, 1)
                pe.wait_ge(gelu_done, EXPERTS * c + EXPERTS)

        @block.scalar
        def _(act):
            with act.Fori(0, 4) as c:
                for e in range(EXPERTS):
                    act.wait_ge(hidden_filled, EXPERTS * c + e + 1)
                    if e >= 4:
                        act.wait_ge(summed, (EXPERTS + 1) * c + e - 3)
                    act.activation(h[:, e % 4, :], g.st[:, e % 4, :], ACT.Gelu, bias=g.vec(f"eb_{e}")).then_inc(gelu_done, 1)
                act.wait_ge(summed, (EXPERTS + 1) * c + EXPERTS)

        @block.vector
        def _(dve):
            with dve.Fori(0, 4) as c:
                for e in range(EXPERTS):
                    dve.wait_ge(gelu_done, EXPERTS * c + e + 1)
                    if e:
                        dve.wait_ge(summed, (EXPERTS + 1) * c + e)
                    for x in range(2):
                        part, into = h[:, e % 4, x * SEQ:(x + 1) * SEQ], acc[:, x * SEQ:(x + 1) * SEQ]
                        w = gate[:, :, :].rearrange("p b e -> p (b e)")[:, bass.ds((c * 2 + x) * EXPERTS + e, 1)]
                        if e == 0:
                            ins = dve.tensor_scalar(into, part, w, None, ALU.mult)
                        else:
                            ins = dve.scalar_tensor_tensor(out=into, in0=part, scalar=w, in1=into, op0=ALU.mult, op1=ALU.add)
                    ins.then_inc(summed, 1)
                dve.wait_ge(summed, (EXPERTS + 1) * c + EXPERTS)
                xs = g.x[:, cols(c)]
                dve.scalar_tensor_tensor(out=xs, in0=acc[:, :], scalar=g.gates[:, 6:7], in1=xs,
                                         op0=ALU.mult, op1=ALU.add).then_inc(summed, 1)
                dve.wait_ge(summed, (EXPERTS + 1) * c + EXPERTS + 1)


QB, QEPS, ROUND = 128.0, 1e-5, 1.5 * 2.0 ** 23


def quantised_ffn(g, tmp):
    nc = g.nc
    wabs, wq = tmp("q_abs", [P, P], F32), tmp("q_w", [P, P], F32)
    col = tmp("q_columns", [P, 12], F32)
    ext = tmp("q_extrema", [P, 4], F32)
    xq = tmp("q_x", [P, 2, C], F32)
    own, all_max, total = g.sem("q_own"), g.sem("q_all_max"), g.sem("q_total")
    absmax = bass.bass_isa.ReduceOp.max

    def cl(i):
        return col[:, i:i + 1]

    with nc.Block() as block:
        @block.vector
        def _(dve):
            chain = Chain(dve, own)
            w = g.wm("quant")
            dve.tensor_reduce(cl(0), g.y[:, :], AX.X, ALU.max)
            chain.link(dve.tensor_reduce(cl(1), g.y[:, :], AX.X, ALU.min))
            chain.link(dve.tensor_scalar(cl(1), cl(1), -1.0, None, ALU.mult))
            chain.link(dve.tensor_tensor(cl(2), cl(0), cl(1), ALU.max))
            chain.link(dve.tensor_scalar(wabs[:, :], w, -1.0, None, ALU.mult))
            chain.link(dve.tensor_tensor(wabs[:, :], wabs[:, :], w, ALU.max))
            chain.link(dve.tensor_reduce(cl(3), wabs[:, :], AX.X, ALU.add))
            dve.wait_ge(total, 1)
            chain.link(dve.tensor_scalar(cl(4), g.ov[:, 0:1], 1.0 / (P * P), None, ALU.mult))
            chain.link(dve.tensor_scalar(cl(5), cl(4), QEPS, None, ALU.add))
            chain.link(dve.reciprocal(cl(5), cl(5)))
            chain.link(dve.tensor_scalar(wq[:, :], w, cl(5), ROUND, ALU.mult, ALU.add))
            chain.link(dve.tensor_scalar(wq[:, :], wq[:, :], ROUND, 1.0, ALU.subtract, ALU.min))
            chain.link(dve.tensor_scalar(wq[:, :], wq[:, :], -1.0, None, ALU.max))
            dve.wait_ge(all_max, 1)
            chain.link(dve.reciprocal(cl(7), cl(6)))
            chain.link(dve.tensor_tensor(cl(8), cl(6), cl(4), ALU.mult))
            dve.tensor_scalar(cl(8), cl(8), 1.0 / QB, g.gates[:, 7:8], ALU.mult, ALU.mult)

        @block.gpsimd
        def _(pool):
            pool.wait_ge(own, 3)
            pool.partition_all_reduce(cl(6), cl(2), P, absmax).then_inc(all_max, 1)

        @block.tensor
        def _(pe):
            pe.wait_ge(own, 6)
            pe.matmul(g.ov[:, 0:1], g.f("ones"), cl(3), start=True, stop=True).then_inc(total, 1)
    scaled, clipped, filled, updated = g.sem("q_scaled"), g.sem("q_clipped"), g.sem("q_filled"), g.sem("q_updated")
    with nc.Block() as block:
        @block.vector
        def _(dve):
            with dve.Fori(0, 4) as c:
                x = xq[:, 0, :]
                dve.tensor_scalar(x, g.y[:, cols(c)], QB, cl(7), ALU.mult, ALU.mult).then_inc(scaled, 1)
                dve.wait_ge(scaled, c + 1)
                dve.tensor_scalar(x, x, QEPS - QB, QB - QEPS, ALU.max, ALU.min).then_inc(clipped, 1)
                dve.wait_ge(filled, c + 1)
                xs = g.x[:, cols(c)]
                dve.scalar_tensor_tensor(out=xs, in0=g.ov[:, :], scalar=cl(8), in1=xs,
                                         op0=ALU.mult, op1=ALU.add).then_inc(updated, 1)

        @block.tensor
        def _(pe):
            with pe.Fori(0, 4) as c:
                pe.wait_ge(clipped, c + 1)
                pe.matmul(g.ov[:, :], wq[:, :], xq[:, 0, :], start=True, stop=True).then_inc(filled, 1)
                pe.wait_ge(updated, c + 1)


def gated_layers(nc, a, out, stop=99):
    with ExitStack() as ctx:
        g = Core(nc, ctx, a)

        phases = [0]

        def phase(work, *args):
            phases[0] += 1
            tag = f"_{phases[0]}"
            with ExitStack() as inner:
                work(*args, lambda name, shape, dt: inner.enter_context(nc.sbuf_tensor(name + tag, shape, dt)))

        def whole(buf):
            return lambda c: buf[:, cols(c)]

        uses = [0]

        def norm(src, dst, eps, scale=None, shift=None):
            phase(lambda tmp: layernorm(g, uses[0], whole(src), whole(dst), eps, tmp, scale, shift))
            uses[0] += 1

        phase(load_everything, g)
        for l in range(4):
            if 2 * l >= stop:
                break
            norm(g.x, g.y, "eps5")

            def attend(tmp):
                q_all, k_all = tmp("q_all", [P, TOK], F32), tmp("k_all", [P, TOK], F32)
                phase(project, g, l, q_all, k_all)
                phase(cross_attention, g, l, q_all, k_all)

            phase(attend)
            if 2 * l + 1 >= stop:
                break
            norm(g.x, g.y, "eps5")
            if l == 0:
                phase(local_transformer, g)
                add_gated(g)
            elif l == 1:
                phase(moe_ffn, g)
            elif l == 2:
                phase(soft_moe_ffn, g)
            else:
                norm(g.y, g.y, "eps3", g.vec("gamma"), g.vec("beta"))
                phase(quantised_ffn, g)
        stored = g.sem("stored")
        with nc.Block() as block:
            @block.sync
            def _(sp):
                sp.dma_start(out[:, :], g.x[:, :]).then_inc(stored, 16)
                sp.wait_ge(stored, 16)


def lay_out(inputs):
    i = {k: np.asarray(v) for k, v in inputs.items()}
    arr = {}
    arr["xT"] = i["x"].reshape(TOK, P).T
    arr["ctxT"] = i["ctx_1024"].reshape(TOK, P).T
    m = i["mask_SxS2_ik0"]
    arr["mask_q"] = m.reshape(2, P, SEQ).transpose(1, 0, 2)
    arr["mask_k"] = m.T.reshape(2, P, SEQ).transpose(1, 0, 2)
    mb = i["mask_BxS2_ik0"]
    arr["pad_r"] = mb.reshape(1, TOK)
    arr["pad_c"] = mb.reshape(NB, 2, P).transpose(2, 0, 1).reshape(P, 2 * NB)
    arr["gates"] = np.concatenate([i["g_xattn"], i["g_ffn"]]).reshape(1, 8)
    arr["rbias"] = np.concatenate([i["L1_ffn_br"], i["L2_ffn_gate_b"]]).reshape(1, 2 * EXPERTS)
    d = np.arange(P)
    partner = d // HD * HD + (d % HD + HD // 2) % HD
    w = {"q0": i["L0_xattn_Wq"].T, "q0r": i["L0_xattn_Wq"].T[:, partner],
         "k0": i["L0_xattn_Wk"].T, "k0r": i["L0_xattn_Wk"].T[:, partner],
         "v0": i["L0_xattn_Wv"].T, "o0": i["L0_xattn_Wo"].T,
         "q2": i["L2_xattn_Wq"], "k2": i["L2_xattn_Wk"], "v2": i["L2_xattn_Wv"], "o2": i["L2_xattn_Wo"],
         "quant": i["L3_ffn_weight"]}
    for n in "qkvo":
        w[n + "1"] = i["L1_xattn_W" + n].T
        w[n + "3"] = i["L3_xattn_w" + n].T
    v = {"qn": np.tile(i["L0_xattn_q_norm_w"], HEADS), "kn": np.tile(i["L0_xattn_k_norm_w"], HEADS),
         "gamma": i["L3_ffn_ln_gamma"], "beta": i["L3_ffn_ln_beta"], "zero": np.zeros(P, np.float32)}
    v["qnr"], v["knr"] = v["qn"][partner], v["kn"][partner]
    for n in "qkvo":
        v["b" + n + "1"] = i["L1_xattn_b" + n]
        v["b" + n + "3"] = i["L3_xattn_b" + n]
    for e in range(EXPERTS):
        w[f"m1_{e}"], w[f"m2_{e}"] = i["L1_ffn_W1"][e], i["L1_ffn_W2"][e]
        w[f"e_{e}"] = i["L2_ffn_expert_w"][e].T
        v[f"mb1_{e}"], v[f"mb2_{e}"], v[f"eb_{e}"] = i["L1_ffn_b1"][e], i["L1_ffn_b2"][e], i["L2_ffn_expert_b"][e]
        v[f"r1_{e}"], v[f"r2_{e}"] = i["L1_ffn_Wr"][:, e], i["L2_ffn_gate_w"][e]
    arr["w"] = np.concatenate([w[n] for n in W_NAMES], axis=1)
    arr["v"] = np.stack([v[n] for n in V_NAMES], axis=1)
    wa, wf, qk = [], [], []
    hidden = FFC * P
    swap = (np.arange(LHD) + LHD // 2) % LHD
    for n in range(DEPTH):
        wo = i["L0_ffn_Wo"][n].reshape(8, P, P).transpose(1, 0, 2).reshape(P, -1)
        wa.append(np.concatenate([i["L0_ffn_Wqkv"][n], wo], axis=1))
        w1 = np.zeros((P, 2, hidden), np.float32)
        w1[:, :, :FFN_IN] = i["L0_ffn_W1"][n].reshape(P, 2, FFN_IN)
        w2 = np.zeros((hidden, P), np.float32)
        w2[:FFN_IN] = i["L0_ffn_W2"][n]
        b1 = np.zeros((2, hidden), np.float32)
        b1[:, :FFN_IN] = i["L0_ffn_b1"][n].reshape(2, FFN_IN)
        wf.append(np.concatenate([w1.reshape(P, -1), w2.reshape(FFC, P, P).transpose(1, 0, 2).reshape(P, -1),
                                  i["L0_ffn_ln_g"][n][:, None], i["L0_ffn_ln_b"][n][:, None],
                                  b1.reshape(2 * FFC, P).T, i["L0_ffn_b2"][n][:, None]], axis=1))
        qs, ks = i["L0_ffn_q_scale"][n], i["L0_ffn_k_scale"][n]
        qk.append(np.concatenate([qs, qs[swap], ks, ks[swap]]))
    arr["wa"], arr["wf"], arr["qkscale"] = np.concatenate(wa, axis=1), np.concatenate(wf, axis=1), np.stack(qk)
    arr["cf"] = F_TAB.astype(np.float32)
    arr["cb"] = B_TAB.astype(mybir.dt.np(BF16))
    return {k: np.ascontiguousarray(x) for k, x in arr.items()}


def kernel(**inputs):
    import concourse.bacc as bacc
    from concourse.bass_utils import run_bass_kernel_spmd

    nc = bacc.Bacc("TRN2", target_bir_lowering=False, num_devices=1)
    arrays = lay_out(inputs)
    a = {n: nc.dram_tensor("in_" + n, x.shape, mybir.dt.from_np(x.dtype), kind="ExternalInput").ap()
         for n, x in arrays.items()}
    out = nc.dram_tensor("out_x", (P, TOK), F32, kind="ExternalOutput").ap()
    gated_layers(nc, a, out)
    r = run_bass_kernel_spmd(nc, [{"in_" + n: x for n, x in arrays.items()}], core_ids=[0])
    return np.ascontiguousarray(r.results[0]["out_x"].T).reshape(NB, SEQ, P)
```

```python
from contextlib import ExitStack

import numpy as np

import concourse.bass as bass
from concourse import mybir

F32 = mybir.dt.float32
F32R = mybir.dt.float32r
BF16 = mybir.dt.bfloat16
I32 = mybir.dt.int32
ALU = mybir.AluOpType
ACT = mybir.ActivationFunctionType
AX = mybir.AxisListType

P = 128
NB, SEQ = 8, 256
TOK = NB * SEQ
HEADS = 16
HD = P // HEADS
DEPTH, LHD, WIN = 6, 64, 32
INNER = HEADS * LHD
FFN_IN = int(P * 4 * 2 / 3)
FFC = -(-FFN_IN // P)
EXPERTS = 8
KSPAN = P + WIN
PACK = KSPAN + P
MASKED = -(2.0 ** 100)
C = 512
EXP_AND_LN = "natural_log_exp_and_others"

W_NAMES = (["q0", "q0r", "k0", "k0r", "v0", "o0", "q1", "k1", "v1", "o1", "q2", "k2", "v2", "o2", "q3", "k3", "v3", "o3"]
           + [f"m1_{e}" for e in range(EXPERTS)] + [f"m2_{e}" for e in range(EXPERTS)]
           + [f"e_{e}" for e in range(EXPERTS)] + ["quant"])
W_AT = {n: P * i for i, n in enumerate(W_NAMES)}
V_NAMES = (["bq1", "bk1", "bv1", "bo1", "bq3", "bk3", "bv3", "bo3", "qn", "qnr", "kn", "knr", "gamma", "beta", "zero"]
           + [f"mb1_{e}" for e in range(EXPERTS)] + [f"mb2_{e}" for e in range(EXPERTS)]
           + [f"eb_{e}" for e in range(EXPERTS)] + [f"r1_{e}" for e in range(EXPERTS)] + [f"r2_{e}" for e in range(EXPERTS)])
V_AT = {n: i for i, n in enumerate(V_NAMES)}
D_QKV, D_WO, D_W1, D_W2 = 0, 3 * INNER, 3 * INNER + 8 * P, 3 * INNER + 8 * P + 2 * FFC * P
D_VEC = D_W2 + FFC * P
D_ALL = D_VEC + 3 + 2 * FFC
F_AT, B_AT = {}, {}


def constants():
    f, b = {}, {}
    eye = np.eye(P)
    f["ident"] = eye
    f["mean"] = np.full((P, P), 1.0 / P)
    f["center"] = eye - 1.0 / P
    f["ones"] = np.ones((P, P))
    p = np.arange(P)
    f["headmean"] = (p[:, None] // HD == p[None, :] // HD) / HD
    f["headmask"] = (p[:, None] // HD == np.arange(HEADS)[None, :]) * 1.0
    opad = np.zeros((P, 4, 32))
    for j in range(4):
        opad[:, j, HD * j:HD * j + HD] = 1.0
    f["sumpad"] = opad.reshape(P, -1)
    osel = np.zeros((P, 4, 32))
    osel[:, :, 4:] = 1.0
    for j in range(4):
        osel[:, j, j] = 1.0
    f["sumsel"] = osel.reshape(P, -1)
    t = np.arange(SEQ)
    d = p % HD
    for n, theta, scale in (("q", 32.0, HD ** -0.5), ("k", 1000.0, 1.0)):
        fr = np.float32(theta) ** (-(np.arange(0, HD, 2, dtype=np.float32)) / np.float32(HD))
        ang = (t[None, :].astype(np.float32) * fr[d % (HD // 2)][:, None]).astype(np.float64)
        f[n + "cos"] = np.cos(ang) * scale
        f[n + "sin"] = np.sin(ang) * np.where(d < HD // 2, -1.0, 1.0)[:, None] * scale
    half = np.arange(0, LHD, 2, dtype=np.float32)
    inv = (1.0 / np.float32(10000.0) ** (half / np.float32(LHD))).astype(np.float32)
    fr = (t[:, None].astype(np.float32) * inv[None, :]).astype(np.float64)
    fr = np.concatenate([fr, fr], -1)
    base = (half.astype(np.float64) + 0.4 * LHD) / (1.4 * LHD)
    power = (t - SEQ // 2) / (WIN // 2)
    sc = base[None, :] ** power[:, None]
    sc = np.concatenate([sc, sc], -1)
    sign = np.where(np.arange(LHD) < LHD // 2, -1.0, 1.0)[None, :]
    for n, s in (("lq", 8.0 * sc), ("lk", 1.0 / sc)):
        for w, tab in (("cos", np.cos(fr) * s), ("sin", np.sin(fr) * sign * s)):
            f[n + w] = tab.reshape(2, P, LHD).transpose(1, 0, 2).reshape(P, -1)
    e = np.arange(EXPERTS)
    for n, v in (("eps5", 1e-5), ("eps6", 1e-6), ("eps3", 1e-3), ("lnoff", 10 * np.log(2.0))):
        f[n] = np.full((P, 1), v)
    f["earlier"] = np.broadcast_to((e[None, :] < e[:, None]).reshape(1, -1) * 1.0, (P, EXPERTS * EXPERTS))
    b["ident"] = eye
    first = np.zeros((P, P))
    first[0] = 1.0
    b["first"] = first
    sel = np.zeros((P, HEADS, P))
    for h in range(HEADS):
        sel[h, h] = 1.0
        sel[32 + h, h] = 1.0
    b["sel"] = sel.reshape(P, -1)
    selr = np.zeros((P, HEADS // 2, P))
    for c in range(HEADS // 2):
        for m in range(P):
            h = 2 * c + m // LHD
            selr[32 * (h % 4) + h // 4, c, m] = 1.0
    f["selr"] = selr.reshape(P, -1)
    q0, k0 = np.arange(P)[:, None], np.arange(P)[None, :]
    b["band0"] = np.where((q0 - k0 >= 0) & (q0 - k0 <= WIN), 0.0, MASKED)
    k1 = np.arange(KSPAN)[None, :]
    b["band1"] = np.where((q0 - k1 + WIN >= 0) & (q0 - k1 + WIN <= WIN), 0.0, MASKED)
    qq = np.arange(KSPAN)[None, :]
    b["bandT"] = np.where((qq - q0 >= 0) & (qq - q0 <= WIN), 0.0, MASKED)
    out = []
    for tables, at in ((f, F_AT), (b, B_AT)):
        n = 0
        for name, tab in tables.items():
            at[name] = n
            n += tab.shape[1]
        out.append(np.concatenate([np.asarray(v, np.float64) for v in tables.values()], axis=1))
    return out


F_TAB, B_TAB = constants()



class Chain:

    def __init__(self, eng, sem):
        self.eng, self.sem, self.n, self.off = eng, sem, 0, 0

    def start(self, off):
        self.n, self.off = 0, off

    def link(self, ins):
        ins.then_inc(self.sem, 1)
        self.n += 1
        self.eng.wait_ge(self.sem, self.off + self.n)

    def ends(self, n):
        assert self.n == n, (self.n, n)


class Core:

    def __init__(self, nc, ctx, a):
        self.nc, self.a, self.ctx = nc, a, ctx
        sb = self.sb
        self.x = sb("x", [P, TOK], F32)
        self.y = sb("y", [P, TOK], F32)
        self.ctxT = sb("ctxT", [P, TOK], F32)
        self.w = sb("w", [P, P * len(W_NAMES)], F32)
        self.v = sb("v", [P, len(V_NAMES)], F32)
        self.cf = sb("cf", [P, F_TAB.shape[1]], F32)
        self.cb = sb("cb", [P, B_TAB.shape[1]], BF16)
        self.gates = sb("gates", [P, 8], F32)
        self.gbo = sb("gbo", [P, 4], F32)
        self.rbias = sb("rbias", [P, 2 * EXPERTS], F32)
        self.maskq = sb("maskq", [P, 2, SEQ], BF16)
        self.maskk = sb("maskk", [P, 2, SEQ], BF16)
        self.padrow = sb("padrow", [P, TOK], BF16)
        self.padcol = sb("padcol", [P, 2 * NB], F32)
        self.ring = ctx.enter_context(nc.psum_tensor("ring", [P, 2, C], F32))
        self.st = ctx.enter_context(nc.psum_tensor("st", [P, 4, C], F32))
        self.ov = ctx.enter_context(nc.psum_tensor("ov", [P, C], F32))
        self.sm = ctx.enter_context(nc.psum_tensor("sm", [P, C], F32))
        self.sems = {}

    def sb(self, name, shape, dt):
        return self.ctx.enter_context(self.nc.sbuf_tensor(name, shape, dt))

    def sem(self, name):
        if name not in self.sems:
            self.sems[name] = self.ctx.enter_context(self.nc.semaphore(name))
        return self.sems[name]

    def f(self, name, width=P):
        return self.cf[:, F_AT[name]:F_AT[name] + width]

    def b(self, name, width=P):
        return self.cb[:, B_AT[name]:B_AT[name] + width]

    def wm(self, name):
        return self.w[:, W_AT[name]:W_AT[name] + P]

    def vec(self, name, n=1):
        return self.v[:, V_AT[name]:V_AT[name] + n]


def cols(c, width=C):
    return bass.ds(c * width, width)


def load_everything(g, tmp):
    nc, a = g.nc, g.a
    loaded, prepared = g.sem("inputs_loaded"), g.sem("inputs_prepared")
    mask_q, mask_k, pad_r, pad_c = (tmp(n, s, I32) for n, s in (
        ("mask_q", [P, 2, SEQ]), ("mask_k", [P, 2, SEQ]), ("pad_r", [1, TOK]), ("pad_c", [P, 2 * NB])))
    loads = ((g.x[:, :], a["xT"]), (g.cf[:, :], a["cf"]), (g.ctxT[:, :], a["ctxT"]),
             (g.w[:, :], a["w"]), (g.cb[:, :], a["cb"]), (g.v[:, :], a["v"]),
             (mask_q[:, :, :], a["mask_q"]), (mask_k[:, :, :], a["mask_k"]), (pad_r[:, :], a["pad_r"]),
             (pad_c[:, :], a["pad_c"]), (g.gates[:, :], a["gates"].broadcast_to([P, 8])),
             (g.rbias[:, :], a["rbias"].broadcast_to([P, 2 * EXPERTS])))
    with nc.Block() as block:
        @block.sync
        def _(sp):
            for dst, src in loads:
                sp.dma_start(dst, src).then_inc(loaded, 16)
            sp.wait_ge(loaded, 16 * len(loads))

        @block.scalar
        def _(act):
            act.wait_ge(loaded, 16 * len(loads))
            act.activation(g.gates[:, :], g.gates[:, :], ACT.Tanh).then_inc(prepared, 1)

        @block.vector
        def _(dve):
            dve.memset(g.padrow[:, :], 0.0).then_inc(prepared, 1)
            dve.wait_ge(loaded, 16 * len(loads))
            dve.tensor_scalar(g.maskq[:, :, :], mask_q[:, :, :], 0.0, MASKED, ALU.is_equal, ALU.mult)
            dve.tensor_scalar(g.maskk[:, :, :], mask_k[:, :, :], 0.0, MASKED, ALU.is_equal, ALU.mult)
            dve.tensor_scalar(g.padcol[:, :], pad_c[:, :], 0.0, MASKED, ALU.is_equal, ALU.mult)
            dve.wait_ge(prepared, 2)
            dve.tensor_scalar(g.padrow[0:1, :], pad_r[:, :], 0.0, MASKED, ALU.is_equal, ALU.mult)
            for l in range(4):
                bo = g.vec(f"bo{l}") if l in (1, 3) else g.vec("zero")
                dve.tensor_tensor(g.gbo[:, l:l + 1], g.gates[:, l:l + 1], bo, ALU.mult)


def layernorm(g, use, src, out, eps, tmp, scale=None, shift=None):
    nc = g.nc
    centered, squared, variance, rstd, normed = (
        g.sem("ln_" + n) for n in ("centered", "squared", "variance", "rstd", "normed"))
    sq, rs = tmp("ln_sq", [P, 2, C], F32), tmp("ln_rs", [P, 2, C], F32)
    base = use * 4
    with nc.Block() as block:
        @block.tensor
        def _(pe):
            with pe.Fori(0, 2) as k:
                for u in range(2):
                    pe.matmul(g.st[:, u, :], g.f("center"), src(k * 2 + u), start=True, stop=True).then_inc(centered, 1)
                for u in range(2):
                    pe.wait_ge(squared, base + k * 2 + u + 1)
                    pe.matmul(g.st[:, 2 + u, :], g.f("mean"), sq[:, u, :], start=True, stop=True).then_inc(variance, 1)
                pe.wait_ge(normed, base + k * 2 + 2)

        @block.scalar
        def _(act):
            act.preload_act_table_set(EXP_AND_LN)
            with act.Fori(0, 2) as k:
                for u in range(2):
                    act.wait_ge(centered, base + k * 2 + u + 1)
                    act.activation(sq[:, u, :], g.st[:, u, :], ACT.Square).then_inc(squared, 1)
                for u in range(2):
                    act.wait_ge(variance, base + k * 2 + u + 1)
                    act.activation(rs[:, u, :], g.st[:, 2 + u, :], ACT.Ln, bias=g.f(eps, 1)).then_inc(rstd, 1)
                    act.wait_ge(rstd, 2 * (base + k * 2 + u) + 1)
                    act.activation(rs[:, u, :], rs[:, u, :], ACT.Exp, scale=-0.5).then_inc(rstd, 1)

        @block.vector
        def _(dve):
            affine = g.sem("ln_affine")
            with dve.Fori(0, 2) as k:
                for u in range(2):
                    dve.wait_ge(rstd, 2 * (base + k * 2 + u) + 2)
                    dve.tensor_tensor(out(k * 2 + u), g.st[:, u, :], rs[:, u, :], ALU.mult).then_inc(normed, 1)
                    if scale is not None:
                        dve.wait_ge(normed, base + k * 2 + u + 1)
                        dve.tensor_scalar(out(k * 2 + u), out(k * 2 + u), scale, shift, ALU.mult, ALU.add)


def project(g, l, q_all, k_all, tmp):
    nc = g.nc
    lane = (l - 1) * 4
    filled = g.sem("proj_filled" if l else "rope_filled")
    out_done = g.sem("proj_done" if l else "rope_done")
    if l:
        with nc.Block() as block:
            @block.tensor
            def _(pe):
                with pe.Fori(0, 2) as k:
                    for u in range(2):
                        pe.matmul(g.st[:, 2 * u, :], g.wm(f"q{l}"), g.y[:, cols(k * 2 + u)], start=True, stop=True)
                        pe.matmul(g.st[:, 2 * u + 1, :], g.wm(f"k{l}"), g.ctxT[:, cols(k * 2 + u)],
                                  start=True, stop=True).then_inc(filled, 1)
                    pe.wait_ge(out_done, lane + k * 2 + 2)

            @block.vector
            def _(dve):
                with dve.Fori(0, 2) as k:
                    for u in range(2):
                        dve.wait_ge(filled, lane + k * 2 + u + 1)
                        dve.tensor_scalar(q_all[:, cols(k * 2 + u)], g.st[:, 2 * u, :],
                                          g.vec(f"bq{l}" if l != 2 else "zero"), None, ALU.add)
                        dve.tensor_scalar(k_all[:, cols(k * 2 + u)], g.st[:, 2 * u + 1, :],
                                          g.vec(f"bk{l}" if l != 2 else "zero"), HD ** -0.5,
                                          ALU.add, ALU.mult).then_inc(out_done, 1)
        return

    squared, mean_sq, rstd = g.sem("head_squared"), g.sem("head_mean_sq"), g.sem("head_rstd")
    rotated = g.sem("head_rotated")
    sq, rs, t1, t2 = (tmp(n, [P, 2, C], F32) for n in ("rope_sq", "rope_rs", "rope_t1", "rope_t2"))
    outs = (q_all, k_all)
    with nc.Block() as block:
        @block.tensor
        def _(pe):
            with pe.Fori(0, 4) as c:
                for i, (n, src) in enumerate((("q", g.y), ("k", g.ctxT))):
                    pe.matmul(g.st[:, 2 * i, :], g.wm(n + "0"), src[:, cols(c)], start=True, stop=True)
                    pe.matmul(g.st[:, 2 * i + 1, :], g.wm(n + "0r"), src[:, cols(c)],
                              start=True, stop=True).then_inc(filled, 1)
                for i in range(2):
                    pe.wait_ge(squared, c * 2 + i + 1)
                    pe.matmul(g.ring[:, i, :], g.f("headmean"), sq[:, i, :], start=True, stop=True).then_inc(mean_sq, 1)
                pe.wait_ge(out_done, c * 2 + 2)

        @block.scalar
        def _(act):
            act.preload_act_table_set(EXP_AND_LN)
            with act.Fori(0, 4) as c:
                for i in range(2):
                    act.wait_ge(filled, c * 2 + i + 1)
                    act.activation(sq[:, i, :], g.st[:, 2 * i, :], ACT.Square).then_inc(squared, 1)
                for i in range(2):
                    act.wait_ge(mean_sq, c * 2 + i + 1)
                    act.activation(rs[:, i, :], g.ring[:, i, :], ACT.Ln, bias=g.f("eps6", 1)).then_inc(rstd, 1)
                    act.wait_ge(rstd, 2 * (c * 2 + i) + 1)
                    act.activation(rs[:, i, :], rs[:, i, :], ACT.Exp, scale=-0.5).then_inc(rstd, 1)

        @block.vector
        def _(dve):
            def per_batch(ap):
                return ap.rearrange("p (b s) -> p b s", b=2)

            def twice(name):
                return g.f(name, SEQ).unsqueeze(1).broadcast_to([P, 2, SEQ])

            with dve.Fori(0, 4) as c:
                for i, n in enumerate("qk"):
                    dve.wait_ge(squared, c * 2 + i + 1)
                    dve.scalar_tensor_tensor(out=per_batch(t1[:, i, :]), in0=per_batch(g.st[:, 2 * i, :]),
                                             scalar=g.vec(n + "n"), in1=twice(n + "cos"), op0=ALU.mult, op1=ALU.mult)
                    dve.scalar_tensor_tensor(out=per_batch(t2[:, i, :]), in0=per_batch(g.st[:, 2 * i + 1, :]),
                                             scalar=g.vec(n + "nr"), in1=twice(n + "sin"),
                                             op0=ALU.mult, op1=ALU.mult).then_inc(rotated, 1)
                    dve.wait_ge(rotated, 2 * (c * 2 + i) + 1)
                    dve.tensor_tensor(t1[:, i, :], t1[:, i, :], t2[:, i, :], ALU.add).then_inc(rotated, 1)
                for i in range(2):
                    dve.wait_ge(rotated, 2 * (c * 2 + i) + 2)
                    dve.wait_ge(rstd, 2 * (c * 2 + i) + 2)
                    dve.tensor_tensor(outs[i][:, cols(c)], t1[:, i, :], rs[:, i, :], ALU.mult).then_inc(out_done, 1)


def head_at(n):
    return 4 * (n % 4) + n // 4


def cross_attention(g, l, q_all, k_all, tmp):
    nc = g.nc
    filled, ring_dve = g.sem("x_ring_filled"), g.sem("x_ring_read")
    keys_staged, queries_r, queries_f = g.sem("x_keys_staged"), g.sem("x_queries_r"), g.sem("x_queries_f")
    scores_ready, probs_ready = g.sem("x_scores_ready"), g.sem("x_probs_ready")
    values_summed, sums_read, out_ready = g.sem("x_values_summed"), g.sem("x_sums_read"), g.sem("x_out_ready")
    own = g.sem("x_dve_own")
    vpad_zeroed, pad_staged = g.sem("x_vpad_zeroed"), g.sem("x_pad_staged")
    qm = [tmp(f"qm{u}", [P, HEADS, SEQ], F32) for u in range(2)]
    qmr = [tmp(f"qmr{u}", [P, HEADS, SEQ], F32R) for u in range(2)]
    kt = [tmp(f"kt{u}", [P, SEQ], F32) for u in range(2)]
    ktr = [tmp(f"ktr{u}", [P, SEQ], F32R) for u in range(2)]
    cs = [tmp(f"cs{u}", [P, SEQ], F32) for u in range(2)]
    vpad = [tmp(f"vpad{u}", [P, 2, 4 * 160], F32) for u in range(2)]
    pt = tmp("pt", [P, 8, C], F32)
    mrow = [tmp(f"mrow{u}", [P, 2 * HEADS], F32) for u in range(2)]
    mt = [tmp(f"mt{u}", [P, SEQ], BF16) for u in range(2)]
    on = [tmp(f"on{u}", [P, SEQ], F32) for u in range(2)]
    rsum = tmp("rsum", [P, SEQ], F32)
    upd = tmp("upd", [P, SEQ], F32)
    pad = [tmp(f"pad{u}", [P, 2], F32) for u in range(2)]
    ring = g.ring
    layer_items = 8 * 19
    first = 18

    def item(b, k):
        return l * layer_items + first + 19 * b + k

    with nc.Block() as block:
        @block.tensor
        def _(pe):
            def claim(n):
                pe.wait_ge(ring_dve, n - 1)

            def values(u, b, n, slot):
                pe.wait_ge(keys_staged, 3 * (l * 8 + b) + 2)
                for t in range(2):
                    mm = pe.matmul(ring[:, slot, t * P:(t + 1) * P], cs[u][:, t * P:(t + 1) * P], g.wm(f"v{l}"),
                                   start=True, stop=True)
                mm.then_inc(filled, 1)

            def row_scores(u, b, i, slot):
                t, h0 = i // 8, i % 8 * 2
                for h in (h0, h0 + 1):
                    out = ring[:, slot, (h - h0) * SEQ:(h - h0 + 1) * SEQ]
                    mm = pe.matmul(out, qmr[u][:, h, t * P:(t + 1) * P], ktr[u][:, :], start=True, stop=l not in (1, 2))
                    if l == 1:
                        mm = pe.matmul(out, g.b("ident"), g.maskq[:, t, :], start=False, stop=True)
                    if l == 2:
                        mm = pe.matmul(out, g.b("first"), g.padrow[:, cols(b, SEQ)], start=False, stop=True)
                mm.then_inc(filled, 1)

            def turn_maxima(u, slot):
                for t in range(2):
                    mm = pe.transpose(ring[0:HEADS, slot, t * P:(t + 1) * P], mrow[u][:, t * HEADS:(t + 1) * HEADS],
                                      g.f("ident"))
                mm.then_inc(filled, 1)

            def scores(u, b, quad):
                for j in range(4 * quad, 4 * quad + 4):
                    pair, kc = j // 2, j % 2
                    if j >= 4:
                        pe.wait_ge(probs_ready, 16 * (l * 8 + b) + j - 3)
                    for x in range(2):
                        h = head_at(2 * pair + x)
                        out = g.st[:, j % 4, x * SEQ:(x + 1) * SEQ]
                        pe.matmul(out, kt[u][:, kc * P:(kc + 1) * P], qm[u][:, h, :], start=True, stop=False)
                        if l == 1:
                            pe.matmul(out, g.b("ident"), g.maskk[:, kc, :], start=False, stop=False)
                        mm = pe.matmul(out, g.cb[:, B_AT["sel"] + h * P:B_AT["sel"] + (h + 1) * P], mt[u][:, :],
                                       start=False, stop=True)
                    mm.then_inc(scores_ready, 1)

            def sum_values(u, b, quad):
                pe.wait_ge(probs_ready, 16 * (l * 8 + b) + 4 * (quad + 1))
                for bank, lhs in ((g.ov, lambda kc, c: vpad[u][:, kc, c * 160 + 32 * quad:c * 160 + 32 * quad + 32]),
                                  (g.sm, lambda kc, c: g.cf[:, F_AT["sumpad"] + 32 * quad:F_AT["sumpad"] + 32 * quad + 32])):
                    for kc in range(2):
                        for c in range(4):
                            n = 4 * quad + c
                            mm = pe.matmul(bank[32 * c:32 * c + 32, 0:SEQ], lhs(kc, c),
                                           pt[:, (2 * (n // 2) + kc) % 8, (n % 2) * SEQ:(n % 2 + 1) * SEQ],
                                           start=quad == 0 and kc == 0, stop=quad == 3 and kc == 1)
                mm.then_inc(values_summed, 1)

            def body(b, u, more):
                n, s = item(b, 0), u
                if more:
                    claim(n)
                    values(1 - u, b + 1, n, s % 2)
                    pe.wait_ge(queries_r, l * 8 + b + 2)
                    pe.wait_ge(keys_staged, 3 * (l * 8 + b + 1) + 1)
                pe.wait_ge(queries_f, l * 8 + b + 1)
                pe.wait_ge(keys_staged, 3 * (l * 8 + b) + 3)
                pe.wait_ge(ring_dve, n - 1)
                for quad in range(4):
                    scores(u, b, quad)
                    if more and quad < 3:
                        for i in range((0, 5, 10)[quad], (5, 10, 16)[quad]):
                            claim(n + 1 + i)
                            row_scores(1 - u, b + 1, i, (s + 1 + i) % 2)
                    if quad == 3 and more:
                        pe.wait_ge(ring_dve, n + 17)
                        turn_maxima(1 - u, (s + 17) % 2)
                    if quad:
                        sum_values(u, b, quad - 1)
                sum_values(u, b, 3)
                k = 18 if more else 0
                claim(n + k)
                pe.wait_ge(out_ready, l * 8 + b + 1)
                pe.matmul(ring[:, (s + k) % 2, 0:SEQ], g.wm(f"o{l}"), on[u][:, :], start=True, stop=True).then_inc(filled, 1)

            pe.wait_ge(vpad_zeroed, l + 1)
            values(0, 0, 0, 0)
            pe.wait_ge(queries_r, l * 8 + 1)
            for i in range(16):
                if i >= 1:
                    claim(l * layer_items + 1 + i)
                row_scores(0, 0, i, (1 + i) % 2)
            pe.wait_ge(ring_dve, l * layer_items + 17)
            turn_maxima(0, 1)
            pe.wait_ge(ring_dve, l * layer_items + first)
            with pe.Fori(0, 3) as k:
                body(k * 2, 0, True)
                body(k * 2 + 1, 1, True)
            body(6, 0, True)
            body(7, 1, False)

        @block.scalar
        def _(act):
            act.preload_act_table_set(EXP_AND_LN)
            def stage_r(u, b):
                act.activation(ktr[u][:, :], k_all[:, cols(b, SEQ)], ACT.Copy).then_inc(keys_staged, 1)

            def stage_ctx(u, b):
                act.activation(cs[u][:, :], g.ctxT[:, cols(b, SEQ)], ACT.Copy).then_inc(keys_staged, 1)

            def stage_pad(u, b):
                act.activation(pad[u][:, :], g.padcol[:, bass.ds(b * 2, 2)], ACT.Copy).then_inc(pad_staged, 1)

            def stage_f(u, b):
                act.activation(kt[u][:, :], k_all[:, cols(b, SEQ)], ACT.Copy).then_inc(keys_staged, 1)

            def body(b, u, more, stage):
                if more:
                    stage_ctx(1 - u, b + 1)
                    stage_f(1 - u, b + 1)
                if l == 2:
                    act.wait_ge(pad_staged, b + 1)
                for j in range(16):
                    act.wait_ge(scores_ready, 16 * (l * 8 + b) + j + 1)
                    if j >= 8:
                        act.wait_ge(values_summed, 4 * (l * 8 + b) + j // 4 - 1)
                    kw = {"bias": pad[u][:, j % 2:j % 2 + 1]} if l == 2 else {}
                    act.activation(pt[:, j % 8, :], g.st[:, j % 4, :], ACT.Exp, **kw).then_inc(probs_ready, 1)
                    if j == 0 and l == 2 and more:
                        stage_pad(1 - u, b + 1)
                    if j == 11 and stage:
                        stage_r(u, b + 2)

            stage_r(0, 0)
            stage_ctx(0, 0)
            stage_f(0, 0)
            if l == 2:
                stage_pad(0, 0)
            stage_r(1, 1)
            with act.Fori(0, 3) as k:
                body(k * 2, 0, True, True)
                body(k * 2 + 1, 1, True, True)
            body(6, 0, True, False)
            body(7, 1, False, False)

        @block.vector
        def _(dve):
            chain = Chain(dve, own)

            def queries(dst, u, b, sem):
                for h in range(HEADS):
                    ins = dve.tensor_scalar(dst[u][:, h, :], q_all[:, cols(b, SEQ)], g.f("headmask", HEADS)[:, h:h + 1],
                                            None, ALU.mult)
                ins.then_inc(sem, 1)

            def values(u, n, slot):
                dve.wait_ge(filled, n + 1)
                for t in range(2):
                    dst = vpad[u][:, t, :].rearrange("p (c w) -> p c w", c=4).rearrange(
                        "p c (j s) -> p c j s", j=4)[:, :, :, 0:HD]
                    ins = dve.tensor_copy(dst, ring[:, slot, t * P:(t + 1) * P].rearrange("p (c j s) -> p c j s", c=4, j=4))
                ins.then_inc(ring_dve, 1)

            def row_max(u, i, n, slot):
                dve.wait_ge(filled, n + 1)
                at = i // 8 * HEADS + i % 8 * 2
                dve.tensor_reduce(mrow[u][:, at:at + 2], ring[:, slot, :].rearrange("p (h k) -> p h k", h=2),
                                  AX.X, ALU.max).then_inc(ring_dve, 1)

            def store_maxima(u, n, slot):
                dve.wait_ge(filled, n + 1)
                chain.link(dve.tensor_scalar(mt[u][0:HEADS, :], ring[0:HEADS, slot, 0:SEQ], -1.0, None, ALU.mult))
                dve.scalar_tensor_tensor(out=mt[u][32:32 + HEADS, :], in0=ring[0:HEADS, slot, 0:SEQ], scalar=-1.0,
                                         in1=mt[u][0:HEADS, :], op0=ALU.mult, op1=ALU.subtract).then_inc(ring_dve, 1)

            def normalise(u, b):
                dve.wait_ge(values_summed, 4 * (l * 8 + b + 1))
                chain.link(dve.reciprocal(rsum[:, :], g.sm[:, 0:SEQ]))
                dve.tensor_tensor(on[u][:, :], g.ov[:, 0:SEQ], rsum[:, :], ALU.mult).then_inc(sums_read, 1)
                dve.wait_ge(sums_read, l * 8 + b + 1)
                dve.tensor_scalar(on[u][:, :], on[u][:, :], g.vec(f"bv{l}" if l in (1, 3) else "zero"), None,
                                  ALU.add).then_inc(out_ready, 1)

            def residual(b, n, slot):
                dve.wait_ge(filled, n + 1)
                dve.tensor_scalar(upd[:, :], ring[:, slot, 0:SEQ], g.gates[:, l:l + 1], g.gbo[:, l:l + 1],
                                  ALU.mult, ALU.add).then_inc(ring_dve, 1)
                dve.wait_ge(ring_dve, n + 1)
                xs = g.x[:, cols(b, SEQ)]
                chain.link(dve.tensor_tensor(xs, xs, upd[:, :], ALU.add))

            def body(b, u, more, stage):
                n = item(b, 0)
                chain.start(l * 24 + 1 + b * 3)
                if more:
                    values(1 - u, n, u % 2)
                    for i in range(16):
                        row_max(1 - u, i, n + 1 + i, (u + 1 + i) % 2)
                    store_maxima(1 - u, n + 17, (u + 17) % 2)
                    queries(qm, 1 - u, b + 1, queries_f)
                normalise(u, b)
                residual(b, n + (18 if more else 0), (u + (18 if more else 0)) % 2)
                if stage:
                    queries(qmr, u, b + 2, queries_r)
                chain.ends(3 if more else 2)

            for u in range(2):
                dve.memset(vpad[u][:, :, :], 0.0)
                ins = dve.memset(mt[u][:, :], 0.0)
            ins.then_inc(vpad_zeroed, 1)
            dve.wait_ge(vpad_zeroed, l + 1)
            chain.start(l * 24)
            queries(qmr, 0, 0, queries_r)
            values(0, l * layer_items, 0)
            for i in range(16):
                row_max(0, i, l * layer_items + 1 + i, (1 + i) % 2)
            store_maxima(0, l * layer_items + 17, 1)
            queries(qm, 0, 0, queries_f)
            queries(qmr, 1, 1, queries_r)
            chain.ends(1)
            with dve.Fori(0, 3) as k:
                body(k * 2, 0, True, True)
                body(k * 2 + 1, 1, True, True)
            body(6, 0, True, False)
            body(7, 1, False, False)


FRONT = ["Q0", "K0", "Q1", "K1", "R0a", "R0b", "R0c", "Q2", "K2", "R1a", "R1b", "R1c", "Q3", "K3",
         "R2a", "R2b", "R2c", "R3a", "R3b", "R3c"]
FRONT_ITEMS = len(FRONT) + 1
FRONT_DVE = sum(n[0] != "Q" for n in FRONT) + 1
TAIL_AT = 7
QKV, TAIL = 12, 4
RING = QKV + TAIL
READ = 12
CHAIN = 7
MIDDLE = ["S0", "P0", "S1", "P1", "S2", "P2", "S3", "P3", "V0", "P4", "S4", "P5", "S5", "P6", "V1", "P7",
          "S6", "P8", "S7", "P9", "V2", "P10", "P11", "V3"]


def qkv_at(per_step, s, b0):
    return per_step * s - (0 if b0 else TAIL)


def tail_at(per_step, s, last):
    return per_step * s + (per_step - TAIL if last else 2 * per_step - 2 * TAIL)


def read_by_dve(s, i):
    return FRONT_DVE * s + sum(n[0] != "Q" for n in FRONT[:i + 1])


def read_by_act(s, i):
    return 4 * s + sum(n[0] == "Q" for n in FRONT[:i + 1])


def row_group(name):
    p, part = int(name[1]), name[2]
    return {"a": (0, 4 * p, 4), "b": (1, 4 * p, 2), "c": (1, 4 * p + 2, 2)}[part]


def projection(i):
    return (i // 4, i % 4) if i < 8 else ((i - 8) // 2, 4 + i % 2)


def local_attention(g, d, t):
    nc = g.nc
    filled, ring_act, ring_dve = g.sem("l_ring_filled"), g.sem("l_ring_read_act"), g.sem("l_ring_read_dve")
    front_filled, front_act, front_dve = g.sem("l_front_filled"), g.sem("l_front_read_act"), g.sem("l_front_read_dve")
    q_rounded, k_rounded = g.sem("l_q_rounded"), g.sem("l_k_rounded")
    w_loaded, wf_loaded, tables = g.sem("l_weights_loaded"), g.sem("l_ffn_weights_loaded"), g.sem("l_tables_ready")
    shifted, sq_reduced = g.sem("l_shifted"), g.sem("l_squares_reduced")
    ab_summed, n2_ready, guess, rn_ready = g.sem("l_ab_summed"), g.sem("l_n2_ready"), g.sem("l_rnorm_guess"), g.sem("l_rnorm_ready")
    qk_normed = g.sem("l_qk_normed")
    scores_ready, probs_ready = g.sem("l_scores_ready"), g.sem("l_probs_ready")
    values_summed, values_out = g.sem("l_values_summed"), g.sem("l_values_out")
    recip_ready, out_filled, y_added = g.sem("l_reciprocals_ready"), g.sem("l_out_filled"), g.sem("l_y_added")
    own, aown = g.sem("l_dve_own"), g.sem("l_act_own")
    ring = g.ring
    first = d * NB

    with nc.Block() as block:
        @block.sync
        def _(sp):
            sp.dma_start(t.wf[:, :], g.a["wf"][:, cols(d, D_ALL - D_W1)]).then_inc(wf_loaded, 16)

        @block.tensor
        def _(pe):
            def project(s, i, b0=False):
                tile, j = projection(i)
                if i >= 2 or not b0:
                    pe.wait_ge(ring_act, QKV * s + i - 1)
                    pe.wait_ge(ring_dve, qkv_at(READ, s, b0) + min(i - 1, 8))
                pe.matmul(ring[:, i % 2, :], t.xs[:, tile * P:(tile + 1) * P], t.wa[:, j * C:(j + 1) * C],
                          start=True, stop=True).then_inc(filled, 1)

            def turn(name, bank):
                p = int(name[1]) + (4 if name[0] == "K" else 0)
                for cc in range(2):
                    for tile in range(2):
                        mm = pe.transpose(g.st[:, bank, cc * SEQ + tile * P:cc * SEQ + (tile + 1) * P],
                                          t.qk[:, tile, (2 * p + cc) * P:(2 * p + cc + 1) * P], g.f("ident"))
                mm.then_inc(front_filled, 1)

            def rows(name, bank):
                tile, h0, n = row_group(name)
                width, k0 = (P, 0) if tile == 0 else (KSPAN, P - WIN)
                for x in range(n):
                    c, hh = divmod(h0 + x, 2)
                    out = g.st[:, bank, x * width:(x + 1) * width]
                    pe.matmul(out, t.qzr[:, c, hh, tile * P:(tile + 1) * P], t.ktr[:, c, k0:k0 + width],
                              start=True, stop=False)
                    mm = pe.matmul(out, g.b("ident"), g.b(f"band{tile}", width), start=False, stop=True)
                mm.then_inc(front_filled, 1)

            def tail(s, last=False):
                pe.wait_ge(recip_ready, s + 1)
                for p in range(4):
                    if p < 2 and not last:
                        pe.wait_ge(ring_act, QKV * (s + 1) + 11 + p)
                    pe.wait_ge(ring_dve, tail_at(READ, s, last) + p - 1)
                    for cc in range(2):
                        c = 2 * p + cc
                        mm = pe.matmul(ring[:, p % 2, cc * SEQ:(cc + 1) * SEQ],
                                       g.cf[:, F_AT["selr"] + c * P:F_AT["selr"] + (c + 1) * P], t.rsum[:, :],
                                       start=True, stop=True)
                    mm.then_inc(filled, 1)

            def project_back(s, last=False):
                pe.wait_ge(ring_dve, tail_at(READ, s, last) + TAIL)
                for c in range(8):
                    mm = pe.matmul(g.sm[:, 0:SEQ], t.wa[:, D_WO + c * P:D_WO + (c + 1) * P], t.o[:, c, :],
                                   start=c == 0, stop=c == 7)
                mm.then_inc(out_filled, 1)

            def front(s, after):
                pe.wait_ge(qk_normed, 8 * (s + 1))
                for i, name in enumerate(FRONT):
                    if after and i == TAIL_AT:
                        tail(s - 1)
                    if after and i == TAIL_AT + 5:
                        project_back(s - 1)
                    if i >= 4:
                        if FRONT[i - 4][0] == "Q":
                            pe.wait_ge(front_act, read_by_act(s, i - 4))
                        else:
                            pe.wait_ge(front_dve, read_by_dve(s, i - 4))
                    if name[0] == "R":
                        if name[2] == "a":
                            pe.wait_ge(q_rounded, 4 * s + int(name[1]) + 1)
                            pe.wait_ge(k_rounded, 4 * s + int(name[1]) + 1)
                        rows(name, i % 4)
                    else:
                        turn(name, i % 4)
                pe.wait_ge(front_dve, read_by_dve(s, len(FRONT) - 1))
                for tile in range(2):
                    mm = pe.transpose(g.ov[0:HEADS, tile * P:(tile + 1) * P],
                                      t.mrow[:, tile * HEADS:(tile + 1) * HEADS], g.f("ident"))
                mm.then_inc(front_filled, 1)

            def scores(s, pair):
                for h in (2 * pair, 2 * pair + 1):
                    c, hh = divmod(h, 2)
                    if pair >= 2:
                        pe.wait_ge(probs_ready, 8 * s + pair - 1)
                    for kt, q0, q1, at in ((0, 0, KSPAN, 0), (1, P, SEQ, KSPAN)):
                        out = g.st[:, h % 4, at:at + q1 - q0]
                        pe.matmul(out, t.kt[:, c, kt * P:(kt + 1) * P], t.qz[:, c, hh, q0:q1], start=True, stop=False)
                        pe.matmul(out, g.b("ident"), g.b("bandT", q1 - q0), start=False, stop=False)
                        mm = pe.matmul(out, g.cb[:, B_AT["sel"] + h * P:B_AT["sel"] + (h + 1) * P], t.mt[:, q0:q1],
                                       start=False, stop=True)
                mm.then_inc(scores_ready, 1)

            def sum_values(s, u, quad, after):
                pe.wait_ge(probs_ready, 8 * s + 2 * quad + 2)
                if quad:
                    pe.wait_ge(values_out, 4 * s + quad)
                elif after:
                    pe.wait_ge(y_added, s)
                for kt, q0, q1, at in ((0, 0, KSPAN, 0), (1, P, SEQ, KSPAN)):
                    for x in range(4):
                        h = 4 * quad + x
                        c, hh = divmod(h, 2)
                        pe.matmul(g.ov[hh * LHD:(hh + 1) * LHD, c % 2 * SEQ + q0:c % 2 * SEQ + q1],
                                  t.v[u][:, kt, h * LHD:(h + 1) * LHD], t.pt[:, quad % 2 * 4 + x, at:at + q1 - q0],
                                  start=kt == 0 and x < 2, stop=kt == 1, skip_group_check=True)
                for kt, q0, q1, at in ((0, 0, KSPAN, 0), (1, P, SEQ, KSPAN)):
                    for x in range(4):
                        mm = pe.matmul(g.sm[32 * x:32 * x + 32, q0:q1],
                                       g.cf[:, F_AT["sumsel"] + 32 * quad:F_AT["sumsel"] + 32 * quad + 32],
                                       t.pt[:, quad % 2 * 4 + x, at:at + q1 - q0],
                                       start=kt == 0 and quad == 0, stop=kt == 1 and quad == 3, skip_group_check=True)
                mm.then_inc(values_summed, 1)

            def body(s, u, after, more):
                front(s, after)
                pe.wait_ge(front_dve, FRONT_DVE * (s + 1))
                pe.wait_ge(front_act, 4 * (s + 1))
                if more:
                    pe.wait_ge(shifted, s + 2)
                for item in MIDDLE:
                    kind, n = item[0], int(item[1:])
                    if kind == "S":
                        scores(s, n)
                    if kind == "V":
                        sum_values(s, u, n, after)
                    if kind == "P" and more:
                        project(s + 1, n)

            pe.wait_ge(w_loaded, d * 32 + 32)
            pe.wait_ge(shifted, first + 1)
            for i in range(QKV):
                project(first, i, b0=True)
            body(first, 0, False, True)
            with pe.Fori(0, 3) as kk:
                body(first + kk * 2 + 1, 1, True, True)
                body(first + kk * 2 + 2, 0, True, True)
            body(first + 7, 1, True, False)
            tail(first + 7, last=True)
            project_back(first + 7, last=True)

        @block.scalar
        def _(act):
            act.preload_act_table_set(EXP_AND_LN)
            chain = Chain(act, aown)

            def projected(s, u, i, b0=False):
                tile, j = projection(i)
                act.wait_ge(filled, qkv_at(RING, s, b0) + i + 1)
                if i < 8:
                    if i >= 2:
                        act.wait_ge(sq_reduced, 8 * s + i - 1)
                    act.activation(t.sq[:, i % 2, :], ring[:, i % 2, :], ACT.Square).then_inc(ring_act, 1)
                else:
                    act.activation(t.v[u][:, tile, (j - 4) * C:(j - 3) * C], ring[:, i % 2, :], ACT.Copy).then_inc(ring_act, 1)
                if i in (4, 8):
                    done = i // 4 - 1
                    act.wait_ge(n2_ready, 2 * s + done + 1)
                    chain.link(act.activation(t.lnv[:, done, :], t.n2[:, done, :], ACT.Ln, scale=2.0 ** 20))
                    act.activation(t.rn[:, done, :], t.lnv[:, done, :], ACT.Exp, scale=-0.5,
                                   bias=g.f("lnoff", 1)).then_inc(guess, 1)

            def front(s):
                for i, name in enumerate(FRONT):
                    p, bank = int(name[1]), g.st[:, i % 4, :].rearrange("p (c s) -> p c s", c=2)
                    if name[0] == "Q":
                        act.wait_ge(front_filled, FRONT_ITEMS * s + i + 1)
                        act.activation(t.qz[0:LHD, 2 * p:2 * p + 2, 0, :], bank[0:LHD], ACT.Copy)
                        act.activation(t.qz[LHD:P, 2 * p:2 * p + 2, 1, :], bank[LHD:P], ACT.Copy).then_inc(front_act, 1)
                    if name[0] == "K":
                        act.wait_ge(front_dve, read_by_dve(s, i))
                        act.activation(t.ktr[:, 2 * p:2 * p + 2, :], t.kt[:, 2 * p:2 * p + 2, :],
                                       ACT.Copy).then_inc(k_rounded, 1)

            def probabilities(s, pair):
                act.wait_ge(scores_ready, 8 * s + pair + 1)
                if pair in (4, 6):
                    act.wait_ge(values_summed, 4 * s + pair // 2 - 1)
                act.activation(t.pt[:, pair % 4 * 2:pair % 4 * 2 + 2, :],
                               g.st[:, pair % 2 * 2:pair % 2 * 2 + 2, 0:PACK], ACT.Exp).then_inc(probs_ready, 1)

            def values_to_sbuf(s, quad):
                act.wait_ge(values_summed, 4 * s + quad + 1)
                act.activation(t.o[:, 2 * quad:2 * quad + 2, :].rearrange("p c s -> p (c s)"), g.ov[:, :],
                               ACT.Copy).then_inc(values_out, 1)

            def body(s, u, more):
                front(s)
                chain.start(2 * s + 2)
                for item in MIDDLE:
                    kind, n = item[0], int(item[1:])
                    if kind == "S":
                        probabilities(s, n)
                    if kind == "V":
                        values_to_sbuf(s, n)
                    if kind == "P" and more:
                        projected(s + 1, 1 - u, n)

            chain.start(first * 2)
            for i in range(QKV):
                projected(first, 0, i, b0=True)
            body(first, 0, True)
            with act.Fori(0, 3) as kk:
                body(first + kk * 2 + 1, 1, True)
                body(first + kk * 2 + 2, 0, True)
            body(first + 7, 1, False)

        @block.gpsimd
        def _(pool):
            pool.wait_ge(w_loaded, d * 32 + 32)
            for i, name in enumerate(("lqcos", "lqsin", "lkcos", "lksin")):
                pool.tensor_tensor(t.tab[:, i, :, :], g.f(name, 2 * LHD).rearrange("p (t k) -> p t k", t=2),
                                   t.qkscale[:, i, :].unsqueeze(1).broadcast_to([P, 2, LHD]), ALU.mult).then_inc(tables, 1)

            def rotate(s, i, b0):
                tile, j = projection(i)
                pool.wait_ge(ring_dve, qkv_at(READ, s, b0) + i + 1)
                pool.tensor_tensor(t.qk[:, tile, j * C:(j + 1) * C], t.ta[:, i % 2, :], t.tb[:, i % 2, :],
                                   ALU.add).then_inc(ab_summed, 1)

            def normalise(s, tile, j):
                if j == 0:
                    pool.wait_ge(rn_ready, 2 * s + tile + 1)
                pool.wait_ge(ab_summed, 8 * s + 4 * tile + j + 1)
                part = t.qk[:, tile, j * C:(j + 1) * C].rearrange("p (h k) -> p h k", k=LHD)
                pool.tensor_tensor(part, part, t.rn[:, tile, 8 * j:8 * j + 8].unsqueeze(2).broadcast_to([P, 8, LHD]),
                                   ALU.mult).then_inc(qk_normed, 1)

            def batch(s, b0=False):
                for i in range(8):
                    rotate(s, i, b0)
                    if i >= 5:
                        normalise(s, 0, i - 5)
                normalise(s, 0, 3)
                for j in range(4):
                    normalise(s, 1, j)

            batch(first, b0=True)
            with pool.Fori(1, NB) as b:
                pool.wait_ge(front_filled, FRONT_ITEMS * (first + b - 1) + FRONT.index("K3") + 1)
                batch(first + b)
            pool.wait_ge(wf_loaded, d * 16 + 16)

        @block.vector
        def _(dve):
            chain = Chain(dve, own)

            def shift(b):
                dve.tensor_copy(t.xs[0:64, :], g.y[0:64, cols(b, SEQ)])
                dve.tensor_copy(t.xs[64:P, 1:SEQ], g.y[64:P, bass.ds(b * SEQ, SEQ - 1)]).then_inc(shifted, 1)

            def projected(s, i):
                tile, j = projection(i)
                dve.wait_ge(ring_act, QKV * s + i + 1)
                if i >= 2:
                    dve.wait_ge(ab_summed, 8 * s + i - 1)
                bank = ring[:, i % 2, :].rearrange("p (h k) -> p h k", k=LHD)
                ta = t.ta[:, i % 2, :].rearrange("p (h k) -> p h k", k=LHD)
                tb = t.tb[:, i % 2, :].rearrange("p (h k) -> p h k", k=LHD)
                q = j // 2 * 2

                def table(n, lo, hi):
                    return t.tab[:, q + n, tile, lo:hi].unsqueeze(1).broadcast_to([P, 8, hi - lo])

                half = LHD // 2
                dve.tensor_tensor(ta, bank, table(0, 0, LHD), ALU.mult)
                dve.tensor_tensor(tb[:, :, 0:half], bank[:, :, half:LHD], table(1, 0, half), ALU.mult)
                dve.tensor_tensor(tb[:, :, half:LHD], bank[:, :, 0:half], table(1, half, LHD), ALU.mult).then_inc(ring_dve, 1)
                dve.tensor_reduce(t.n2[:, tile, 8 * j:8 * j + 8],
                                  t.sq[:, i % 2, :].rearrange("p (h k) -> p h k", k=LHD),
                                  AX.X, ALU.add).then_inc(sq_reduced, 1)
                if j == 3:
                    dve.wait_ge(sq_reduced, 8 * s + i + 1)
                    dve.tensor_scalar(t.n2[:, tile, :], t.n2[:, tile, :], 1e-24, None, ALU.max).then_inc(n2_ready, 1)

            def refine(s, tile):
                dve.wait_ge(guess, 2 * s + tile + 1)
                r, n2, w = t.rn[:, tile, :], t.n2[:, tile, :], t.nw[:, tile, :]
                chain.link(dve.tensor_tensor(w, r, r, ALU.mult))
                chain.link(dve.tensor_tensor(w, w, n2, ALU.mult))
                chain.link(dve.tensor_scalar(w, w, -0.5, 1.5, ALU.mult, ALU.add))
                dve.tensor_tensor(r, r, w, ALU.mult).then_inc(rn_ready, 1)

            def batch(s):
                for i in range(8):
                    projected(s, i)
                    if i == 5:
                        refine(s, 0)
                refine(s, 1)

            def reciprocals(s):
                dve.wait_ge(values_summed, 4 * (s + 1))
                dve.reciprocal(t.rsum[:, :], g.sm[:, 0:SEQ]).then_inc(recip_ready, 1)

            def normalise(s, p, last=False):
                dve.wait_ge(filled, tail_at(RING, s, last) + p + 1)
                dve.wait_ge(values_out, 4 * s + p + 1)
                o = t.o[:, 2 * p:2 * p + 2, :].rearrange("p c s -> p (c s)")
                dve.tensor_tensor(o, o, ring[:, p % 2, :], ALU.mult).then_inc(ring_dve, 1)

            def add_output(s, b):
                dve.wait_ge(out_filled, s + 1)
                ys = g.y[:, cols(b, SEQ)]
                dve.tensor_tensor(ys, ys, g.sm[:, 0:SEQ], ALU.add).then_inc(y_added, 1)

            def front(s, b, after):
                if after:
                    reciprocals(s - 1)
                for i, name in enumerate(FRONT):
                    if after and i == TAIL_AT:
                        for p in range(4):
                            normalise(s - 1, p)
                    if after and i == TAIL_AT + 5:
                        add_output(s - 1, b - 1)
                    p = int(name[1])
                    if name[0] == "Q":
                        continue
                    dve.wait_ge(front_filled, FRONT_ITEMS * s + i + 1)
                    if name[0] == "K":
                        bank = g.st[:, i % 4, :].rearrange("p (c s) -> p c s", c=2)
                        dve.tensor_copy(t.kt[:, 2 * p:2 * p + 2, :], bank).then_inc(front_dve, 1)
                        dve.wait_ge(front_act, 4 * s + p + 1)
                        dve.tensor_copy(t.qzr[:, 2 * p:2 * p + 2, :, :], t.qz[:, 2 * p:2 * p + 2, :, :]).then_inc(q_rounded, 1)
                    if name[0] == "R":
                        tile, h0, m = row_group(name)
                        width = P if tile == 0 else KSPAN
                        dve.tensor_reduce(t.mrow[:, tile * HEADS + h0:tile * HEADS + h0 + m],
                                          g.st[:, i % 4, 0:m * width].rearrange("p (h k) -> p h k", h=m),
                                          AX.X, ALU.max).then_inc(front_dve, 1)

            def store_maxima(s):
                dve.wait_ge(front_filled, FRONT_ITEMS * (s + 1))
                chain.link(dve.tensor_scalar(t.mt[0:HEADS, :], g.ov[0:HEADS, 0:SEQ], -1.0, None, ALU.mult))
                dve.scalar_tensor_tensor(out=t.mt[32:32 + HEADS, :], in0=g.ov[0:HEADS, 0:SEQ], scalar=-1.0,
                                         in1=t.mt[0:HEADS, :], op0=ALU.mult, op1=ALU.subtract).then_inc(front_dve, 1)

            def body(b, after, more):
                s = first + b
                chain.start(CHAIN * s + 6)
                front(s, b, after)
                store_maxima(s)
                if more:
                    shift(b + 1)
                    batch(s + 1)
                chain.ends(CHAIN if more else 1)

            shift(0)
            dve.wait_ge(tables, d * 4 + 4)
            chain.start(CHAIN * first)
            batch(first)
            chain.ends(6)
            body(0, False, True)
            with dve.Fori(1, NB - 1) as b:
                body(b, True, True)
            body(NB - 1, True, False)
            reciprocals(first + NB - 1)
            for p in range(4):
                normalise(first + NB - 1, p, last=True)
            add_output(first + NB - 1, NB - 1)


def load_attention_weights(g, d, t, sp):
    loaded = g.sem("l_weights_loaded")
    sp.dma_start(t.qkscale[:, :, :], g.a["qkscale"][bass.ds(d, 1), :].rearrange("o (r k) -> o r k", r=4)
                 .broadcast_to([P, 4, LHD])).then_inc(loaded, 16)
    sp.dma_start(t.wa[:, :], g.a["wa"][:, cols(d, D_W1)]).then_inc(loaded, 16)


def local_ffn(g, d, t):
    nc = g.nc
    shifted, centered, squared, variance, rstd, normed = (
        g.sem("f_" + n) for n in ("shifted", "centered", "squared", "variance", "rstd", "normed"))
    pair_filled, gelu_done, gated, sum_filled, updated = (
        g.sem("f_" + n) for n in ("pair_filled", "gelu_done", "gated", "sum_filled", "updated"))
    vec = D_VEC - D_W1
    gain, bias, b2 = (t.wf[:, vec + i:vec + i + 1] for i in (0, 1, 2 + 2 * FFC))
    with nc.Block() as block:
        @block.sync
        def _(sp):
            load_attention_weights(g, d + 1, t, sp)

        @block.tensor
        def _(pe):
            with pe.Fori(0, 2) as k:
                for u in range(2):
                    pe.wait_ge(shifted, d * 4 + k * 2 + u + 1)
                    pe.matmul(g.st[:, u, :], g.f("center"), t.fs[:, u, :], start=True, stop=True).then_inc(centered, 1)
                for u in range(2):
                    pe.wait_ge(squared, d * 4 + k * 2 + u + 1)
                    pe.matmul(g.st[:, 2 + u, :], g.f("mean"), t.fsq[:, u, :], start=True, stop=True).then_inc(variance, 1)
                pe.wait_ge(normed, 2 * (d * 4 + k * 2) + 4)

            def pair(c, i):
                if i >= 2:
                    pe.wait_ge(gated, 3 * (d * 4 + c) + i - 1)
                for x in range(2):
                    mm = pe.matmul(g.st[:, 2 * (i % 2) + x, :], t.wf[:, (x * FFC + i) * P:(x * FFC + i + 1) * P],
                                   t.xn[:, cols(c)], start=True, stop=True)
                mm.then_inc(pair_filled, 1)

            def down(c, i):
                pe.wait_ge(gated, 3 * (d * 4 + c) + i + 1)
                w2 = D_W2 - D_W1 + i * P
                mm = pe.matmul(g.ov[:, :], t.wf[:, w2:w2 + P], t.h[:, i, :], start=i == 0, stop=i == FFC - 1)
                if i == FFC - 1:
                    mm.then_inc(sum_filled, 1)

            with pe.Fori(0, 4) as c:
                pair(c, 0)
                pair(c, 1)
                down(c, 0)
                pair(c, 2)
                down(c, 1)
                down(c, 2)
                pe.wait_ge(updated, d * 4 + c + 1)

        @block.scalar
        def _(act):
            act.preload_act_table_set(EXP_AND_LN)
            with act.Fori(0, 2) as k:
                for u in range(2):
                    act.wait_ge(centered, d * 4 + k * 2 + u + 1)
                    act.activation(t.fsq[:, u, :], g.st[:, u, :], ACT.Square).then_inc(squared, 1)
                for u in range(2):
                    act.wait_ge(variance, d * 4 + k * 2 + u + 1)
                    act.activation(t.frs[:, u, :], g.st[:, 2 + u, :], ACT.Ln, bias=g.f("eps5", 1)).then_inc(rstd, 1)
                    act.wait_ge(rstd, 2 * (d * 4 + k * 2 + u) + 1)
                    act.activation(t.frs[:, u, :], t.frs[:, u, :], ACT.Exp, scale=-0.5).then_inc(rstd, 1)
            with act.Fori(0, 4) as c:
                for i in range(FFC):
                    act.wait_ge(pair_filled, 3 * (d * 4 + c) + i + 1)
                    act.activation(t.gl[:, i % 2, :], g.st[:, 2 * (i % 2) + 1, :], ACT.Gelu,
                                   bias=t.wf[:, vec + 2 + FFC + i:vec + 3 + FFC + i]).then_inc(gelu_done, 1)

        @block.vector
        def _(dve):
            with dve.Fori(0, 2) as k:
                for u in range(2):
                    c = k * 2 + u
                    src = g.y[:, cols(c)].rearrange("p (b s) -> p b s", b=2)
                    dst = t.fs[:, u, :].rearrange("p (b s) -> p b s", b=2)
                    dve.memset(dst[64:P, :, 0:1], 0.0)
                    dve.tensor_copy(dst[0:64], src[0:64])
                    dve.tensor_copy(dst[64:P, :, 1:SEQ], src[64:P, :, 0:SEQ - 1]).then_inc(shifted, 1)
                for u in range(2):
                    c = k * 2 + u
                    dve.wait_ge(rstd, 2 * (d * 4 + c) + 2)
                    dve.tensor_tensor(t.xn[:, cols(c)], g.st[:, u, :], t.frs[:, u, :], ALU.mult).then_inc(normed, 1)
                    dve.wait_ge(normed, 2 * (d * 4 + c) + 1)
                    dve.tensor_scalar(t.xn[:, cols(c)], t.xn[:, cols(c)], gain, bias, ALU.mult, ALU.add).then_inc(normed, 1)
            with dve.Fori(0, 4) as c:
                for i in range(FFC):
                    dve.wait_ge(gelu_done, 3 * (d * 4 + c) + i + 1)
                    dve.scalar_tensor_tensor(out=t.h[:, i, :], in0=g.st[:, 2 * (i % 2), :],
                                             scalar=t.wf[:, vec + 2 + i:vec + 3 + i], in1=t.gl[:, i % 2, :],
                                             op0=ALU.add, op1=ALU.mult).then_inc(gated, 1)
                dve.wait_ge(sum_filled, d * 4 + c + 1)
                ys = g.y[:, cols(c)]
                dve.scalar_tensor_tensor(out=ys, in0=g.ov[:, :], scalar=b2, in1=ys,
                                         op0=ALU.add, op1=ALU.add).then_inc(updated, 1)


class LocalMemory:

    def __init__(self, tmp):
        self.qkscale = tmp("l_qkscale", [P, 4, LHD], F32)
        self.tab = tmp("l_tab", [P, 4, 2, LHD], F32)
        self.wa = tmp("l_wa", [P, D_W1], F32)
        self.wf = tmp("l_wf", [P, D_ALL - D_W1], F32)
        self.xs = tmp("l_xs", [P, SEQ], F32)
        self.sq = tmp("l_sq", [P, 2, C], F32)
        self.ta = tmp("l_ta", [P, 2, C], F32)
        self.tb = tmp("l_tb", [P, 2, C], F32)
        self.n2 = tmp("l_n2", [P, 2, 2 * HEADS], F32)
        self.lnv = tmp("l_lnv", [P, 2, 2 * HEADS], F32)
        self.rn = tmp("l_rn", [P, 2, 2 * HEADS], F32)
        self.nw = tmp("l_nw", [P, 2, 2 * HEADS], F32)
        self.qk = tmp("l_qk", [P, 2, 2 * INNER], F32)
        self.qz = tmp("l_qz", [P, 8, 2, SEQ], F32)
        self.qzr = tmp("l_qzr", [P, 8, 2, SEQ], F32R)
        self.kt = tmp("l_kt", [P, 8, SEQ], F32)
        self.ktr = tmp("l_ktr", [P, 8, SEQ], F32R)
        self.v = [tmp(f"l_v{u}", [P, 2, INNER], F32) for u in range(2)]
        self.mrow = tmp("l_mrow", [P, 2 * HEADS], F32)
        self.mt = tmp("l_mt", [P, SEQ], BF16)
        self.pt = tmp("l_pt", [P, 8, PACK], F32)
        self.rsum = tmp("l_rsum", [P, SEQ], F32)
        self.o = tmp("l_o", [P, 8, SEQ], F32)


class FfnMemory:

    def __init__(self, t):
        self.wf, self.wa, self.qkscale = t.wf, t.wa, t.qkscale
        big = t.qk[:, :, :].rearrange("p a b -> p (a b)")
        self.xn = big[:, 0:TOK]
        at = TOK
        self.fs = t.tb[:, :, :]
        self.fsq = big[:, at:at + 2 * C].rearrange("p (u s) -> p u s", u=2)
        self.frs = big[:, at + 2 * C:at + 4 * C].rearrange("p (u s) -> p u s", u=2)
        self.gl = t.ta[:, :, :]
        self.h = t.o[:, :, :].rearrange("p c s -> p (c s)")[:, 0:FFC * C].rearrange("p (i s) -> p i s", i=FFC)


def local_transformer(g, tmp):
    nc = g.nc
    t = LocalMemory(tmp)
    zeroed = g.sem("l_zeroed")
    with nc.Block() as block:
        @block.sync
        def _(sp):
            load_attention_weights(g, 0, t, sp)

        @block.vector
        def _(dve):
            dve.memset(t.qz[:, :, :, :], 0.0)
            dve.memset(t.xs[:, :], 0.0)
            dve.memset(t.mt[:, :], 0.0).then_inc(zeroed, 1)
            dve.wait_ge(zeroed, 1)
    with nc.Fori(0, DEPTH) as d:
        local_attention(g, d, t)
        local_ffn(g, d, FfnMemory(t))


def add_gated(g):
    with g.nc.Block() as block:
        @block.vector
        def _(dve):
            dve.wait_ge(g.sem("l_weights_loaded"), 32 * (DEPTH + 1))
            dve.scalar_tensor_tensor(out=g.x[:, :], in0=g.y[:, :], scalar=g.gates[:, 4:5], in1=g.x[:, :],
                                     op0=ALU.mult, op1=ALU.add)


def gate_scores(g, pooled, weights, bias, prod, out, sem, seen):
    nc = g.nc
    with nc.Block() as block:
        @block.vector
        def _(dve):
            shape = [P, NB, EXPERTS]
            dve.tensor_tensor(prod[:, :, :], pooled.unsqueeze(2).broadcast_to(shape),
                              weights.unsqueeze(1).broadcast_to(shape), ALU.mult).then_inc(sem, 1)
            dve.wait_ge(sem, seen + 2)
            dve.tensor_tensor(out[:, :, :], g.ov[:, 0:NB * EXPERTS].rearrange("p (b e) -> p b e", b=NB),
                              bias.unsqueeze(1).broadcast_to(shape), ALU.add)

        @block.tensor
        def _(pe):
            pe.wait_ge(sem, seen + 1)
            pe.matmul(g.ov[:, 0:NB * EXPERTS], g.f("ones"), prod[:, :, :].rearrange("p b e -> p (b e)"),
                      start=True, stop=True).then_inc(sem, 1)


def moe_ffn(g, tmp):
    nc = g.nc
    prod, sc = tmp("m_prod", [P, NB, EXPERTS], F32), tmp("m_scores", [P, NB, EXPERTS], F32)
    above, tied = (tmp(n, [P, NB, EXPERTS, EXPERTS], F32) for n in ("m_above", "m_tied"))
    gate, gb = tmp("m_gate", [P, NB, EXPERTS], F32), tmp("m_gate_bias", [P, NB], F32)
    h, tmp_out = tmp("m_hidden", [P, 4, C], F32), tmp("m_out", [P, C], F32)
    first_tokens = g.y[:, :].rearrange("p (b s) -> p b s", b=NB)[:, :, 0]
    gate_scores(g, first_tokens, g.vec("r1_0", EXPERTS), g.rbias[:, 0:EXPERTS], prod, sc, g.sem("gate_steps"), 0)
    own = g.sem("m_own")
    hidden_filled, gelu_done, gated = g.sem("m_hidden_filled"), g.sem("m_gelu_done"), g.sem("m_gated")
    out_filled, updated = g.sem("m_out_filled"), g.sem("m_updated")
    wide = [P, NB, EXPERTS, EXPERTS]
    with nc.Block() as block:
        @block.vector
        def _(dve):
            chain = Chain(dve, own)
            mine = sc[:, :, :].unsqueeze(3).broadcast_to(wide)
            others = sc[:, :, :].unsqueeze(2).broadcast_to(wide)
            flat = [P, NB, EXPERTS * EXPERTS]
            dve.tensor_tensor(above[:, :, :, :], others, mine, ALU.is_gt)
            chain.link(dve.tensor_tensor(tied[:, :, :, :], others, mine, ALU.is_equal))
            tf, af = (x[:, :, :, :].rearrange("p b e j -> p b (e j)") for x in (tied, above))
            chain.link(dve.tensor_tensor(tf, tf, g.f("earlier", EXPERTS * EXPERTS).unsqueeze(1).broadcast_to(flat), ALU.mult))
            chain.link(dve.tensor_tensor(af, af, tf, ALU.add))
            chain.link(dve.tensor_reduce(gate[:, :, :], above[:, :, :, :], AX.X, ALU.add))
            chain.link(dve.tensor_scalar(gate[:, :, :], gate[:, :, :], 2.0, 0.5, ALU.is_lt, ALU.mult))
            chain.link(dve.tensor_tensor(prod[:, :, :], gate[:, :, :],
                                         g.vec("mb2_0", EXPERTS).unsqueeze(1).broadcast_to([P, NB, EXPERTS]), ALU.mult))
            dve.tensor_reduce(gb[:, :], prod[:, :, :], AX.X, ALU.add)
    with nc.Block() as block:
        @block.tensor
        def _(pe):
            def down(c, e):
                pe.wait_ge(gated, EXPERTS * c + e + 1)
                mm = pe.matmul(g.ov[:, :], g.wm(f"m2_{e}"), h[:, e % 4, :], start=e == 0, stop=e == EXPERTS - 1)
                if e == EXPERTS - 1:
                    mm.then_inc(out_filled, 1)

            with pe.Fori(0, 4) as c:
                for e in range(EXPERTS):
                    if e >= 4:
                        pe.wait_ge(gelu_done, EXPERTS * c + e - 3)
                    pe.matmul(g.st[:, e % 4, :], g.wm(f"m1_{e}"), g.y[:, cols(c)], start=True, stop=True)\
                        .then_inc(hidden_filled, 1)
                    if e >= 2:
                        down(c, e - 2)
                down(c, EXPERTS - 2)
                down(c, EXPERTS - 1)
                pe.wait_ge(updated, 2 * c + 2)

        @block.scalar
        def _(act):
            with act.Fori(0, 4) as c:
                for e in range(EXPERTS):
                    act.wait_ge(hidden_filled, EXPERTS * c + e + 1)
                    act.activation(h[:, e % 4, :], g.st[:, e % 4, :], ACT.Gelu, bias=g.vec(f"mb1_{e}")).then_inc(gelu_done, 1)

        @block.vector
        def _(dve):
            with dve.Fori(0, 4) as c:
                for e in range(EXPERTS):
                    dve.wait_ge(gelu_done, EXPERTS * c + e + 1)
                    for x in range(2):
                        part = h[:, e % 4, x * SEQ:(x + 1) * SEQ]
                        ins = dve.tensor_scalar(part, part, gate[:, :, :].rearrange("p b e -> p (b e)")[
                            :, bass.ds((c * 2 + x) * EXPERTS + e, 1)], None, ALU.mult)
                    ins.then_inc(gated, 1)
                dve.wait_ge(out_filled, c + 1)
                for x in range(2):
                    ins = dve.tensor_scalar(tmp_out[:, x * SEQ:(x + 1) * SEQ], g.ov[:, x * SEQ:(x + 1) * SEQ],
                                            gb[:, bass.ds(c * 2 + x, 1)], g.gates[:, 5:6], ALU.add, ALU.mult)
                ins.then_inc(updated, 1)
                dve.wait_ge(updated, 2 * c + 1)
                xs = g.x[:, cols(c)]
                dve.tensor_tensor(xs, xs, tmp_out[:, :], ALU.add).then_inc(updated, 1)


def soft_moe_ffn(g, tmp):
    nc = g.nc
    pooled, prod, sc = tmp("s_pooled", [P, NB], F32), tmp("s_prod", [P, NB, EXPERTS], F32), tmp("s_scores", [P, NB, EXPERTS], F32)
    top, ex, total = tmp("s_top", [P, NB, 8], F32), tmp("s_exp", [P, NB, EXPERTS], F32), tmp("s_total", [P, NB], F32)
    gate = tmp("s_gate", [P, NB, EXPERTS], F32)
    h, acc = tmp("s_hidden", [P, 4, C], F32), tmp("s_acc", [P, C], F32)
    shape = [P, NB, EXPERTS]
    own = g.sem("s_own")
    with nc.Block() as block:
        @block.vector
        def _(dve):
            chain = Chain(dve, own)
            chain.link(dve.tensor_reduce(pooled[:, :], g.y[:, :].rearrange("p (b s) -> p b s", b=NB), AX.X, ALU.add))
            dve.tensor_scalar(pooled[:, :], pooled[:, :], 1.0 / SEQ, None, ALU.mult)
    gate_scores(g, pooled[:, :], g.vec("r2_0", EXPERTS), g.rbias[:, EXPERTS:2 * EXPERTS], prod, sc, g.sem("gate_steps"), 2)
    exp_done = g.sem("s_exp_done")
    with nc.Block() as block:
        @block.scalar
        def _(act):
            act.preload_act_table_set(EXP_AND_LN)
            act.wait_ge(own, 2 + NB)
            act.activation(ex[:, :, :], ex[:, :, :], ACT.Exp).then_inc(exp_done, 1)

        @block.vector
        def _(dve):
            chain = Chain(dve, own)
            chain.start(1)
            for b in range(NB):
                chain.link(dve.max(top[:, b, :], sc[:, b, :]))
            chain.link(dve.tensor_tensor(ex[:, :, :], sc[:, :, :], top[:, :, 0:1].broadcast_to(shape), ALU.subtract))
            chain.link(dve.tensor_tensor(gate[:, :, :], sc[:, :, :], top[:, :, 1:2].broadcast_to(shape), ALU.is_ge))
            dve.wait_ge(exp_done, 1)
            chain.link(dve.tensor_tensor(gate[:, :, :], gate[:, :, :], ex[:, :, :], ALU.mult))
            chain.link(dve.tensor_reduce(total[:, :], gate[:, :, :], AX.X, ALU.add))
            chain.link(dve.reciprocal(total[:, :], total[:, :]))
            dve.tensor_tensor(gate[:, :, :], gate[:, :, :], total[:, :].unsqueeze(2).broadcast_to(shape), ALU.mult)
    hidden_filled, gelu_done, summed = g.sem("s_hidden_filled"), g.sem("s_gelu_done"), g.sem("s_summed")
    with nc.Block() as block:
        @block.tensor
        def _(pe):
            with pe.Fori(0, 4) as c:
                for e in range(EXPERTS):
                    if e >= 4:
                        pe.wait_ge(gelu_done, EXPERTS * c + e - 3)
                    pe.matmul(g.st[:, e % 4, :], g.wm(f"e_{e}"), g.y[:, cols(c)], start=True, stop=True)\
                        .then_inc(hidden_filled, 1)
                pe.wait_ge(gelu_done, EXPERTS * c + EXPERTS)

        @block.scalar
        def _(act):
            with act.Fori(0, 4) as c:
                for e in range(EXPERTS):
                    act.wait_ge(hidden_filled, EXPERTS * c + e + 1)
                    if e >= 4:
                        act.wait_ge(summed, (EXPERTS + 1) * c + e - 3)
                    act.activation(h[:, e % 4, :], g.st[:, e % 4, :], ACT.Gelu, bias=g.vec(f"eb_{e}")).then_inc(gelu_done, 1)
                act.wait_ge(summed, (EXPERTS + 1) * c + EXPERTS)

        @block.vector
        def _(dve):
            with dve.Fori(0, 4) as c:
                for e in range(EXPERTS):
                    dve.wait_ge(gelu_done, EXPERTS * c + e + 1)
                    if e:
                        dve.wait_ge(summed, (EXPERTS + 1) * c + e)
                    for x in range(2):
                        part, into = h[:, e % 4, x * SEQ:(x + 1) * SEQ], acc[:, x * SEQ:(x + 1) * SEQ]
                        w = gate[:, :, :].rearrange("p b e -> p (b e)")[:, bass.ds((c * 2 + x) * EXPERTS + e, 1)]
                        if e == 0:
                            ins = dve.tensor_scalar(into, part, w, None, ALU.mult)
                        else:
                            ins = dve.scalar_tensor_tensor(out=into, in0=part, scalar=w, in1=into, op0=ALU.mult, op1=ALU.add)
                    ins.then_inc(summed, 1)
                dve.wait_ge(summed, (EXPERTS + 1) * c + EXPERTS)
                xs = g.x[:, cols(c)]
                dve.scalar_tensor_tensor(out=xs, in0=acc[:, :], scalar=g.gates[:, 6:7], in1=xs,
                                         op0=ALU.mult, op1=ALU.add).then_inc(summed, 1)
                dve.wait_ge(summed, (EXPERTS + 1) * c + EXPERTS + 1)


QB, QEPS, ROUND = 128.0, 1e-5, 1.5 * 2.0 ** 23


def quantised_ffn(g, tmp):
    nc = g.nc
    wabs, wq = tmp("q_abs", [P, P], F32), tmp("q_w", [P, P], F32)
    col = tmp("q_columns", [P, 12], F32)
    ext = tmp("q_extrema", [P, 4], F32)
    xq = tmp("q_x", [P, 2, C], F32)
    own, all_max, total = g.sem("q_own"), g.sem("q_all_max"), g.sem("q_total")
    absmax = bass.bass_isa.ReduceOp.max

    def cl(i):
        return col[:, i:i + 1]

    with nc.Block() as block:
        @block.vector
        def _(dve):
            chain = Chain(dve, own)
            w = g.wm("quant")
            dve.tensor_reduce(cl(0), g.y[:, :], AX.X, ALU.max)
            chain.link(dve.tensor_reduce(cl(1), g.y[:, :], AX.X, ALU.min))
            chain.link(dve.tensor_scalar(cl(1), cl(1), -1.0, None, ALU.mult))
            chain.link(dve.tensor_tensor(cl(2), cl(0), cl(1), ALU.max))
            chain.link(dve.tensor_scalar(wabs[:, :], w, -1.0, None, ALU.mult))
            chain.link(dve.tensor_tensor(wabs[:, :], wabs[:, :], w, ALU.max))
            chain.link(dve.tensor_reduce(cl(3), wabs[:, :], AX.X, ALU.add))
            dve.wait_ge(total, 1)
            chain.link(dve.tensor_scalar(cl(4), g.ov[:, 0:1], 1.0 / (P * P), None, ALU.mult))
            chain.link(dve.tensor_scalar(cl(5), cl(4), QEPS, None, ALU.add))
            chain.link(dve.reciprocal(cl(5), cl(5)))
            chain.link(dve.tensor_scalar(wq[:, :], w, cl(5), ROUND, ALU.mult, ALU.add))
            chain.link(dve.tensor_scalar(wq[:, :], wq[:, :], ROUND, 1.0, ALU.subtract, ALU.min))
            chain.link(dve.tensor_scalar(wq[:, :], wq[:, :], -1.0, None, ALU.max))
            dve.wait_ge(all_max, 1)
            chain.link(dve.reciprocal(cl(7), cl(6)))
            chain.link(dve.tensor_tensor(cl(8), cl(6), cl(4), ALU.mult))
            dve.tensor_scalar(cl(8), cl(8), 1.0 / QB, g.gates[:, 7:8], ALU.mult, ALU.mult)

        @block.gpsimd
        def _(pool):
            pool.wait_ge(own, 3)
            pool.partition_all_reduce(cl(6), cl(2), P, absmax).then_inc(all_max, 1)

        @block.tensor
        def _(pe):
            pe.wait_ge(own, 6)
            pe.matmul(g.ov[:, 0:1], g.f("ones"), cl(3), start=True, stop=True).then_inc(total, 1)
    scaled, clipped, filled, updated = g.sem("q_scaled"), g.sem("q_clipped"), g.sem("q_filled"), g.sem("q_updated")
    with nc.Block() as block:
        @block.vector
        def _(dve):
            with dve.Fori(0, 4) as c:
                x = xq[:, 0, :]
                dve.tensor_scalar(x, g.y[:, cols(c)], QB, cl(7), ALU.mult, ALU.mult).then_inc(scaled, 1)
                dve.wait_ge(scaled, c + 1)
                dve.tensor_scalar(x, x, QEPS - QB, QB - QEPS, ALU.max, ALU.min).then_inc(clipped, 1)
                dve.wait_ge(filled, c + 1)
                xs = g.x[:, cols(c)]
                dve.scalar_tensor_tensor(out=xs, in0=g.ov[:, :], scalar=cl(8), in1=xs,
                                         op0=ALU.mult, op1=ALU.add).then_inc(updated, 1)

        @block.tensor
        def _(pe):
            with pe.Fori(0, 4) as c:
                pe.wait_ge(clipped, c + 1)
                pe.matmul(g.ov[:, :], wq[:, :], xq[:, 0, :], start=True, stop=True).then_inc(filled, 1)
                pe.wait_ge(updated, c + 1)


def gated_layers(nc, a, out, stop=99):
    with ExitStack() as ctx:
        g = Core(nc, ctx, a)

        phases = [0]

        def phase(work, *args):
            phases[0] += 1
            tag = f"_{phases[0]}"
            with ExitStack() as inner:
                work(*args, lambda name, shape, dt: inner.enter_context(nc.sbuf_tensor(name + tag, shape, dt)))

        def whole(buf):
            return lambda c: buf[:, cols(c)]

        uses = [0]

        def norm(src, dst, eps, scale=None, shift=None):
            phase(lambda tmp: layernorm(g, uses[0], whole(src), whole(dst), eps, tmp, scale, shift))
            uses[0] += 1

        phase(load_everything, g)
        for l in range(4):
            if 2 * l >= stop:
                break
            norm(g.x, g.y, "eps5")

            def attend(tmp):
                q_all, k_all = tmp("q_all", [P, TOK], F32), tmp("k_all", [P, TOK], F32)
                phase(project, g, l, q_all, k_all)
                phase(cross_attention, g, l, q_all, k_all)

            phase(attend)
            if 2 * l + 1 >= stop:
                break
            norm(g.x, g.y, "eps5")
            if l == 0:
                phase(local_transformer, g)
                add_gated(g)
            elif l == 1:
                phase(moe_ffn, g)
            elif l == 2:
                phase(soft_moe_ffn, g)
            else:
                norm(g.y, g.y, "eps3", g.vec("gamma"), g.vec("beta"))
                phase(quantised_ffn, g)
        stored = g.sem("stored")
        with nc.Block() as block:
            @block.sync
            def _(sp):
                sp.dma_start(out[:, :], g.x[:, :]).then_inc(stored, 16)
                sp.wait_ge(stored, 16)


def lay_out(inputs):
    i = {k: np.asarray(v) for k, v in inputs.items()}
    arr = {}
    arr["xT"] = i["x"].reshape(TOK, P).T
    arr["ctxT"] = i["ctx_1024"].reshape(TOK, P).T
    m = i["mask_SxS2_ik0"]
    arr["mask_q"] = m.reshape(2, P, SEQ).transpose(1, 0, 2)
    arr["mask_k"] = m.T.reshape(2, P, SEQ).transpose(1, 0, 2)
    mb = i["mask_BxS2_ik0"]
    arr["pad_r"] = mb.reshape(1, TOK)
    arr["pad_c"] = mb.reshape(NB, 2, P).transpose(2, 0, 1).reshape(P, 2 * NB)
    arr["gates"] = np.concatenate([i["g_xattn"], i["g_ffn"]]).reshape(1, 8)
    arr["rbias"] = np.concatenate([i["L1_ffn_br"], i["L2_ffn_gate_b"]]).reshape(1, 2 * EXPERTS)
    d = np.arange(P)
    partner = d // HD * HD + (d % HD + HD // 2) % HD
    w = {"q0": i["L0_xattn_Wq"].T, "q0r": i["L0_xattn_Wq"].T[:, partner],
         "k0": i["L0_xattn_Wk"].T, "k0r": i["L0_xattn_Wk"].T[:, partner],
         "v0": i["L0_xattn_Wv"].T, "o0": i["L0_xattn_Wo"].T,
         "q2": i["L2_xattn_Wq"], "k2": i["L2_xattn_Wk"], "v2": i["L2_xattn_Wv"], "o2": i["L2_xattn_Wo"],
         "quant": i["L3_ffn_weight"]}
    for n in "qkvo":
        w[n + "1"] = i["L1_xattn_W" + n].T
        w[n + "3"] = i["L3_xattn_w" + n].T
    v = {"qn": np.tile(i["L0_xattn_q_norm_w"], HEADS), "kn": np.tile(i["L0_xattn_k_norm_w"], HEADS),
         "gamma": i["L3_ffn_ln_gamma"], "beta": i["L3_ffn_ln_beta"], "zero": np.zeros(P, np.float32)}
    v["qnr"], v["knr"] = v["qn"][partner], v["kn"][partner]
    for n in "qkvo":
        v["b" + n + "1"] = i["L1_xattn_b" + n]
        v["b" + n + "3"] = i["L3_xattn_b" + n]
    for e in range(EXPERTS):
        w[f"m1_{e}"], w[f"m2_{e}"] = i["L1_ffn_W1"][e], i["L1_ffn_W2"][e]
        w[f"e_{e}"] = i["L2_ffn_expert_w"][e].T
        v[f"mb1_{e}"], v[f"mb2_{e}"], v[f"eb_{e}"] = i["L1_ffn_b1"][e], i["L1_ffn_b2"][e], i["L2_ffn_expert_b"][e]
        v[f"r1_{e}"], v[f"r2_{e}"] = i["L1_ffn_Wr"][:, e], i["L2_ffn_gate_w"][e]
    arr["w"] = np.concatenate([w[n] for n in W_NAMES], axis=1)
    arr["v"] = np.stack([v[n] for n in V_NAMES], axis=1)
    wa, wf, qk = [], [], []
    hidden = FFC * P
    swap = (np.arange(LHD) + LHD // 2) % LHD
    for n in range(DEPTH):
        wo = i["L0_ffn_Wo"][n].reshape(8, P, P).transpose(1, 0, 2).reshape(P, -1)
        wa.append(np.concatenate([i["L0_ffn_Wqkv"][n], wo], axis=1))
        w1 = np.zeros((P, 2, hidden), np.float32)
        w1[:, :, :FFN_IN] = i["L0_ffn_W1"][n].reshape(P, 2, FFN_IN)
        w2 = np.zeros((hidden, P), np.float32)
        w2[:FFN_IN] = i["L0_ffn_W2"][n]
        b1 = np.zeros((2, hidden), np.float32)
        b1[:, :FFN_IN] = i["L0_ffn_b1"][n].reshape(2, FFN_IN)
        wf.append(np.concatenate([w1.reshape(P, -1), w2.reshape(FFC, P, P).transpose(1, 0, 2).reshape(P, -1),
                                  i["L0_ffn_ln_g"][n][:, None], i["L0_ffn_ln_b"][n][:, None],
                                  b1.reshape(2 * FFC, P).T, i["L0_ffn_b2"][n][:, None]], axis=1))
        qs, ks = i["L0_ffn_q_scale"][n], i["L0_ffn_k_scale"][n]
        qk.append(np.concatenate([qs, qs[swap], ks, ks[swap]]))
    wa.append(np.zeros_like(wa[0]))
    qk.append(np.zeros_like(qk[0]))
    arr["wa"], arr["wf"], arr["qkscale"] = np.concatenate(wa, axis=1), np.concatenate(wf, axis=1), np.stack(qk)
    arr["cf"] = F_TAB.astype(np.float32)
    arr["cb"] = B_TAB.astype(mybir.dt.np(BF16))
    return {k: np.ascontiguousarray(x) for k, x in arr.items()}


def kernel(**inputs):
    import concourse.bacc as bacc
    from concourse.bass_utils import run_bass_kernel_spmd

    nc = bacc.Bacc("TRN2", target_bir_lowering=False, num_devices=1)
    arrays = lay_out(inputs)
    a = {n: nc.dram_tensor("in_" + n, x.shape, mybir.dt.from_np(x.dtype), kind="ExternalInput").ap()
         for n, x in arrays.items()}
    out = nc.dram_tensor("out_x", (P, TOK), F32, kind="ExternalOutput").ap()
    gated_layers(nc, a, out)
    r = run_bass_kernel_spmd(nc, [{"in_" + n: x for n, x in arrays.items()}], core_ids=[0])
    return np.ascontiguousarray(r.results[0]["out_x"].T).reshape(NB, SEQ, P)
```
